# Optimizing a Trainium2 kernel written in Bass

```python
import numpy as np
import jax
import jax.numpy as jnp

def _softmax(x, axis=-1):
    return jax.nn.softmax(x, axis=axis)

def _gelu(x):
    return jax.nn.gelu(x, approximate=True)

def _silu(x):
    return jax.nn.silu(x)

def _sigmoid(x):
    return jax.nn.sigmoid(x)

def _layernorm(x, axis=-1, eps=1e-05):
    m = jnp.mean(x, axis=axis, keepdims=True)
    v = jnp.var(x, axis=axis, keepdims=True)
    return (x - m) / jnp.sqrt(v + eps)

def _scatter_add(tgt, idx, src, axis=0):
    return tgt.at[idx].add(src)

def _segment_sum(src, seg, n):
    return jax.ops.segment_sum(src, seg, n)
kernel_name = 'mk_decoder_postln_d1_seqx_r8_e6f4ec'

def setup_inputs(seed: int=0):
    np.random.seed(seed)
    _w = jnp.asarray

    def _rec_inputs():
        import jax
        import jax.numpy as jnp
        _rk = jax.random.key(seed)
        x = -0.0005207 + 1.001 * jax.random.normal(jax.random.fold_in(_rk, 1), (8, 100, 512), jnp.float32)
        _lenS = 100 - jax.random.randint(jax.random.fold_in(_rk, 7), (8,), 0, max(1, 100 // 4) + 1, jnp.int32)
        _lenS2 = 1444 - jax.random.randint(jax.random.fold_in(_rk, 8), (8,), 0, max(1, 1444 // 4) + 1, jnp.int32)
        _ctx_4096P = jax.random.normal(jax.random.fold_in(_rk, 11), (8, 16, 512), jnp.float32)
        _ctx_4096c = jax.random.dirichlet(jax.random.fold_in(_rk, 511), 0.3 * jnp.ones((16,), jnp.float32), (8, 1444))
        _ctx_4096t = jnp.einsum('bsk,bkd->bsd', _ctx_4096c, _ctx_4096P)
        _ctx_4096t = _ctx_4096t * jax.lax.rsqrt(jnp.mean(jnp.square(_ctx_4096t)) + 1e-12) * 0.953939
        ctx_4096 = -0.00010331 + 0.999899 * (_ctx_4096t + 0.3 * jax.random.normal(jax.random.fold_in(_rk, 611), (8, 1444, 512), jnp.float32))
        return (x, ctx_4096)
    x, ctx_4096 = _rec_inputs()

    def _L0_attn_setup():
        import jax, jax.numpy as jnp
        import numpy as np
        N_STATE = 64
        SEQ_L = 512
        BATCH, HCH = (16, 64)
        DT_MIN, DT_MAX = (0.001, 0.1)

        def _make_DPLR_HiPPO(N):
            P = np.sqrt(1 + 2 * np.arange(N))
            A = P[:, None] * P[None, :]
            A = np.tril(A) - np.diag(np.arange(N))
            nhippo = -A
            p = 0.5 * np.sqrt(2 * np.arange(1, N + 1) + 1.0)
            q = 2 * p
            S = nhippo + p[:, None] * q[None, :]
            Lambda, V = np.linalg.eig(S)
            Vc = V.conj().T
            p_t = Vc @ p
            q_t = Vc @ q.conj()
            return (Lambda, p_t, q_t, Vc)

        def _ri(z):
            return np.stack([z.real, z.imag], axis=-1).astype(np.float32)

        def _cplx(x_ri):
            return x_ri[..., 0] + 1j * x_ri[..., 1]

        def _s4_kernel(Lambda, p, q, B, Ct, step, L):
            Omega = jnp.exp(-2j * jnp.pi * (jnp.arange(L) / L))
            g = 2.0 / step * ((1.0 - Omega) / (1.0 + Omega))
            c = 2.0 / (1.0 + Omega)
            denom = g[:, None] - Lambda[None, :]
            cauchy = lambda v: (v[None, :] / denom).sum(-1)
            k00 = cauchy(Ct.conj() * B)
            k01 = cauchy(Ct.conj() * p)
            k10 = cauchy(q.conj() * B)
            k11 = cauchy(q.conj() * p)
            at_roots = c * (k00 - k01 * (1.0 / (1.0 + k11)) * k10)
            return jnp.fft.ifft(at_roots, L).real
        key = jax.random.key(seed)
        k_u, k_ct, k_b, k_d, k_ls = jax.random.split(key, 5)
        Lambda, p, q, Vc = _make_DPLR_HiPPO(N_STATE)
        u = jax.random.normal(k_u, (BATCH, HCH, SEQ_L), dtype=jnp.float32)
        Ct_ri = jax.random.normal(k_ct, (1, N_STATE, 2), dtype=jnp.float32) / np.sqrt(N_STATE)
        Bp = jax.random.normal(k_b, (N_STATE, 1), dtype=jnp.float32) / np.sqrt(N_STATE)
        D = jax.random.uniform(k_d, (1,), dtype=jnp.float32)
        log_step = jax.random.uniform(k_ls, (1,), dtype=jnp.float32, minval=np.log(DT_MIN), maxval=np.log(DT_MAX))
        return {'u': u, 'Lambda_ri': jnp.asarray(_ri(Lambda)), 'p_ri': jnp.asarray(_ri(p)), 'q_ri': jnp.asarray(_ri(q)), 'Vc_ri': jnp.asarray(_ri(Vc)), 'Ct_ri': Ct_ri, 'Bp': Bp, 'D': D, 'log_step': log_step}
    _L0_attn_all = _L0_attn_setup()
    _L0_attn_in = {k: v for k, v in _L0_attn_all.items() if k in ('Lambda_ri', 'p_ri', 'q_ri', 'Vc_ri', 'Ct_ri', 'Bp', 'D', 'log_step')}
    del _L0_attn_all

    def _L0_xattn_setup():
        import jax, jax.numpy as jnp
        import numpy as np
        import math
        HIDDEN = 512
        N_HEADS = 32
        HEAD_DIM = 128
        N_KV_HEADS = 4
        N_GROUPS = N_HEADS // N_KV_HEADS
        key = jax.random.key(seed)
        ks = jax.random.split(key, 6)
        B, NL, S = (8, 64, 512)
        latents = jax.random.normal(ks[0], (B, NL, HIDDEN), dtype=jnp.float32)
        context = jax.random.normal(ks[1], (B, S, HIDDEN), dtype=jnp.float32)
        scale = 1.0 / math.sqrt(HIDDEN)
        Wq = jax.random.normal(ks[2], (HIDDEN, N_HEADS * HEAD_DIM), dtype=jnp.float32) * scale
        Wk = jax.random.normal(ks[3], (HIDDEN, N_KV_HEADS * HEAD_DIM), dtype=jnp.float32) * scale
        Wv = jax.random.normal(ks[4], (HIDDEN, N_KV_HEADS * HEAD_DIM), dtype=jnp.float32) * scale
        Wo = jax.random.normal(ks[5], (N_HEADS * HEAD_DIM, HIDDEN), dtype=jnp.float32) * scale
        return {'latents': latents, 'context': context, 'Wq': Wq, 'Wk': Wk, 'Wv': Wv, 'Wo': Wo}
    _L0_xattn_all = _L0_xattn_setup()
    _L0_xattn_in = {k: v for k, v in _L0_xattn_all.items() if k in ('Wq', 'Wk', 'Wv', 'Wo')}
    del _L0_xattn_all

    def _L0_ffn_setup():
        import jax, jax.numpy as jnp
        import numpy as np
        DIM = 512
        HID = 1376
        R = 16
        SCALING = 32.0 / 16.0

        def _lora_linear(x, w, a, b):
            base = jnp.einsum('bsd,od->bso', x, w)
            low = jnp.einsum('bsr,or->bso', jnp.einsum('bsd,rd->bsr', x, a), b)
            return base + low * SCALING
        key = jax.random.key(seed)
        ks = jax.random.split(key, 10)
        s_in = 1.0 / np.sqrt(DIM)
        s_hid = 1.0 / np.sqrt(HID)
        return {'x': jax.random.normal(ks[0], (4, 256, DIM), jnp.float32), 'w1': jax.random.normal(ks[1], (HID, DIM), jnp.float32) * s_in, 'w3': jax.random.normal(ks[2], (HID, DIM), jnp.float32) * s_in, 'w2': jax.random.normal(ks[3], (DIM, HID), jnp.float32) * s_hid, 'lora_A1': jax.random.normal(ks[4], (R, DIM), jnp.float32) * s_in, 'lora_B1': jax.random.normal(ks[5], (HID, R), jnp.float32) * 0.02, 'lora_A3': jax.random.normal(ks[6], (R, DIM), jnp.float32) * s_in, 'lora_B3': jax.random.normal(ks[7], (HID, R), jnp.float32) * 0.02, 'lora_A2': jax.random.normal(ks[8], (R, HID), jnp.float32) * s_hid, 'lora_B2': jax.random.normal(ks[9], (DIM, R), jnp.float32) * 0.02}
    _L0_ffn_all = _L0_ffn_setup()
    _L0_ffn_in = {k: v for k, v in _L0_ffn_all.items() if k in ('w1', 'w3', 'w2', 'lora_A1', 'lora_B1', 'lora_A3', 'lora_B3', 'lora_A2', 'lora_B2')}
    del _L0_ffn_all
    return {'x': x, 'ctx_4096': ctx_4096, 'L0_attn_Lambda_ri': _L0_attn_in['Lambda_ri'], 'L0_attn_p_ri': _L0_attn_in['p_ri'], 'L0_attn_q_ri': _L0_attn_in['q_ri'], 'L0_attn_Vc_ri': _L0_attn_in['Vc_ri'], 'L0_attn_Ct_ri': _L0_attn_in['Ct_ri'], 'L0_attn_Bp': _L0_attn_in['Bp'], 'L0_attn_D': _L0_attn_in['D'], 'L0_attn_log_step': _L0_attn_in['log_step'], 'L0_xattn_Wq': _L0_xattn_in['Wq'], 'L0_xattn_Wk': _L0_xattn_in['Wk'], 'L0_xattn_Wv': _L0_xattn_in['Wv'], 'L0_xattn_Wo': _L0_xattn_in['Wo'], 'L0_ffn_w1': _L0_ffn_in['w1'], 'L0_ffn_w3': _L0_ffn_in['w3'], 'L0_ffn_w2': _L0_ffn_in['w2'], 'L0_ffn_lora_A1': _L0_ffn_in['lora_A1'], 'L0_ffn_lora_B1': _L0_ffn_in['lora_B1'], 'L0_ffn_lora_A3': _L0_ffn_in['lora_A3'], 'L0_ffn_lora_B3': _L0_ffn_in['lora_B3'], 'L0_ffn_lora_A2': _L0_ffn_in['lora_A2'], 'L0_ffn_lora_B2': _L0_ffn_in['lora_B2']}

def reference(x, ctx_4096, L0_attn_Lambda_ri, L0_attn_p_ri, L0_attn_q_ri, L0_attn_Vc_ri, L0_attn_Ct_ri, L0_attn_Bp, L0_attn_D, L0_attn_log_step, L0_xattn_Wq, L0_xattn_Wk, L0_xattn_Wv, L0_xattn_Wo, L0_ffn_w1, L0_ffn_w3, L0_ffn_w2, L0_ffn_lora_A1, L0_ffn_lora_B1, L0_ffn_lora_A3, L0_ffn_lora_B3, L0_ffn_lora_A2, L0_ffn_lora_B2):
    import jax
    import jax.numpy as jnp

    def _L0_attn_ref(u, Lambda_ri, p_ri, q_ri, Vc_ri, Ct_ri, Bp, D, log_step):
        import jax, jax.numpy as jnp
        import numpy as np
        N_STATE = 64
        SEQ_L = 512
        BATCH, HCH = (16, 64)
        DT_MIN, DT_MAX = (0.001, 0.1)

        def _make_DPLR_HiPPO(N):
            P = np.sqrt(1 + 2 * np.arange(N))
            A = P[:, None] * P[None, :]
            A = np.tril(A) - np.diag(np.arange(N))
            nhippo = -A
            p = 0.5 * np.sqrt(2 * np.arange(1, N + 1) + 1.0)
            q = 2 * p
            S = nhippo + p[:, None] * q[None, :]
            Lambda, V = np.linalg.eig(S)
            Vc = V.conj().T
            p_t = Vc @ p
            q_t = Vc @ q.conj()
            return (Lambda, p_t, q_t, Vc)

        def _ri(z):
            return np.stack([z.real, z.imag], axis=-1).astype(np.float32)

        def _cplx(x_ri):
            return x_ri[..., 0] + 1j * x_ri[..., 1]

        def _s4_kernel(Lambda, p, q, B, Ct, step, L):
            Omega = jnp.exp(-2j * jnp.pi * (jnp.arange(L) / L))
            g = 2.0 / step * ((1.0 - Omega) / (1.0 + Omega))
            c = 2.0 / (1.0 + Omega)
            denom = g[:, None] - Lambda[None, :]
            cauchy = lambda v: (v[None, :] / denom).sum(-1)
            k00 = cauchy(Ct.conj() * B)
            k01 = cauchy(Ct.conj() * p)
            k10 = cauchy(q.conj() * B)
            k11 = cauchy(q.conj() * p)
            at_roots = c * (k00 - k01 * (1.0 / (1.0 + k11)) * k10)
            return jnp.fft.ifft(at_roots, L).real
        L = u.shape[-1]
        Lambda = _cplx(Lambda_ri)
        p = _cplx(p_ri)
        q = _cplx(q_ri)
        Vc = _cplx(Vc_ri)
        Ct = _cplx(Ct_ri).reshape(-1)
        B = (Vc @ Bp.astype(Vc.dtype)).reshape(-1)
        step = jnp.exp(log_step)[0]
        K = _s4_kernel(Lambda, p, q, B, Ct, step, L).astype(u.dtype)
        n = 2 * L
        y = jnp.fft.irfft(jnp.fft.rfft(u, n=n) * jnp.fft.rfft(K, n=n), n=n)[..., :L]
        return y + D[0] * u

    def _L0_xattn_ref(latents, context, Wq, Wk, Wv, Wo):
        import jax, jax.numpy as jnp
        import numpy as np
        import math
        HIDDEN = 512
        N_HEADS = 32
        HEAD_DIM = 128
        N_KV_HEADS = 4
        N_GROUPS = N_HEADS // N_KV_HEADS
        b, q_len, _ = latents.shape
        kv_len = q_len + context.shape[1]
        hidden_states = jnp.concatenate([context, latents], axis=1)
        q = (latents @ Wq).reshape(b, q_len, N_KV_HEADS, N_GROUPS, HEAD_DIM)
        k = (hidden_states @ Wk).reshape(b, kv_len, N_KV_HEADS, HEAD_DIM)
        v = (hidden_states @ Wv).reshape(b, kv_len, N_KV_HEADS, HEAD_DIM)
        scale = 1.0 / math.sqrt(HEAD_DIM)
        scores = jnp.einsum('bqhgd,bkhd->bhgqk', q, k) * scale
        attn = jax.nn.softmax(scores.astype(jnp.float32), axis=-1).astype(q.dtype)
        out = jnp.einsum('bhgqk,bkhd->bqhgd', attn, v)
        out = out.reshape(b, q_len, N_HEADS * HEAD_DIM)
        return out @ Wo

    def _L0_ffn_ref(x, w1, w3, w2, lora_A1, lora_B1, lora_A3, lora_B3, lora_A2, lora_B2):
        import jax, jax.numpy as jnp
        import numpy as np
        DIM = 512
        HID = 1376
        R = 16
        SCALING = 32.0 / 16.0

        def _lora_linear(x, w, a, b):
            base = jnp.einsum('bsd,od->bso', x, w)
            low = jnp.einsum('bsr,or->bso', jnp.einsum('bsd,rd->bsr', x, a), b)
            return base + low * SCALING
        h1 = _lora_linear(x, w1, lora_A1, lora_B1)
        h3 = _lora_linear(x, w3, lora_A3, lora_B3)
        g = jax.nn.silu(h1) * h3
        return _lora_linear(g, w2, lora_A2, lora_B2)
    x = _layernorm(x + _L0_attn_ref(x, L0_attn_Lambda_ri, L0_attn_p_ri, L0_attn_q_ri, L0_attn_Vc_ri, L0_attn_Ct_ri, L0_attn_Bp, L0_attn_D, L0_attn_log_step), axis=-1)
    x = _layernorm(x + _L0_xattn_ref(x, ctx_4096, L0_xattn_Wq, L0_xattn_Wk, L0_xattn_Wv, L0_xattn_Wo), axis=-1)
    x = _layernorm(x + _L0_ffn_ref(x, L0_ffn_w1, L0_ffn_w3, L0_ffn_w2, L0_ffn_lora_A1, L0_ffn_lora_B1, L0_ffn_lora_A3, L0_ffn_lora_B3, L0_ffn_lora_A2, L0_ffn_lora_B2), axis=-1)
    return x

_drawn_inputs = setup_inputs


def setup_inputs(seed=0):
    import zlib

    import numpy as np

    out = dict(_drawn_inputs(seed))
    spreads = {}
    factors = {'L0_attn_Lambda_ri': 8.0,
     'L0_attn_p_ri': 8.0,
     'L0_attn_q_ri': 8.0,
     'L0_attn_Vc_ri': 8.0,
     'L0_attn_Ct_ri': 8.0,
     'L0_attn_Bp': 8.0}
    for name, (base, spread) in spreads.items():
        noise = np.random.default_rng([zlib.crc32(name.encode()), seed]).standard_normal(out[name].shape)
        drawn = base * np.exp(spread * noise) if base else spread * noise
        out[name] = jnp.asarray(drawn.astype(out[name].dtype))
    for name, factor in factors.items():
        out[name] = (out[name] * factor).astype(out[name].dtype)
    return out
```

```python
import math
from contextlib import ExitStack

import numpy as np
import concourse.bass as bass
from concourse import mybir

FP32 = mybir.dt.float32
FP16 = mybir.dt.float16
BF16 = mybir.dt.bfloat16
ALU = mybir.AluOpType
ACT = mybir.ActivationFunctionType
AX = mybir.AxisListType

B, TOK, DM = 8, 100, 512
NTOK = B * TOK
CTX = 1444
KEYS = CTX + TOK
NH, NKV, HD = 32, 4, 128
G = NH // NKV
HID, RANK = 1376, 16
NST = 64
KC = DM // 128
EPS = 1e-5
LORA = 2.0

NCH = -(-KEYS // 128)
LASTK = KEYS - 128 * (NCH - 1)
NCT = -(-CTX // 128)
KT_N = KEYS // 4
GQ = G * TOK
HALF = GQ // 2
TH = NTOK // 2

SX = 32.0
SW = 512.0
SQ = 32.0
SP_LOG2 = 13
SO = 256.0
SG = 64.0
SR = 1024.0


def ch_rows(c):
    return 128 if c < NCH - 1 else LASTK


def split_chain(eng, sem):
    count = [0]

    def link(ins):
        count[0] += 1
        ins.then_inc(sem, 1)
        eng.wait_ge(sem, count[0])

    return link


def layernorm_rows(nc, dve, act_sqrt_ready, act_sqrt_done, link, z, stats, mv, var_eps, std, rstd, tmp, n):
    link(nc.vector.bn_stats(stats, z))
    link(nc.vector.bn_aggr(mv, stats))
    nc.vector.tensor_scalar(var_eps, mv[:, 1:2], EPS, None, ALU.add).then_inc(act_sqrt_ready, 1)
    dve.wait_ge(act_sqrt_done, n + 1)
    link(nc.vector.reciprocal(rstd, std))
    link(nc.vector.tensor_tensor(tmp, rstd, rstd, ALU.mult))
    dve.wait_ge(act_sqrt_ready, n + 1)
    link(nc.vector.tensor_tensor(tmp, tmp, var_eps, ALU.mult))
    link(nc.vector.tensor_scalar(tmp, tmp, -0.5, 1.5, ALU.mult, ALU.add))
    link(nc.vector.tensor_tensor(rstd, rstd, tmp, ALU.mult))


def s4_and_queries(nc, dram):
    with ExitStack() as ctx:
        sb = lambda n, s, d=FP32: ctx.enter_context(nc.sbuf_tensor(n, s, d))
        sem = lambda n: ctx.enter_context(nc.semaphore(n))
        ident = sb("a_ident", [128, 128])
        lam, pq, ct = sb("lam", [NST, 2]), sb("pq", [NST, 2, 2]), sb("ct", [NST, 2])
        vc, bp = sb("vc", [NST, NST, 2]), sb("bp", [NST, NST])
        vcb, bpair = sb("vcb", [NST, NST, 2]), sb("bpair", [NST, 2, 2])
        bswap = sb("bswap", [NST, 2, 2])
        num, numx = sb("num", [NST, 2, 2, 2]), sb("numx", [NST, 2, 2, 2])
        ls, alpha, nlam, alr = sb("ls", [NST, 1]), sb("alpha", [NST, 1]), sb("nlam", [NST, 2]), sb("alr", [NST, 1])
        els = sb("els", [NST, 1])
        omega = sb("omega", [NST, 3, DM])
        dre, dim, tmpa, tmpb = (sb(f"s4_{n}", [NST, DM]) for n in ("dre", "dim", "ta", "tb"))
        rre, rim = sb("s4_rre", [NST, DM]), sb("s4_rim", [NST, DM])
        ksum = sb("ksum", [128, KC, 4, 2])
        wpl = sb("wpl", [128, 2, KC])
        cx = [sb(f"cx{i}", [128, 2, KC]) for i in range(8)]
        cxt = sb("cxt", [128, 2, KC])
        bfly, bt = sb("bfly", [128, 2, 4]), sb("bt", [128, 4, 2])
        dft = sb("dft", [128, 2, DM])
        krow = sb("krow", [1, 128 + DM])
        toep = sb("toep", [128, DM])
        dsk, dsk1 = sb("dsk", [TOK, 1]), sb("dsk1", [TOK, 1])
        xs, xr, x1 = (sb(n, [TOK, B, DM]) for n in ("xs", "xr", "x1"))
        xt = sb("xt", [128, KC, NTOK])
        z = sb("z", [TOK, 2, DM])
        stats, mv, ve, std = sb("stats", [TOK, 6]), sb("mv", [TOK, B, 2]), sb("ve", [TOK, B]), sb("std", [TOK, B])
        rstd, tmp1 = sb("rstd", [TOK, B]), sb("tmp1", [TOK, 1])
        x1t = sb("x1t", [128, 2, KC, NTOK], FP16)
        wq32 = sb("wq32", [128, 2, KC, 512])
        wq16 = sb("wq16", [128, 2, 2, KC, 512], FP16)
        qst = sb("qst", [128, 2, B, GQ], FP16)
        ring = ctx.enter_context(nc.psum_tensor("a_ring", [128, 2, 2, 512], FP32))
        pmisc = ctx.enter_context(nc.psum_tensor("a_misc", [128, 4, 512], FP32))

        names = ("xr_done", "x_in", "param_in", "table_in", "dft_in", "alpha_exp", "dve_chain", "res_done", "ksum_mm",
                 "bfly_done", "kt_mm", "krow_done", "krow_out", "toep_in", "xT_mm", "xT_done", "y_mm", "y_used",
                 "sqrt_in", "sqrt_out", "x1_done", "x1T_mm", "ring_hi", "ring_free", "x1_out",
                 "wsplit_hi", "wsplit_done", "q_mm", "wq_in0", "wq_in1", "store0", "store1")
        s = {n: sem("a_" + n) for n in names}
        wq_in = (s["wq_in0"], s["wq_in1"])
        stores = (s["store0"], s["store1"])
        wq_v = dram["wq"].rearrange("(c p) n -> p c n", c=KC)
        qd = dram["q_d"].rearrange("l (b k) p n -> l k p b n", k=NKV)
        def qst_half(part, h, hf):
            return qst[:, part, 4 * hf:4 * hf + 4, h * TOK:(h + 1) * TOK]

        def ring_half(h, hf):
            return ring[:, h % 2, hf, 0:TH].rearrange("p (b n) -> p b n", n=TOK)

        def x1t_lo(V, dve, b):
            dve.wait_ge(s["ring_hi"], b + 1)
            V.scalar_tensor_tensor(x1t[:, 1, :, b * TOK:(b + 1) * TOK], ring[:, b % 2, 0, :].rearrange("p (c n) -> p c n", c=KC)[:, :, 0:TOK],
                                   SX, x1t[:, 0, :, b * TOK:(b + 1) * TOK], ALU.mult, ALU.subtract).then_inc(s["ring_free"], 1)

        def q_schedule(eng, split, evac):
            def group(j, last=False):
                split(j, 1)
                for h in range(4):
                    evac(j, h)
                if not last:
                    split(j + 1, 0)
                for h in range(4, G):
                    evac(j, h)
            split(0, 0)
            with eng.Fori(0, NKV - 1) as j:
                group(j)
            group(NKV - 1, last=True)

        def x1t_hi(A, act, b):
            act.wait_ge(s["x1T_mm"], b + 1)
            A.mul(x1t[:, 0, :, b * TOK:(b + 1) * TOK],
                  ring[:, b % 2, 0, :].rearrange("p (c n) -> p c n", c=KC)[:, :, 0:TOK], SX).then_inc(s["ring_hi"], 1)

        block = ctx.enter_context(nc.Block())

        @block.sync
        def _(sp):
            sp.dma_start(vc[:], dram["vc"]).then_inc(s["param_in"], 16)
            for dst, src in ((lam[:], dram["lam"]), (pq[:, 0, :], dram["p"]), (pq[:, 1, :], dram["q"]),
                             (ct[:], dram["ct"][0])):
                sp.dma_start(dst, src).then_inc(s["param_in"], 16)
            sp.dma_start(bp[:], dram["bp"].rearrange("k o -> o k").to_broadcast([NST, NST])).then_inc(s["param_in"], 16)
            sp.dma_start(ls[:], dram["ls"][None, :].to_broadcast([NST, 1])).then_inc(s["param_in"], 16)
            sp.dma_start(dsk[:], dram["dskip"][None, :].to_broadcast([TOK, 1])).then_inc(s["param_in"], 16)
            sp.dma_start(omega[:], dram["omega"][None, :, :].to_broadcast([NST, 3, DM])).then_inc(s["table_in"], 16)
            sp.dma_start(ident[:], dram["ident"]).then_inc(s["x_in"], 16)
            sp.dma_start(xs[:], dram["x"].rearrange("b t d -> t b d")).then_inc(s["x_in"], 16)
            sp.dma_start(wpl[:], dram["wpl"]).then_inc(s["dft_in"], 16)
            sp.dma_start(dft[:], dram["dft"]).then_inc(s["dft_in"], 16)
            for tl in range(2):
                sp.dma_start(wq32[:, tl], wq_v[:, :, 512 * tl:512 * (tl + 1)]).then_inc(wq_in[tl], 16)
            sp.wait_ge(s["krow_done"], 1)
            sp.dma_start(dram["kpad"], krow[:]).then_inc(s["krow_out"], 16)
            sp.wait_ge(s["krow_out"], 16)
            sp.dma_start(toep[:], bass.AP(dram["kpad"].tensor, 1, [[1, 128], [1, DM]])).then_inc(s["toep_in"], 16)
            for b in range(B):
                sp.wait_ge(s["x1_done"], b + 1)
                sp.dma_start(dram["x1_d"][:, b, :], x1[:, b, :]).then_inc(s["x1_out"], 16)
            sp.wait_ge(s["ring_free"], B)
            for part in range(2):
                sp.dma_start(dram["x1t_d"][part], x1t[:, part]).then_inc(stores[part], 16)

            def group(j, last=False):
                for tl in range(2):
                    if not last:
                        sp.wait_ge(s["wsplit_done"], 2 * j + tl + 1)
                        sp.dma_start(wq32[:, tl], wq_v[:, :, bass.ds(1024 * j + 1024 + 512 * tl, 512)]).then_inc(wq_in[tl], 16)
                for tl in range(2):
                    sp.wait_ge(s["ring_free"], B + G * j + 4 * tl + 4)
                    for part in range(2):
                        sp.dma_start(qd[part, bass.ds(j, 1), :, :, 400 * tl:400 * (tl + 1)].rearrange("o p b n -> (o p) b n"),
                                     qst[:, part, :, 400 * tl:400 * (tl + 1)]).then_inc(stores[tl], 16)

            with sp.Fori(0, NKV - 1) as j:
                group(j)
            group(NKV - 1, last=True)
            for tl in range(2):
                sp.wait_ge(stores[tl], 16 + 32 * NKV)
            sp.wait_ge(s["x1_out"], 16 * B)

        @block.vector
        def _(dve):
            link = split_chain(dve, s["dve_chain"])
            V = nc.vector
            dve.wait_ge(s["param_in"], 16 * 8)
            link(V.tensor_tensor(vcb[:], vc[:], bp[:].rearrange("n (k o) -> n k o", o=1).to_broadcast([NST, NST, 2]), ALU.mult))
            link(V.tensor_reduce(bpair[:, 0, :], vcb[:].rearrange("n k c -> n c k"), AX.X, ALU.add))
            link(V.tensor_copy(bpair[:, 1, :], pq[:, 0, :]))
            link(V.tensor_copy(bswap[:, :, 0], bpair[:, :, 1]))
            link(V.tensor_scalar(bswap[:, :, 1], bpair[:, :, 0], -1.0, None, ALU.mult))
            for a, src in enumerate((ct[:], pq[:, 1, :])):
                link(V.tensor_scalar(num[:, a], bpair[:], src[:, 0:1], None, ALU.mult))
                link(V.scalar_tensor_tensor(num[:, a], bswap[:], src[:, 1:2], num[:, a], ALU.mult, ALU.add))
            link(V.tensor_scalar(numx[:, :, :, 0], num[:, :, :, 1], -1.0, None, ALU.mult))
            link(V.tensor_copy(numx[:, :, :, 1], num[:, :, :, 0]))
            link(V.tensor_scalar(nlam[:], lam[:], -1.0, None, ALU.mult))
            dve.wait_ge(s["alpha_exp"], 1)
            link(V.tensor_scalar(alpha[:], els[:], 2.0, None, ALU.mult))
            link(V.tensor_tensor(alr[:], alpha[:], lam[:, 0:1], ALU.add))
            link(V.tensor_scalar(dsk1[:], dsk[:], 1.0, None, ALU.add))
            dve.wait_ge(s["table_in"], 16)
            one_m, one_p, sin = omega[:, 0, :], omega[:, 1, :], omega[:, 2, :]
            link(V.tensor_scalar(tmpa[:], one_m, alpha[:], None, ALU.mult))
            link(V.scalar_tensor_tensor(tmpa[:], sin, nlam[:, 1:2], tmpa[:], ALU.mult, ALU.add))
            link(V.scalar_tensor_tensor(dre[:], one_p, nlam[:, 0:1], tmpa[:], ALU.mult, ALU.add))
            link(V.tensor_scalar(tmpb[:], sin, alr[:], None, ALU.mult))
            link(V.scalar_tensor_tensor(dim[:], one_p, nlam[:, 1:2], tmpb[:], ALU.mult, ALU.add))
            link(V.tensor_tensor(tmpa[:], dre[:], dre[:], ALU.mult))
            link(V.tensor_tensor(tmpb[:], dim[:], dim[:], ALU.mult))
            link(V.tensor_tensor(tmpa[:], tmpa[:], tmpb[:], ALU.add))
            link(V.reciprocal(tmpb[:], tmpa[:]))
            link(V.tensor_tensor(rre[:], dre[:], tmpb[:], ALU.mult))
            V.scalar_tensor_tensor(rim[:], dim[:], -1.0, tmpb[:], ALU.mult, ALU.mult).then_inc(s["res_done"], 1)
            dve.wait_ge(s["ksum_mm"], 1)
            link(V.tensor_copy(ksum[:], pmisc[:, 0, 0:KC * 8].rearrange("p (c v r) -> p c v r", c=KC, v=4)))
            dve.wait_ge(s["dft_in"], 32)
            kv = [ksum[:, :, v, :].rearrange("p c r -> p r c") for v in range(4)]

            def cmul(dst, a, b):
                link(V.tensor_tensor(dst[:, 0, :], a[:, 0, :], b[:, 0, :], ALU.mult))
                link(V.tensor_tensor(cxt[:, 0, :], a[:, 1, :], b[:, 1, :], ALU.mult))
                link(V.tensor_tensor(dst[:, 0, :], dst[:, 0, :], cxt[:, 0, :], ALU.subtract))
                link(V.tensor_tensor(dst[:, 1, :], a[:, 0, :], b[:, 1, :], ALU.mult))
                link(V.tensor_tensor(cxt[:, 1, :], a[:, 1, :], b[:, 0, :], ALU.mult))
                link(V.tensor_tensor(dst[:, 1, :], dst[:, 1, :], cxt[:, 1, :], ALU.add))

            wk11, k0110, nume, quot = cx[0], cx[1], cx[2], cx[3]
            cmul(wk11, wpl[:], kv[3])
            link(V.tensor_scalar(wk11[:, 0, :], wk11[:, 0, :], 1.0, None, ALU.add))
            cmul(k0110, kv[1], kv[2])
            cmul(nume, wpl[:], k0110[:])
            sq, inv, conj = cx[4], cx[5], cx[6]
            link(V.tensor_tensor(sq[:], wk11[:], wk11[:], ALU.mult))
            link(V.tensor_tensor(inv[:, 0, :], sq[:, 0, :], sq[:, 1, :], ALU.add))
            link(V.reciprocal(inv[:, 1, :], inv[:, 0, :]))
            link(V.tensor_tensor(conj[:, 0, :], wk11[:, 0, :], inv[:, 1, :], ALU.mult))
            link(V.scalar_tensor_tensor(conj[:, 1, :], wk11[:, 1, :], -1.0, inv[:, 1, :], ALU.mult, ALU.mult))
            cmul(quot, nume[:], conj[:])
            at = cx[7]
            link(V.tensor_tensor(at[:], kv[0], quot[:], ALU.subtract))
            s02, d02, s13, d13 = (bt[:, i, :] for i in range(4))
            link(V.tensor_tensor(s02, at[:, :, 0], at[:, :, 2], ALU.add))
            link(V.tensor_tensor(d02, at[:, :, 0], at[:, :, 2], ALU.subtract))
            link(V.tensor_tensor(s13, at[:, :, 1], at[:, :, 3], ALU.add))
            link(V.tensor_tensor(d13, at[:, :, 1], at[:, :, 3], ALU.subtract))
            link(V.tensor_tensor(bfly[:, :, 0], s02, s13, ALU.add))
            link(V.tensor_tensor(bfly[:, :, 2], s02, s13, ALU.subtract))
            link(V.tensor_tensor(bfly[:, 0, 1:2], d02[:, 0:1], d13[:, 1:2], ALU.subtract))
            link(V.tensor_tensor(bfly[:, 1, 1:2], d02[:, 1:2], d13[:, 0:1], ALU.add))
            link(V.tensor_tensor(bfly[:, 0, 3:4], d02[:, 0:1], d13[:, 1:2], ALU.add))
            link(V.tensor_tensor(bfly[:, 1, 3:4], d02[:, 1:2], d13[:, 0:1], ALU.subtract))
            V.memset(krow[0:1, 0:128], 0.0).then_inc(s["bfly_done"], 1)
            dve.wait_ge(s["kt_mm"], 1)
            V.tensor_copy(krow[0:1, 128:].rearrange("o (u r) -> o u r", r=4),
                          pmisc[0:1, 1, :].rearrange("o (r u) -> o u r", r=4)).then_inc(s["krow_done"], 1)
            for b in range(B):
                dve.wait_ge(s["y_mm"], b + 1)
                V.scalar_tensor_tensor(z[:, b % 2], xs[:, b, :], dsk1[:], pmisc[0:TOK, 2 + b % 2, :],
                                       ALU.mult, ALU.add).then_inc(s["y_used"], 1)
                dve.wait_ge(s["y_used"], b + 1)
                layernorm_rows(nc, dve, s["sqrt_in"], s["sqrt_out"], link, z[:, b % 2], stats[:], mv[:, b, :],
                               ve[:, b:b + 1], std[:, b:b + 1], rstd[:, b:b + 1], tmp1[:], b)
                V.tensor_scalar(x1[:, b, :], z[:, b % 2], mv[:, b, 0:1], rstd[:, b:b + 1],
                                ALU.subtract, ALU.mult).then_inc(s["x1_done"], 1)
                if b >= 1:
                    x1t_lo(V, dve, b - 1)
            x1t_lo(V, dve, B - 1)

            def split_lo(j, tl):
                dve.wait_ge(s["wsplit_hi"], 2 * j + tl + 1)
                V.scalar_tensor_tensor(wq16[:, tl, 1].rearrange("p c n -> p (c n)"), wq32[:, tl].rearrange("p c n -> p (c n)"), SW,
                                       wq16[:, tl, 0].rearrange("p c n -> p (c n)"), ALU.mult, ALU.subtract).then_inc(s["wsplit_done"], 1)

            def evac(j, h):
                dve.wait_ge(s["ring_hi"], B + G * j + h + 1)
                for hf in range(2):
                    lo = V.scalar_tensor_tensor(qst_half(1, h, hf), ring_half(h, hf), SQ / (SX * SW), qst_half(0, h, hf),
                                                ALU.mult, ALU.subtract)
                lo.then_inc(s["ring_free"], 1)

            q_schedule(dve, split_lo, evac)

        @block.scalar
        def _(act):
            A = nc.scalar
            act.wait_ge(s["param_in"], 16 * 8)
            A.activation(els[:], ls[:], ACT.Exp, scale=-1.0).then_inc(s["alpha_exp"], 1)
            act.wait_ge(s["x_in"], 32)
            for b in range(B):
                A.copy(xr[:, b, :], xs[:, b, ::-1]).then_inc(s["xr_done"], 1)
            for b in range(B):
                act.wait_ge(s["xT_mm"], b + 1)
                A.copy(xt[:, :, b * TOK:(b + 1) * TOK],
                       ring[:, b % 2, 1, :].rearrange("p (c n) -> p c n", c=KC)[:, :, 0:TOK]).then_inc(s["xT_done"], 1)
            for b in range(B):
                act.wait_ge(s["sqrt_in"], b + 1)
                A.activation(std[:, b:b + 1], ve[:, b:b + 1], ACT.Sqrt).then_inc(s["sqrt_out"], 1)
                if b >= 1:
                    x1t_hi(A, act, b - 1)
            x1t_hi(A, act, B - 1)

            def split_hi(j, tl):
                act.wait_ge(wq_in[tl], 16 * j + 16)
                A.mul(wq16[:, tl, 0], wq32[:, tl], SW).then_inc(s["wsplit_hi"], 1)

            def evac(j, h):
                act.wait_ge(s["q_mm"], G * j + h + 1)
                if h % 4 == 0:
                    act.wait_ge(stores[h // 4], 16 + 32 * j)
                for hf in range(2):
                    hi = A.mul(qst_half(0, h, hf), ring_half(h, hf), SQ / (SX * SW))
                hi.then_inc(s["ring_hi"], 1)

            q_schedule(act, split_hi, evac)

        @block.tensor
        def _(pe):
            T = nc.tensor
            pe.wait_ge(s["x_in"], 32)
            for b in range(B):
                pe.wait_ge(s["xr_done"], b + 1)
                if b >= 2:
                    pe.wait_ge(s["xT_done"], b - 1)
                for c in range(KC):
                    mm = T.transpose(ring[:, b % 2, 1, 128 * c:128 * c + TOK], xr[:, b, DM - 128 * (c + 1):DM - 128 * c], ident[0:TOK, 0:TOK])
                mm.then_inc(s["xT_mm"], 1)
            pe.wait_ge(s["res_done"], 1)
            for c in range(KC):
                out = pmisc[:, 0, 8 * c:8 * (c + 1)]
                T.matmul(out, rre[:, 128 * c:128 * (c + 1)], num[:].rearrange("n a b r -> n (a b r)"), start=True, stop=False)
                mm = T.matmul(out, rim[:, 128 * c:128 * (c + 1)], numx[:].rearrange("n a b r -> n (a b r)"), start=False, stop=True)
            mm.then_inc(s["ksum_mm"], 1)
            pe.wait_ge(s["bfly_done"], 1)
            for r in range(4):
                out = pmisc[0:1, 1, 128 * r:128 * (r + 1)]
                for part in range(2):
                    mm = T.matmul(out, bfly[:, part, r:r + 1], dft[:, part, r:DM:4], start=(part == 0), stop=(part == 1))
            mm.then_inc(s["kt_mm"], 1)
            pe.wait_ge(s["toep_in"], 16)
            pe.wait_ge(s["xT_done"], B)

            def x1_transpose(b):
                pe.wait_ge(s["x1_done"], b + 1)
                if b >= 2:
                    pe.wait_ge(s["ring_free"], b - 1)
                for c in range(KC):
                    mm = T.transpose(ring[:, b % 2, 0, 128 * c:128 * c + TOK], x1[:, b, 128 * c:128 * (c + 1)], ident[0:TOK, 0:TOK])
                mm.then_inc(s["x1T_mm"], 1)

            for b in range(B):
                if b >= 2:
                    pe.wait_ge(s["y_used"], b - 1)
                for c in range(KC):
                    mm = T.matmul(pmisc[0:TOK, 2 + b % 2, 128 * c:DM], xt[:, c, b * TOK:(b + 1) * TOK],
                                  toep[:, 0:DM - 128 * c], start=(c == 0), stop=(c == KC - 1))
                mm.then_inc(s["y_mm"], 1)
                if b >= 1:
                    x1_transpose(b - 1)
            x1_transpose(B - 1)

            def heads(j):
                for h in range(G):
                    tl = h // 4
                    if h % 4 == 0:
                        pe.wait_ge(s["wsplit_done"], 2 * j + tl + 1)
                    pe.wait_ge(s["ring_free"], B + G * j + h - 1)
                    w0 = 128 * (h % 4)
                    for hf in range(2):
                        n = 0
                        for wp, xp in ((0, 0), (0, 1), (1, 0)):
                            for c in range(KC):
                                mm = T.matmul(ring[:, h % 2, hf, 0:TH], wq16[:, tl, wp, c, w0:w0 + 128],
                                              x1t[:, xp, c, TH * hf:TH * (hf + 1)], start=(n == 0), stop=(n == 11))
                                n += 1
                    mm.then_inc(s["q_mm"], 1)

            with pe.Fori(0, NKV - 1) as j:
                heads(j)
            heads(NKV - 1)


PARTS = ((0, 0), (0, 1), (1, 0))
NTASK0 = NCT + NCH + 4


def batch_tasks(has_next):
    keys = lambda nxt, h: [("K", nxt, h, i) for i in range(4)]
    if not has_next:
        return [keys(0, 1), keys(0, 2), keys(0, 3), []]
    tt = [("T", 1, 0, i) for i in range(NCT)]
    vv = [("V", 1, 0, i) for i in range(NCH)]
    return [keys(0, 1) + tt[0:3] + vv[0:1] + tt[3:4] + vv[1:2] + tt[4:6],
            keys(0, 2) + tt[6:8] + vv[2:3] + tt[8:10] + vv[3:4] + tt[10:12] + vv[4:5],
            keys(0, 3) + vv[5:9],
            keys(1, 0) + vv[9:13]]


def pair_plan(last):
    plan, n = [], 0
    for bb in range(2):
        for tasks in batch_tasks(not (last and bb == 1)):
            plan.append([(t, n + i) for i, t in enumerate(tasks)])
            n += len(tasks)
    return plan, n


PLAN, NTASK = pair_plan(False)
PLAN_LAST, _ = pair_plan(True)


def number_of(plan, what):
    return next(n for step in plan for t, n in step if t == what[0] and what[1] <= n < what[2])


def attention(nc, dram):
    with ExitStack() as ctx:
        sb = lambda n, s, d=FP32: ctx.enter_context(nc.sbuf_tensor(n, s, d))
        sem = lambda n: ctx.enter_context(nc.semaphore(n))
        ident, identh = sb("b_ident", [128, 128]), sb("b_identh", [128, 128], BF16)
        ones = sb("ones", [128, 1])
        ebias = sb("ebias", [128, 1])
        wk16, wv16 = sb("wk16", [128, 2, KC, 512], FP16), sb("wv16", [128, 2, KC, 512], FP16)
        cnat = sb("cnat", [128, 3, DM])
        ctxt = sb("ctxt", [128, 2, 2, KC, KEYS], FP16)
        kt = sb("kt", [128, 2, 2, KEYS], FP16)
        v16 = sb("v16", [128, 2, 2, NCH, 512], FP16)
        q16 = sb("q16", [128, 2, 2, GQ], FP16)
        sc = sb("sc", [128, NCH, GQ])
        p32 = sb("p32", [128, 4, GQ])
        rm, acc, o32 = sb("rm", [128, GQ]), sb("acc", [128, GQ]), sb("o32", [128, GQ])
        ost = sb("ost", [128, 2, 2, GQ], FP16)
        m32, r32 = sb("m32", [TOK, G]), sb("r32", [TOK, G])
        mh, ml = sb("mh", [TOK, G], BF16), sb("ml", [TOK, G], BF16)
        rh, rl = sb("rh", [TOK, G], FP16), sb("rl", [TOK, G], FP16)
        pair = ctx.enter_context(nc.psum_tensor("pair", [128, 2, 2, 512], FP32))
        pv = ctx.enter_context(nc.psum_tensor("pv", [128, 2, 512], FP32))
        misc = ctx.enter_context(nc.psum_tensor("misc", [128, 2, 512], FP32))
        w32 = sc[:, :, :].rearrange("p c n -> p (c n)")[:, 0:2 * KC * 512].rearrange("p (w c n) -> p w c n", w=2, c=KC)
        pp = sc[:, :, :].bitcast(FP16)

        names = ("const_in", "wk_in", "wv_in", "w_hi", "w_lo", "const_set", "s_mm", "s_copied", "rm_done", "sum_mm", "small",
                 "r_done", "rb_mm", "on_done", "o_copied", "o_hi", "o_lo", "max_mm", "m_done", "mb_mm", "sub_done",
                 "exp_done", "p_hi", "p_lo", "acc_done", "pv_mm", "task_mm", "task_hi", "task_lo",
                 "lat_in0", "lat_in1", "q_in0", "q_in1", "out0", "out1", "cn0", "cn1", "cn2")
        s = {n: sem("b_" + n) for n in names}
        lat_in, q_in, outs = ((s[n + "0"], s[n + "1"]) for n in ("lat_in", "q_in", "out"))
        cn_in = (s["cn0"], s["cn1"], s["cn2"])

        def p_part(part, c, r0, r1, c0, c1):
            return pp[r0:r1, c, GQ * part + c0:GQ * part + c1]

        def two(ap):
            return ap.rearrange("p (a n) -> p a n", a=2)

        def task_bank(task, n):
            kind, nxt, h, i = task
            bank = misc[:, (NTASK0 + n) % 2, :]
            if kind == "K":
                return bank[:, 0:KT_N]
            if kind == "V":
                return bank[0:ch_rows(i), :]
            r = min(128, CTX - 128 * i)
            return bank.rearrange("p (c n) -> p c n", c=KC)[:, :, 0:r]

        def task_dst(task, bpar, hpar, part):
            kind, nxt, h, i = task
            if kind == "K":
                return kt[:, hpar, part, KT_N * i:KT_N * (i + 1)]
            if kind == "V":
                return v16[0:ch_rows(i), bpar, part, i, :]
            r = min(128, CTX - 128 * i)
            return ctxt[:, bpar, part, :, 128 * i:128 * i + r]

        def task_scale(task):
            return SX if task[0] == "T" else SQ / (SX * SW)

        prologue_tasks = [("T", 0, 0, i) for i in range(NCT)] + [("V", 0, 0, i) for i in range(NCH)] + \
                         [("K", 0, 0, i) for i in range(4)]
        block = ctx.enter_context(nc.Block())

        @block.sync
        def _(sp):
            ctx_rows = dram["ctx"]

            def load_tile(b, t):
                r = min(128, CTX - 128 * t)
                src = ctx_rows[bass.ds(b, 1), 128 * t:128 * t + r, :].rearrange("o p d -> (o p) d")
                sp.dma_start(cnat[0:r, t % 3, :], src).then_inc(cn_in[t % 3], 16)

            def load_rows(b, par):
                for part in range(2):
                    sp.dma_start(ctxt[:, par, part, :, CTX:KEYS],
                                 dram["x1t_d"][part, :, :, bass.ds(b * TOK, TOK)]).then_inc(lat_in[par], 16)

            def load_q(gs, par):
                for part in range(2):
                    sp.dma_start(q16[:, par, part, :],
                                 dram["q_d"][part, bass.ds(gs, 1), :, :].rearrange("o p n -> (o p) n")).then_inc(q_in[par], 16)

            def tile_number(plan, bb, t):
                return next(n for step in plan[4 * bb:4 * bb + 4] for task, n in step if task[0] == "T" and task[3] == t)

            for par in range(2):
                sp.dma_start(ident[64 * par:64 * (par + 1), :], dram["ident"][64 * par:64 * (par + 1), :]).then_inc(outs[par], 16)
            sp.dma_start(w32[:, 0], dram["wk"].rearrange("(c p) n -> p c n", c=KC)).then_inc(s["wk_in"], 16)
            for t in range(3):
                load_tile(0, t)
            sp.dma_start(w32[:, 1], dram["wv"].rearrange("(c p) n -> p c n", c=KC)).then_inc(s["wv_in"], 16)
            load_rows(0, 0)
            load_q(0, 0)
            load_q(1, 1)
            for t in range(3, NCT):
                sp.wait_ge(s["task_mm"], t - 2)
                load_tile(0, t)
            sp.wait_ge(s["task_mm"], NCT)
            for t in range(3):
                load_tile(1, t)

            def body(it, plan, last):
                for st in range(8):
                    bb, h, gs = st // 4, st % 4, 8 * it + st
                    b = 2 * it + bb
                    has_next = not (last and bb == 1)
                    base = NTASK0 + NTASK * it
                    if h == 0 and has_next:
                        sp.wait_ge(s["task_mm"], base + plan[st][0][1])
                        load_rows(b + 1, (bb + 1) % 2)
                    if h in (0, 1) and has_next:
                        for t in (range(3, 9) if h == 0 else range(9, NCT)):
                            sp.wait_ge(s["task_mm"], base + tile_number(plan, bb, t - 3) + 1)
                            load_tile(b + 1, t)
                    if h == 3 and not last:
                        sp.wait_ge(s["task_mm"], base + tile_number(plan, bb, NCT - 1) + 1)
                        for t in range(3):
                            load_tile(b + 2, t)
                    if not (last and st >= 6):
                        sp.wait_ge(s["s_mm"], NCH * (gs + 1))
                        load_q(gs + 2, st % 2)
                    sp.wait_ge(s["o_lo"], gs + 1)
                    for part in range(2):
                        sp.dma_start(dram["o_d"][part, h, bass.ds(b, 1), :, :].rearrange("o p n -> (o p) n"),
                                     ost[:, st % 2, part, :]).then_inc(outs[st % 2], 16)

            with sp.Fori(0, B // 2 - 1) as it:
                body(it, PLAN, False)
            body(B // 2 - 1, PLAN_LAST, True)
            for par in range(2):
                sp.wait_ge(outs[par], 16 + 32 * (NKV * B // 2))

        @block.tensor
        def _(pe):
            T = nc.tensor

            def do_task(task, n, idx, bpar, hpar, waits=()):
                kind, nxt, h, i = task
                if waits:
                    for sm, v in waits:
                        pe.wait_ge(sm, v)
                if not isinstance(idx, int) or idx >= 2:
                    pe.wait_ge(s["task_lo"], idx - 1)
                out = task_bank(task, n)
                if kind == "T":
                    for c in range(KC):
                        mm = T.transpose(misc[:, (NTASK0 + n) % 2, 128 * c:128 * (c + 1)], cnat[:, i % 3, 128 * c:128 * (c + 1)], ident[:])
                else:
                    k = 0
                    for wp, xp in PARTS:
                        for c in range(KC):
                            if kind == "K":
                                lhs, rhs = wk16[:, wp, c, HD * h:HD * (h + 1)], ctxt[:, bpar, xp, c, KT_N * i:KT_N * (i + 1)]
                            else:
                                lhs, rhs = ctxt[:, bpar, xp, c, 128 * i:128 * i + ch_rows(i)], wv16[:, wp, c, :]
                            mm = T.matmul(out, lhs, rhs, start=(k == 0), stop=(k == 11))
                            k += 1
                mm.then_inc(s["task_mm"], 1)

            def scores_chunks(gs, par):
                for c in range(NCH):
                    if c == 0 and not (isinstance(gs, int) and gs == 0):
                        pe.wait_ge(s["sub_done"], NCH * gs)
                    if c >= 2:
                        pe.wait_ge(s["s_copied"], NCH * gs + c - 1)
                    r = ch_rows(c)
                    for kp, qp in PARTS:
                        for hf in range(2):
                            mm = T.matmul(pair[0:r, c % 2, hf, 0:HALF], kt[:, par, kp, 128 * c:128 * c + r],
                                          q16[:, par, qp, HALF * hf:HALF * (hf + 1)], start=(kp == 0 and qp == 0), stop=(kp == 1))
                    mm.then_inc(s["s_mm"], 1)

            def broadcast(cols, to):
                for g in range(G):
                    for part in range(2):
                        mm = T.matmul(pair[:, to, g // 4, TOK * (g % 4):TOK * (g % 4 + 1)],
                                      cols[part][:, g:g + 1].to_broadcast([TOK, 128]), identh[0:TOK, 0:TOK],
                                      start=(part == 0), stop=(part == 1))
                return mm

            for par in range(2):
                pe.wait_ge(outs[par], 16)
            for n, task in enumerate(prologue_tasks):
                kind, i = task[0], task[3]
                waits = []
                if kind == "T":
                    waits.append((cn_in[i % 3], 16 * (i // 3 + 1)))
                elif kind == "V":
                    waits.append((s["task_lo"], i + 1 if i < NCT else NCT))
                    if i == 0:
                        waits.append((s["w_lo"], 2))
                    if i == NCT - 1:
                        waits.append((lat_in[0], 32))
                do_task(task, n - NTASK0, n, 0, 0, waits)
            pe.wait_ge(s["const_set"], 3)
            pe.wait_ge(q_in[0], 32)
            pe.wait_ge(s["task_lo"], NTASK0)
            scores_chunks(0, 0)
            do_task(PLAN[0][0][0], 0, NTASK0, 0, 1)

            def body(it, plan, last):
                base = NTASK0 + NTASK * it
                for st in range(8):
                    bb, h, gs = st // 4, st % 4, 8 * it + st
                    final = last and st == 7

                    def side(k, tasks, nst):
                        task, n = tasks[k]
                        nbb, kind, i = nst // 4, task[0], task[3]
                        bpar = (nbb + task[1]) % 2
                        waits = []
                        nb = 2 * it + nbb + 1
                        if kind == "T":
                            waits.append((cn_in[i % 3], 64 * nb + 16 * (i // 3 + 1)))
                        if kind == "V":
                            t = min(i, NCT - 1)
                            tn = next(m for step in plan[4 * nbb:4 * nbb + 4] for tk, m in step if tk[0] == "T" and tk[3] == t)
                            waits.append((s["task_lo"], base + tn + 1))
                        if kind == "K" and task[1] == 1 and i == 0:
                            tn = next(m for step in plan[4 * nbb:4 * nbb + 4] for tk, m in step if tk[0] == "T" and tk[3] == NCT - 1)
                            waits.append((s["task_lo"], base + tn + 1))
                            waits.append((lat_in[bpar], 32 * it + 32 * ((nbb + 1) // 2 + 1)))
                        do_task(task, n, base + n, bpar, (nst + 1) % 2, waits)

                    tasks = plan[st]
                    pe.wait_ge(s["rm_done"], (NCH - 1) * (gs + 1))
                    pe.wait_ge(s["s_copied"], NCH * (gs + 1))
                    for g in range(G):
                        mm = T.transpose(pair[0:TOK, 1, g // 4, 128 * (g % 4):128 * (g % 4 + 1)], rm[:, TOK * g:TOK * (g + 1)], ident[:])
                    mm.then_inc(s["max_mm"], 1)
                    if len(tasks) > 1:
                        side(1, tasks, st)
                    pe.wait_ge(s["m_done"], gs + 1)
                    broadcast((mh, ml), 0).then_inc(s["mb_mm"], 1)
                    for k in range(2, len(tasks)):
                        side(k, tasks, st)
                    if h == 0:
                        pe.wait_ge(s["task_lo"], base + plan[st][0][1])
                    for c in range(NCH):
                        pe.wait_ge(s["p_lo"], NCH * gs + c + 1)
                        r = ch_rows(c)
                        for vp, pt in PARTS:
                            for hf in range(2):
                                mm = T.matmul(pv[:, hf, 0:HALF], v16[0:r, bb, vp, c, HD * h:HD * (h + 1)],
                                              p_part(pt, c, 0, r, HALF * hf, HALF * (hf + 1)),
                                              start=(c == 0 and vp == 0 and pt == 0), stop=(c == NCH - 1 and vp == 1))
                    mm.then_inc(s["pv_mm"], 1)
                    nst = st + 1
                    if not final:
                        pe.wait_ge(q_in[nst % 2], 32 * (4 * it + nst // 2 + 1))
                        keys_end = max(n for (t, n) in tasks if t[0] == "K") + 1
                        pe.wait_ge(s["task_lo"], base + keys_end)
                        scores_chunks(gs + 1, nst % 2)
                        pe.wait_ge(s["s_copied"], NCH * (gs + 1) + NCH - 1)
                    else:
                        pe.wait_ge(s["sub_done"], NCH * (gs + 1))
                    pe.wait_ge(s["acc_done"], (NCH - 1) * (gs + 1))
                    for g in range(G):
                        mm = T.matmul(pair[0:TOK, 1, 0, HALF + g:HALF + g + 1], acc[:, TOK * g:TOK * (g + 1)], ones[:], start=True, stop=True)
                    mm.then_inc(s["sum_mm"], 1)
                    if not final:
                        if nst < 8:
                            if plan[nst]:
                                side(0, plan[nst], nst)
                        else:
                            do_task(PLAN[0][0][0], NTASK, base + NTASK, 0, 1)
                        pe.wait_ge(s["s_copied"], NCH * (gs + 2))
                    pe.wait_ge(s["r_done"], gs + 1)
                    broadcast((rh, rl), 0).then_inc(s["rb_mm"], 1)

            with pe.Fori(0, B // 2 - 1) as it:
                body(it, PLAN, False)
            body(B // 2 - 1, PLAN_LAST, True)

        @block.scalar
        def _(act):
            A = nc.scalar

            def hi(task, n, idx, bpar, hpar):
                act.wait_ge(s["task_mm"], idx + 1)
                A.mul(task_dst(task, bpar, hpar, 0), task_bank(task, n), task_scale(task)).then_inc(s["task_hi"], 1)

            def copies(gs):
                for c in range(NCH):
                    act.wait_ge(s["s_mm"], NCH * gs + c + 1)
                    r = ch_rows(c)
                    A.copy(two(sc[0:r, c, :]), pair[0:r, c % 2, :, 0:HALF]).then_inc(s["s_copied"], 1)

            for w in range(2):
                act.wait_ge(s[("wk_in", "wv_in")[w]], 16)
                A.mul((wk16, wv16)[w][:, 0], w32[:, w], SW).then_inc(s["w_hi"], 1)
            for n, task in enumerate(prologue_tasks):
                hi(task, n - NTASK0, n, 0, 0)
            copies(0)
            hi(PLAN[0][0][0], 0, NTASK0, 0, 1)
            act.wait_ge(s["const_set"], 3)

            def body(it, plan, last):
                base = NTASK0 + NTASK * it
                for st in range(8):
                    gs = 8 * it + st
                    final = last and st == 7

                    def side(k, tasks, nst):
                        task, n = tasks[k]
                        hi(task, n, base + n, (nst // 4 + task[1]) % 2, (nst + 1) % 2)

                    tasks = plan[st]
                    if len(tasks) > 1:
                        side(1, tasks, st)

                    def p_high(c):
                        r = ch_rows(c)
                        act.wait_ge(s["exp_done"], NCH * gs + c + 1)
                        A.copy(p_part(0, c, 0, r, 0, GQ), p32[0:r, c % 4, :]).then_inc(s["p_hi"], 1)

                    for c in range(NCH):
                        r = ch_rows(c)
                        act.wait_ge(s["sub_done"], NCH * gs + c + 1)
                        if c >= 4:
                            act.wait_ge(s["p_lo"], NCH * gs + c - 3)
                            act.wait_ge(s["acc_done"], (NCH - 1) * gs + max(1, c - 4))
                        A.activation(p32[0:r, c % 4, :], sc[0:r, c, :], ACT.Exp, bias=ebias[0:r, :],
                                     scale=1.0 / (SQ * SQ * math.sqrt(HD))).then_inc(s["exp_done"], 1)
                        if c >= 1:
                            p_high(c - 1)
                        if 2 <= c + 1 < len(tasks):
                            side(c + 1, tasks, st)
                    p_high(NCH - 1)
                    for k in range(NCH + 1, len(tasks)):
                        side(k, tasks, st)
                    act.wait_ge(s["pv_mm"], gs + 1)
                    A.mul(two(o32[:]), pv[:, :, 0:HALF], SO / (2.0 ** SP_LOG2 * SQ * SR)).then_inc(s["o_copied"], 1)
                    nst = st + 1
                    if not final:
                        copies(gs + 1)
                        if nst < 8:
                            if plan[nst]:
                                side(0, plan[nst], nst)
                        else:
                            hi(PLAN[0][0][0], NTASK, base + NTASK, 0, 1)
                    act.wait_ge(s["on_done"], gs + 1)
                    act.wait_ge(outs[st % 2], 16 + 32 * (4 * it + st // 2))
                    A.copy(ost[:, st % 2, 0, :], o32[:]).then_inc(s["o_hi"], 1)

            with act.Fori(0, B // 2 - 1) as it:
                body(it, PLAN, False)
            body(B // 2 - 1, PLAN_LAST, True)

        @block.vector
        def _(dve):
            V = nc.vector

            def lo(task, n, idx, bpar, hpar):
                dve.wait_ge(s["task_hi"], idx + 1)
                V.scalar_tensor_tensor(task_dst(task, bpar, hpar, 1), task_bank(task, n), task_scale(task),
                                       task_dst(task, bpar, hpar, 0), ALU.mult, ALU.subtract).then_inc(s["task_lo"], 1)

            def running_max(gs):
                for c in range(1, NCH):
                    r = ch_rows(c)
                    dve.wait_ge(s["s_copied"], NCH * gs + c + 1)
                    if c >= 2:
                        dve.wait_ge(s["rm_done"], (NCH - 1) * gs + c - 1)
                    V.tensor_tensor(rm[0:r, :], sc[0:r, 0, :] if c == 1 else rm[0:r, :], sc[0:r, c, :], ALU.max).then_inc(s["rm_done"], 1)

            V.memset(ebias[:], SP_LOG2 * math.log(2.0)).then_inc(s["const_set"], 1)
            V.memset(ones[:], 2.0 ** -SP_LOG2).then_inc(s["const_set"], 1)
            for par in range(2):
                dve.wait_ge(outs[par], 16)
            V.tensor_copy(identh[:], ident[:]).then_inc(s["const_set"], 1)
            for w in range(2):
                dve.wait_ge(s["w_hi"], w + 1)
                w16 = (wk16, wv16)[w]
                V.scalar_tensor_tensor(w16[:, 1].rearrange("p c n -> p (c n)"), w32[:, w].rearrange("p c n -> p (c n)"), SW,
                                       w16[:, 0].rearrange("p c n -> p (c n)"), ALU.mult, ALU.subtract).then_inc(s["w_lo"], 1)
            for n, task in enumerate(prologue_tasks):
                lo(task, n - NTASK0, n, 0, 0)
            running_max(0)
            lo(PLAN[0][0][0], 0, NTASK0, 0, 1)

            def body(it, plan, last):
                base = NTASK0 + NTASK * it
                for st in range(8):
                    gs = 8 * it + st
                    final = last and st == 7

                    def side(k, tasks, nst):
                        task, n = tasks[k]
                        lo(task, n, base + n, (nst // 4 + task[1]) % 2, (nst + 1) % 2)

                    tasks = plan[st]
                    dve.wait_ge(s["max_mm"], gs + 1)
                    V.tensor_reduce(m32[:], pair[0:TOK, 1, :, :].rearrange("p a (g k) -> p (a g) k", k=128), AX.X, ALU.max).then_inc(s["small"], 1)
                    dve.wait_ge(s["small"], 4 * gs + 1)
                    V.tensor_copy(mh[:], m32[:]).then_inc(s["small"], 1)
                    dve.wait_ge(s["small"], 4 * gs + 2)
                    V.tensor_tensor(ml[:], m32[:], mh[:], ALU.subtract).then_inc(s["m_done"], 1)
                    if len(tasks) > 1:
                        side(1, tasks, st)

                    def p_low(c):
                        r = ch_rows(c)
                        dve.wait_ge(s["p_hi"], NCH * gs + c + 1)
                        V.tensor_tensor(p_part(1, c, 0, r, 0, GQ), p32[0:r, c % 4, :], p_part(0, c, 0, r, 0, GQ), ALU.subtract).then_inc(s["p_lo"], 1)

                    dve.wait_ge(s["mb_mm"], gs + 1)
                    for c in range(NCH):
                        r = ch_rows(c)
                        V.tensor_tensor(two(sc[0:r, c, :]), two(sc[0:r, c, :]), pair[0:r, 0, :, 0:HALF], ALU.subtract).then_inc(s["sub_done"], 1)
                        if c >= 2:
                            p_low(c - 2)
                        if 2 <= c + 1 < len(tasks):
                            side(c + 1, tasks, st)
                    p_low(NCH - 2)
                    p_low(NCH - 1)
                    for k in range(NCH + 1, len(tasks)):
                        side(k, tasks, st)
                    if not final:
                        running_max(gs + 1)
                    dve.wait_ge(s["sum_mm"], gs + 1)
                    V.reciprocal(r32[:], pair[0:TOK, 1, 0, HALF:HALF + G]).then_inc(s["small"], 1)
                    dve.wait_ge(s["small"], 4 * gs + 3)
                    V.tensor_scalar(rh[:], r32[:], SR, None, ALU.mult).then_inc(s["small"], 1)
                    dve.wait_ge(s["small"], 4 * gs + 4)
                    V.scalar_tensor_tensor(rl[:], r32[:], SR, rh[:], ALU.mult, ALU.subtract).then_inc(s["r_done"], 1)
                    nst = st + 1
                    if not final:
                        if nst < 8:
                            if plan[nst]:
                                side(0, plan[nst], nst)
                        else:
                            lo(PLAN[0][0][0], NTASK, base + NTASK, 0, 1)
                    dve.wait_ge(s["rb_mm"], gs + 1)
                    dve.wait_ge(s["o_copied"], gs + 1)
                    V.tensor_tensor(two(o32[:]), two(o32[:]), pair[:, 0, :, 0:HALF], ALU.mult).then_inc(s["on_done"], 1)

            with dve.Fori(0, B // 2 - 1) as it:
                body(it, PLAN, False)
            body(B // 2 - 1, PLAN_LAST, True)

        @block.gpsimd
        def _(pool):
            P = nc.gpsimd

            def body(it):
                for st in range(8):
                    gs = 8 * it + st
                    for c in range(1, NCH):
                        r = ch_rows(c)
                        pool.wait_ge(s["exp_done"], NCH * gs + c + 1)
                        if c >= 2:
                            pool.wait_ge(s["acc_done"], (NCH - 1) * gs + c - 1)
                        P.tensor_tensor(acc[0:r, :], p32[0:r, 0, :] if c == 1 else acc[0:r, :], p32[0:r, c % 4, :], ALU.add).then_inc(s["acc_done"], 1)
                    pool.wait_ge(s["o_hi"], gs + 1)
                    P.tensor_tensor(ost[:, st % 2, 1, :], o32[:], ost[:, st % 2, 0, :], ALU.subtract).then_inc(s["o_lo"], 1)

            with pool.Fori(0, B // 2) as it:
                body(it)


HT = -(-HID // 128)
HCUTS = ((0, 512), (512, 1024), (1024, HID))


def h_rows(t):
    return min(128, HID - 128 * t)


def prep_tasks():
    tasks = []
    for w in range(2):
        tasks += [("B", w, i) for i in range(3)]
        for t in range(HT + 1):
            tasks += [("E", w, t)] * (t < HT) + [("X", w, t - 1)] * (t >= 1)
    tasks += [("B", 2, 0)] + [("E", 2, (t, i)) for t in range(KC) for i in range(len(HCUTS))]
    tasks += [("X", 2, t) for t in range(HT)]
    return tasks


PREP = prep_tasks()


def ffn_phase(nc, dram):
    with ExitStack() as ctx:
        sb = lambda n, s, d=FP32: ctx.enter_context(nc.sbuf_tensor(n, s, d))
        sem = lambda n: ctx.enter_context(nc.semaphore(n))
        ident = sb("c_ident", [128, 128])
        zrow = sb("zrow", [1, 512], FP16)
        w13t = sb("w13t", [128, 2, 2, KC, HID], FP16)
        w2t = sb("w2t", [128, 2, HT, DM], FP16)
        xr = sb("xr_c", [TOK, B, DM])
        xt16 = sb("xt16", [128, 2, KC, NTOK], FP16)
        region = sb("region", [128, 28288])
        flat16 = region[:].bitcast(FP16)
        wn13 = region[:, 0:2 * HT * DM].rearrange("p (w t n) -> p w t n", w=2, t=HT)
        wn2 = region[:, 2 * HT * DM:2 * HT * DM + KC * HID].rearrange("p (t n) -> p t n", t=KC)
        at0 = 2 * HT * DM + KC * HID
        bn = region[:, at0:at0 + 3 * HT * RANK].rearrange("p (w t n) -> p w t n", w=3, t=HT)
        at1 = at0 + 3 * HT * RANK
        la = region[0:RANK, at1:at1 + HID]
        lb = region[0:RANK, at1 + HID:at1 + 2 * HID]
        la13 = sb("la13", [RANK, 2, DM])
        o16 = flat16[:, 0:2 * 2 * B * GQ].rearrange("p (s l b n) -> p s l b n", s=2, l=2, b=B)
        w0 = 2 * 2 * B * GQ
        wo16 = flat16[:, w0:w0 + 2 * 2 * G * DM].rearrange("p (s l g n) -> p s l g n", s=2, l=2, g=G)
        w1 = (w0 + 2 * 2 * G * DM) // 2
        wo32 = region[:, w1:w1 + G * DM].rearrange("p (g n) -> p g n", g=G)
        att = region[:, w1 + G * DM:w1 + G * DM + KC * NTOK].rearrange("p (c n) -> p c n", c=KC)
        g16 = flat16[:, 0:2 * HT * NTOK].rearrange("p (l t n) -> p l t n", l=2, t=HT)
        a = HT * NTOK
        sg = region[:, a:a + 2 * NTOK].rearrange("p (s n) -> p s n", s=2)
        g32 = region[:, a + 2 * NTOK:a + 4 * NTOK].rearrange("p (s n) -> p s n", s=2)
        z = sb("z_c", [TOK, 2, DM])
        stats, mv, ve, std = sb("stats_c", [TOK, 6]), sb("mv_c", [TOK, 2 * B, 2]), sb("ve_c", [TOK, 2 * B]), sb("std_c", [TOK, 2 * B])
        rstd, tmp1 = sb("rstd_c", [TOK, 2 * B]), sb("tmp1_c", [TOK, 1])
        ps = ctx.enter_context(nc.psum_tensor("ps_c", [128, 8, 512], FP32))

        names = ("w1_in", "w2_in", "w3_in", "id_in", "x1_in", "prep_mm", "prep_hi", "prep_done", "zrow_set", "wo_in0", "wo_in1",
                 "o_in0", "o_in1", "wo_hi", "wo_lo", "wo_mm", "proj_mm", "att_done", "turn_mm", "turn_used", "x2_done",
                 "x2T_mm", "x2T_hi", "x2T_done", "sqrt_in", "sqrt_out", "chain", "h_mm", "silu", "g_done", "g_hi", "g_lo",
                 "y_mm", "y_used", "y_done", "out_done")
        s = {n: sem("c_" + n) for n in names}
        w_in = (s["w1_in"], s["w3_in"], s["w2_in"])
        wo_in, o_in = (s["wo_in0"], s["wo_in1"]), (s["o_in0"], s["o_in1"])
        NP = len(PREP)
        x_ord = [i for i, t in enumerate(PREP) if t[0] == "X"]

        def x_operands(w, t):
            r = h_rows(t)
            if w < 2:
                return (lambda bank: bank.rearrange("p (c n) -> p c n", c=KC)[:, :, 0:r]), (lambda part: w13t[:, w, part, :, 128 * t:128 * t + r])
            return (lambda bank: bank[0:r, :]), (lambda part: w2t[0:r, part, t, :])

        block = ctx.enter_context(nc.Block())

        @block.sync
        def _(sp):
            sp.dma_start(ident[:], dram["ident"]).then_inc(s["id_in"], 16)
            full = 128 * (HT - 1)
            for w, (wn, ln, an) in enumerate((("w1", "lb1", "la1"), ("w3", "lb3", "la3"))):
                src, bsrc = dram[wn], dram[ln]
                sp.dma_start(bn[:, w, 0:HT - 1, :], bsrc[0:full].rearrange("(t p) n -> p t n", p=128)).then_inc(w_in[w], 16)
                sp.dma_start(bn[0:HID - full, w, HT - 1, :], bsrc[full:HID]).then_inc(w_in[w], 16)
                sp.dma_start(la13[:, w, :], dram[an]).then_inc(w_in[w], 16)
                sp.dma_start(wn13[:, w, 0:HT - 1, :], src[0:full].rearrange("(t p) n -> p t n", p=128)).then_inc(w_in[w], 16)
                sp.dma_start(wn13[0:HID - full, w, HT - 1, :], src[full:HID]).then_inc(w_in[w], 16)
            sp.dma_start(bn[:, 2, 0:KC, :], dram["lb2"].rearrange("(t p) n -> p t n", p=128)).then_inc(w_in[2], 16)
            sp.dma_start(la, dram["la2"]).then_inc(w_in[2], 16)
            sp.dma_start(wn2, dram["w2"].rearrange("(t p) n -> p t n", p=128)).then_inc(w_in[2], 16)
            sp.dma_start(xr[:], dram["x1_d"]).then_inc(s["x1_in"], 16)
            sp.wait_ge(s["prep_done"], NP)

            wo_v = dram["wo"].rearrange("(k g p) n -> k p g n", k=NKV, g=G)

            def load_o(kv, sl):
                for part in range(2):
                    sp.dma_start(o16[:, sl, part], dram["o_d"][part, bass.ds(kv, 1)].rearrange("k b p n -> (k p) b n")).then_inc(o_in[sl], 16)

            def load_wo(kv, sl):
                sp.dma_start(wo32, wo_v[bass.ds(kv, 1)].rearrange("k p g n -> (k p) g n")).then_inc(wo_in[sl], 16)

            load_wo(0, 0)
            load_o(0, 0)
            load_o(1, 1)

            def body(j, last=False):
                sp.wait_ge(s["wo_lo"], 2 * j + 1)
                load_wo(2 * j + 1, 1)
                if not last:
                    sp.wait_ge(s["wo_lo"], 2 * j + 2)
                    load_wo(2 * j + 2, 0)
                    for sl in range(2):
                        sp.wait_ge(s["wo_mm"], 2 * j + sl + 1)
                        load_o(2 * j + 2 + sl, sl)

            body(0)
            body(1, last=True)
            for b in range(B):
                sp.wait_ge(s["y_done"], b + 1)
                sp.dma_start(dram["out"][b], xr[:, b, :]).then_inc(s["out_done"], 16)
            sp.wait_ge(s["out_done"], 16 * B)

        @block.tensor
        def _(pe):
            T = nc.tensor
            pe.wait_ge(s["id_in"], 16)
            e_done = {(t[1], t[2]): i for i, t in enumerate(PREP) if t[0] == "E"}
            b_done = {(t[1], t[2]): i for i, t in enumerate(PREP) if t[0] == "B"}
            for n, (kind, w, i) in enumerate(PREP):
                if n >= 8:
                    pe.wait_ge(s["prep_done"], n - 7)
                bank = ps[:, n % 8, :]
                if kind == "B":
                    if i == 0:
                        pe.wait_ge(w_in[w], 80 if w < 2 else 48)
                    for t in range(4 * i, min(4 * i + 4, HT if w < 2 else KC)):
                        r = h_rows(t) if w < 2 else 128
                        mm = T.transpose(bank[0:RANK, 128 * (t % 4):128 * (t % 4) + r], bn[0:r, w, t, :], ident[0:r, 0:r])
                elif kind == "E":
                    if w < 2:
                        pe.wait_ge(s["prep_done"], b_done[(w, 2)] + 1)
                        mm = T.matmul(bank[0:h_rows(i), :], lb[:, 128 * i:128 * i + h_rows(i)], la13[:, w, :], start=True, stop=True)
                    else:
                        pe.wait_ge(s["prep_done"], b_done[(2, 0)] + 1)
                        t, cut = i
                        c0, c1 = HCUTS[cut]
                        mm = T.matmul(bank[:, 0:c1 - c0], lb[:, 128 * t:128 * (t + 1)], la[:, c0:c1], start=True, stop=True)
                else:
                    r = h_rows(i)
                    if w < 2:
                        pe.wait_ge(s["prep_done"], e_done[(w, i)] + 1)
                        for c in range(KC):
                            mm = T.transpose(bank[:, 128 * c:128 * c + r], wn13[0:r, w, i, 128 * c:128 * (c + 1)], ident[0:r, 0:r])
                    else:
                        pe.wait_ge(s["prep_done"], e_done[(2, (KC - 1, len(HCUTS) - 1))] + 1)
                        for t in range(KC):
                            mm = T.transpose(bank[0:r, 128 * t:128 * (t + 1)], wn2[:, t, 128 * i:128 * i + r], ident[:])
                mm.then_inc(s["prep_mm"], 1)
            pe.wait_ge(s["prep_done"], NP)
            pe.wait_ge(s["zrow_set"], 1)

            def edge(stop):
                for k in range(8):
                    mm = T.matmul(ps[:, k, 0:TH], zrow[:, 0:128], zrow[:, 0:TH], start=not stop, stop=stop)
                return mm

            edge(False)

            def body(j):
                for sl in range(2):
                    pe.wait_ge(s["wo_lo"], 2 * j + sl + 1)
                    pe.wait_ge(o_in[sl], 32 * j + 32)
                    for g in range(G):
                        for m in range(KC):
                            for wp, op in PARTS:
                                for hf in range(2):
                                    mm = T.matmul(ps[:, 2 * m + hf, 0:TH], wo16[:, sl, wp, g, 128 * m:128 * (m + 1)],
                                                  o16[:, sl, op, 4 * hf:4 * hf + 4, TOK * g:TOK * (g + 1)], start=False, stop=False)
                    mm.then_inc(s["wo_mm"], 1)

            with pe.Fori(0, NKV // 2) as j:
                body(j)
            edge(True).then_inc(s["proj_mm"], 1)
            pe.wait_ge(s["att_done"], 2 * KC)

            def x2_turn(b):
                pe.wait_ge(s["x2_done"], b + 1)
                if b >= 2:
                    pe.wait_ge(s["x2T_done"], b - 1)
                for c in range(KC):
                    mm = T.transpose(ps[:, 2 + b % 2, 128 * c:128 * c + TOK], xr[:, b, 128 * c:128 * (c + 1)], ident[0:TOK, 0:TOK])
                mm.then_inc(s["x2T_mm"], 1)

            for b in range(B):
                if b >= 2:
                    pe.wait_ge(s["turn_used"], b - 1)
                for c in range(KC):
                    mm = T.transpose(ps[0:TOK, b % 2, 128 * c:128 * (c + 1)], att[:, c, TOK * b:TOK * (b + 1)], ident[:])
                mm.then_inc(s["turn_mm"], 1)
                if b >= 1:
                    x2_turn(b - 1)
            x2_turn(B - 1)
            pe.wait_ge(s["x2T_done"], B)
            for t in range(HT):
                r, k0 = h_rows(t), 4 * (t % 2)
                if t >= 2:
                    pe.wait_ge(s["g_done"], t - 1)
                for w in range(2):
                    for n, (wp, xp) in enumerate(PARTS):
                        for c in range(KC):
                            for hf in range(2):
                                mm = T.matmul(ps[0:r, k0 + 2 * w + hf, 0:TH], w13t[:, w, wp, c, 128 * t:128 * t + r],
                                              xt16[:, xp, c, TH * hf:TH * (hf + 1)], start=(n == 0 and c == 0), stop=(n == 2 and c == KC - 1))
                mm.then_inc(s["h_mm"], 1)
            pe.wait_ge(s["g_lo"], HT)
            for b in range(B):
                if b >= 2:
                    pe.wait_ge(s["y_used"], b - 1)
                for n, (gp, wp) in enumerate(PARTS):
                    for t in range(HT):
                        r = h_rows(t)
                        mm = T.matmul(ps[0:TOK, b % 2, :], g16[0:r, gp, t, TOK * b:TOK * (b + 1)], w2t[0:r, wp, t, :],
                                      start=(n == 0 and t == 0), stop=(n == 2 and t == HT - 1))
                mm.then_inc(s["y_mm"], 1)

        @block.scalar
        def _(act):
            A = nc.scalar
            for n, (kind, w, i) in enumerate(PREP):
                if kind == "X":
                    cols, dst = x_operands(w, i)
                    act.wait_ge(s["prep_mm"], n + 1)
                    A.mul(dst(0), cols(ps[:, n % 8, :]), SW).then_inc(s["prep_hi"], 1)

            def split(kv, sl):
                act.wait_ge(wo_in[sl], 16 * (kv // 2) + 16)
                if kv >= 2:
                    act.wait_ge(s["wo_mm"], kv - 1)
                A.mul(wo16[:, sl, 0], wo32, SW).then_inc(s["wo_hi"], 1)

            for kv in range(NKV):
                split(kv, kv % 2)
            act.wait_ge(s["proj_mm"], 1)
            for k in range(2 * KC):
                A.mul(att[:, k // 2, TH * (k % 2):TH * (k % 2 + 1)], ps[:, k, 0:TH], 1.0 / (SO * SW)).then_inc(s["att_done"], 1)

            def x2t_hi(b):
                act.wait_ge(s["x2T_mm"], b + 1)
                A.mul(xt16[:, 0, :, b * TOK:(b + 1) * TOK],
                      ps[:, 2 + b % 2, :].rearrange("p (c n) -> p c n", c=KC)[:, :, 0:TOK], SX).then_inc(s["x2T_hi"], 1)

            for b in range(B):
                act.wait_ge(s["sqrt_in"], b + 1)
                A.activation(std[:, b:b + 1], ve[:, b:b + 1], ACT.Sqrt).then_inc(s["sqrt_out"], 1)
                if b >= 1:
                    x2t_hi(b - 1)
            x2t_hi(B - 1)

            def g_high(t):
                r = h_rows(t)
                act.wait_ge(s["g_done"], t + 1)
                A.copy(g16[0:r, 0, t, :], g32[0:r, t % 2, :]).then_inc(s["g_hi"], 1)

            for t in range(HT):
                r, k0 = h_rows(t), 4 * (t % 2)
                act.wait_ge(s["h_mm"], t + 1)
                A.activation(sg[0:r, t % 2, :].rearrange("p (a n) -> p a n", a=2), ps[0:r, k0:k0 + 2, 0:TH], ACT.Silu,
                             scale=1.0 / (SX * SW)).then_inc(s["silu"], 1)
                if t >= 1:
                    g_high(t - 1)
            g_high(HT - 1)
            for b in range(B):
                act.wait_ge(s["sqrt_in"], B + b + 1)
                A.activation(std[:, B + b:B + b + 1], ve[:, B + b:B + b + 1], ACT.Sqrt).then_inc(s["sqrt_out"], 1)

        @block.vector
        def _(dve):
            V = nc.vector
            link = split_chain(dve, s["chain"])
            V.memset(zrow[:], 0.0).then_inc(s["zrow_set"], 1)
            for n, (kind, w, i) in enumerate(PREP):
                bank = ps[:, n % 8, :]
                if kind == "B":
                    dve.wait_ge(s["prep_mm"], n + 1)
                    c0, c1 = 512 * i, min(512 * i + 512, HID if w < 2 else DM)
                    V.tensor_copy(lb[:, c0:c1], bank[0:RANK, 0:c1 - c0]).then_inc(s["prep_done"], 1)
                elif kind == "E":
                    dve.wait_ge(s["prep_mm"], n + 1)
                    if w < 2:
                        wn, pr = wn13[0:h_rows(i), w, i, :], bank[0:h_rows(i), :]
                    else:
                        c0, c1 = HCUTS[i[1]]
                        wn, pr = wn2[:, i[0], c0:c1], bank[:, 0:c1 - c0]
                    V.scalar_tensor_tensor(wn, pr, LORA, wn, ALU.mult, ALU.add).then_inc(s["prep_done"], 1)
                else:
                    cols, dst = x_operands(w, i)
                    dve.wait_ge(s["prep_hi"], x_ord.index(n) + 1)
                    V.scalar_tensor_tensor(dst(1), cols(bank), SW, dst(0), ALU.mult, ALU.subtract).then_inc(s["prep_done"], 1)
            for kv in range(NKV):
                sl = kv % 2
                dve.wait_ge(s["wo_hi"], kv + 1)
                V.scalar_tensor_tensor(wo16[:, sl, 1].rearrange("p g n -> p (g n)"), wo32.rearrange("p g n -> p (g n)"), SW,
                                       wo16[:, sl, 0].rearrange("p g n -> p (g n)"), ALU.mult, ALU.subtract).then_inc(s["wo_lo"], 1)

            def x2t_lo(b):
                dve.wait_ge(s["x2T_hi"], b + 1)
                V.scalar_tensor_tensor(xt16[:, 1, :, b * TOK:(b + 1) * TOK],
                                       ps[:, 2 + b % 2, :].rearrange("p (c n) -> p c n", c=KC)[:, :, 0:TOK], SX,
                                       xt16[:, 0, :, b * TOK:(b + 1) * TOK], ALU.mult, ALU.subtract).then_inc(s["x2T_done"], 1)

            def normalise(n, b, ready, used, bank, scale, done):
                dve.wait_ge(ready, b + 1)
                V.scalar_tensor_tensor(z[:, b % 2], bank, scale, xr[:, b, :], ALU.mult, ALU.add).then_inc(used, 1)
                dve.wait_ge(used, b + 1)
                layernorm_rows(nc, dve, s["sqrt_in"], s["sqrt_out"], link, z[:, b % 2], stats[:], mv[:, n, :],
                               ve[:, n:n + 1], std[:, n:n + 1], rstd[:, n:n + 1], tmp1[:], n)
                V.tensor_scalar(xr[:, b, :], z[:, b % 2], mv[:, n, 0:1], rstd[:, n:n + 1], ALU.subtract, ALU.mult).then_inc(done, 1)

            dve.wait_ge(s["x1_in"], 16)
            for b in range(B):
                normalise(b, b, s["turn_mm"], s["turn_used"], ps[0:TOK, b % 2, :], 1.0, s["x2_done"])
                if b >= 1:
                    x2t_lo(b - 1)
            x2t_lo(B - 1)

            def g_low(t):
                r = h_rows(t)
                dve.wait_ge(s["g_hi"], t + 1)
                V.tensor_tensor(g16[0:r, 1, t, :], g32[0:r, t % 2, :], g16[0:r, 0, t, :], ALU.subtract).then_inc(s["g_lo"], 1)

            for t in range(HT):
                r, k0 = h_rows(t), 4 * (t % 2)
                dve.wait_ge(s["silu"], t + 1)
                if t >= 2:
                    dve.wait_ge(s["g_lo"], t - 1)
                V.scalar_tensor_tensor(g32[0:r, t % 2, :].rearrange("p (a n) -> p a n", a=2), ps[0:r, k0 + 2:k0 + 4, 0:TH],
                                       SG / (SX * SW), sg[0:r, t % 2, :].rearrange("p (a n) -> p a n", a=2),
                                       ALU.mult, ALU.mult).then_inc(s["g_done"], 1)
                if t >= 1:
                    g_low(t - 1)
            g_low(HT - 1)
            for b in range(B):
                normalise(B + b, b, s["y_mm"], s["y_used"], ps[0:TOK, b % 2, :], 1.0 / (SG * SW), s["y_done"])


def build(nc, dram):
    scratch = lambda n, s, d=FP32: nc.dram_tensor(n, s, d).ap()
    dram["kpad"] = scratch("kpad", (1, 128 + DM))
    dram["x1_d"] = scratch("x1_d", (TOK, B, DM))
    dram["x1t_d"] = scratch("x1t_d", (2, 128, KC, NTOK), FP16)
    dram["q_d"] = scratch("q_d", (2, B * NKV, 128, GQ), FP16)
    dram["o_d"] = scratch("o_d", (2, NKV, B, 128, GQ), FP16)
    s4_and_queries(nc, dram)
    attention(nc, dram)
    ffn_phase(nc, dram)


_INS = {"x": "x", "ctx_4096": "ctx", "L0_attn_Lambda_ri": "lam", "L0_attn_p_ri": "p", "L0_attn_q_ri": "q",
        "L0_attn_Vc_ri": "vc", "L0_attn_Ct_ri": "ct", "L0_attn_Bp": "bp", "L0_attn_D": "dskip",
        "L0_attn_log_step": "ls", "L0_xattn_Wq": "wq", "L0_xattn_Wk": "wk", "L0_xattn_Wv": "wv", "L0_xattn_Wo": "wo",
        "L0_ffn_w1": "w1", "L0_ffn_w3": "w3", "L0_ffn_w2": "w2", "L0_ffn_lora_A1": "la1", "L0_ffn_lora_B1": "lb1",
        "L0_ffn_lora_A3": "la3", "L0_ffn_lora_B3": "lb3", "L0_ffn_lora_A2": "la2", "L0_ffn_lora_B2": "lb2"}


def shape_tables():
    m = np.arange(DM)
    th = 2 * np.pi * m / DM
    omega = np.stack([1 - np.cos(th), 1 + np.cos(th), np.sin(th)])
    omega[:2] = np.abs(omega[:2])
    wpl = np.stack([(1 + np.cos(th)).reshape(KC, 128).T, (-np.sin(th)).reshape(KC, 128).T], axis=1)
    ang = 2 * np.pi * np.outer(np.arange(128), m) / DM
    dft = np.stack([np.cos(ang), -np.sin(ang)], axis=1) * (2.0 / DM)
    return {"omega": omega.astype(np.float32), "wpl": wpl.astype(np.float32), "dft": dft.astype(np.float32),
            "ident": np.eye(128, dtype=np.float32)}


def kernel(**inputs):
    import numpy as _np
    import concourse.bacc as _bacc
    from concourse import mybir as _mybir
    from concourse.bass_utils import run_bass_kernel_spmd as _run

    nc = _bacc.Bacc("TRN2", target_bir_lowering=False, num_devices=1, dynamic_dma_scratch_size=1024)
    arrays, dram = {}, {}
    given = {short: inputs[name] for name, short in _INS.items()} | shape_tables()
    for short, a in given.items():
        a = _np.ascontiguousarray(a)
        arrays[f"in_{short}_dram"] = a
        dram[short] = nc.dram_tensor(f"in_{short}_dram", a.shape, _mybir.dt.from_np(a.dtype), kind="ExternalInput").ap()
    dram["out"] = nc.dram_tensor("out_0_dram", (B, TOK, DM), FP32, kind="ExternalOutput").ap()
    build(nc, dram)
    r = _run(nc, [arrays], core_ids=[0])
    return r.results[0]["out_0_dram"]
```

```python
import math
from contextlib import ExitStack

import numpy as np
import concourse.bass as bass
from concourse import mybir

FP32 = mybir.dt.float32
FP16 = mybir.dt.float16
BF16 = mybir.dt.bfloat16
ALU = mybir.AluOpType
ACT = mybir.ActivationFunctionType
AX = mybir.AxisListType

B, TOK, DM = 8, 100, 512
NTOK = B * TOK
CTX = 1444
KEYS = CTX + TOK
NH, NKV, HD = 32, 4, 128
G = NH // NKV
HID, RANK = 1376, 16
NST = 64
KC = DM // 128
EPS = 1e-5
LORA = 2.0

NCH = -(-KEYS // 128)
LASTK = KEYS - 128 * (NCH - 1)
NCT = -(-CTX // 128)
KT_N = KEYS // 4
GQ = G * TOK
HALF = GQ // 2
TH = NTOK // 2

SX = 32.0
SW = 512.0
SQ = 32.0
SP_LOG2 = 13
SO = 256.0
SG = 64.0
SR = 1024.0


def ch_rows(c):
    return 128 if c < NCH - 1 else LASTK


def split_chain(eng, sem):
    count = [0]

    def link(ins):
        count[0] += 1
        ins.then_inc(sem, 1)
        eng.wait_ge(sem, count[0])

    return link


def layernorm_rows(nc, dve, act_sqrt_ready, act_sqrt_done, link, z, stats, mv, var_eps, std, rstd, tmp, n):
    link(nc.vector.bn_stats(stats, z))
    link(nc.vector.bn_aggr(mv, stats))
    nc.vector.tensor_scalar(var_eps, mv[:, 1:2], EPS, None, ALU.add).then_inc(act_sqrt_ready, 1)
    dve.wait_ge(act_sqrt_done, n + 1)
    link(nc.vector.reciprocal(rstd, std))
    link(nc.vector.tensor_tensor(tmp, rstd, rstd, ALU.mult))
    dve.wait_ge(act_sqrt_ready, n + 1)
    link(nc.vector.tensor_tensor(tmp, tmp, var_eps, ALU.mult))
    link(nc.vector.tensor_scalar(tmp, tmp, -0.5, 1.5, ALU.mult, ALU.add))
    link(nc.vector.tensor_tensor(rstd, rstd, tmp, ALU.mult))


def s4_and_queries(nc, dram):
    with ExitStack() as ctx:
        sb = lambda n, s, d=FP32: ctx.enter_context(nc.sbuf_tensor(n, s, d))
        sem = lambda n: ctx.enter_context(nc.semaphore(n))
        ident = sb("a_ident", [128, 128])
        lam, pq, ct = sb("lam", [NST, 2]), sb("pq", [NST, 2, 2]), sb("ct", [NST, 2])
        vc, bp = sb("vc", [NST, NST, 2]), sb("bp", [NST, NST])
        vcb, bpair = sb("vcb", [NST, NST, 2]), sb("bpair", [NST, 2, 2])
        bswap = sb("bswap", [NST, 2, 2])
        num, numx = sb("num", [NST, 2, 2, 2]), sb("numx", [NST, 2, 2, 2])
        ls, alpha, nlam, alr = sb("ls", [NST, 1]), sb("alpha", [NST, 1]), sb("nlam", [NST, 2]), sb("alr", [NST, 1])
        els = sb("els", [NST, 1])
        omega = sb("omega", [NST, 3, DM])
        dre, dim, tmpa, tmpb = (sb(f"s4_{n}", [NST, DM]) for n in ("dre", "dim", "ta", "tb"))
        rre, rim = sb("s4_rre", [NST, DM]), sb("s4_rim", [NST, DM])
        ksum = sb("ksum", [128, KC, 4, 2])
        wpl = sb("wpl", [128, 2, KC])
        cx = [sb(f"cx{i}", [128, 2, KC]) for i in range(8)]
        cxt = sb("cxt", [128, 2, KC])
        bfly, bt = sb("bfly", [128, 2, 4]), sb("bt", [128, 4, 2])
        dft = sb("dft", [128, 2, DM])
        krow = sb("krow", [1, 128 + DM])
        toep = sb("toep", [128, DM])
        dsk, dsk1 = sb("dsk", [TOK, 1]), sb("dsk1", [TOK, 1])
        xs, xr, x1 = (sb(n, [TOK, B, DM]) for n in ("xs", "xr", "x1"))
        xt = sb("xt", [128, KC, NTOK])
        z = sb("z", [TOK, 2, DM])
        stats, mv, ve, std = sb("stats", [TOK, 6]), sb("mv", [TOK, B, 2]), sb("ve", [TOK, B]), sb("std", [TOK, B])
        rstd, tmp1 = sb("rstd", [TOK, B]), sb("tmp1", [TOK, 1])
        x1t = sb("x1t", [128, 2, KC, NTOK], FP16)
        wq32 = sb("wq32", [128, 2, KC, 512])
        wq16 = sb("wq16", [128, 2, 2, KC, 512], FP16)
        qst = sb("qst", [128, 2, B, GQ], FP16)
        ring = ctx.enter_context(nc.psum_tensor("a_ring", [128, 2, 2, 512], FP32))
        pmisc = ctx.enter_context(nc.psum_tensor("a_misc", [128, 4, 512], FP32))

        names = ("xr_done", "x_in", "param_in", "table_in", "dft_in", "alpha_exp", "dve_chain", "res_done", "ksum_mm",
                 "bfly_done", "kt_mm", "krow_done", "krow_out", "toep_in", "xT_mm", "xT_done", "y_mm", "y_used",
                 "sqrt_in", "sqrt_out", "x1_done", "x1T_mm", "ring_hi", "ring_free", "x1_out",
                 "wsplit_hi", "wsplit_done", "q_mm", "wq_in0", "wq_in1", "store0", "store1")
        s = {n: sem("a_" + n) for n in names}
        wq_in = (s["wq_in0"], s["wq_in1"])
        stores = (s["store0"], s["store1"])
        wq_v = dram["wq"].rearrange("(c p) n -> p c n", c=KC)
        qd = dram["q_d"].rearrange("l (b k) p n -> l k p b n", k=NKV)
        def qst_half(part, h, hf):
            return qst[:, part, 4 * hf:4 * hf + 4, h * TOK:(h + 1) * TOK]

        def ring_half(h, hf):
            return ring[:, h % 2, hf, 0:TH].rearrange("p (b n) -> p b n", n=TOK)

        def x1t_lo(V, dve, b):
            dve.wait_ge(s["ring_hi"], b + 1)
            V.scalar_tensor_tensor(x1t[:, 1, :, b * TOK:(b + 1) * TOK], ring[:, b % 2, 0, :].rearrange("p (c n) -> p c n", c=KC)[:, :, 0:TOK],
                                   SX, x1t[:, 0, :, b * TOK:(b + 1) * TOK], ALU.mult, ALU.subtract).then_inc(s["ring_free"], 1)

        def q_schedule(eng, split, evac):
            def group(j, last=False):
                split(j, 1)
                for h in range(4):
                    evac(j, h)
                if not last:
                    split(j + 1, 0)
                for h in range(4, G):
                    evac(j, h)
            split(0, 0)
            with eng.Fori(0, NKV - 1) as j:
                group(j)
            group(NKV - 1, last=True)

        def x1t_hi(A, act, b):
            act.wait_ge(s["x1T_mm"], b + 1)
            A.mul(x1t[:, 0, :, b * TOK:(b + 1) * TOK],
                  ring[:, b % 2, 0, :].rearrange("p (c n) -> p c n", c=KC)[:, :, 0:TOK], SX).then_inc(s["ring_hi"], 1)

        block = ctx.enter_context(nc.Block())

        @block.sync
        def _(sp):
            sp.dma_start(vc[:], dram["vc"]).then_inc(s["param_in"], 16)
            for dst, src in ((lam[:], dram["lam"]), (pq[:, 0, :], dram["p"]), (pq[:, 1, :], dram["q"]),
                             (ct[:], dram["ct"][0])):
                sp.dma_start(dst, src).then_inc(s["param_in"], 16)
            sp.dma_start(bp[:], dram["bp"].rearrange("k o -> o k").to_broadcast([NST, NST])).then_inc(s["param_in"], 16)
            sp.dma_start(ls[:], dram["ls"][None, :].to_broadcast([NST, 1])).then_inc(s["param_in"], 16)
            sp.dma_start(dsk[:], dram["dskip"][None, :].to_broadcast([TOK, 1])).then_inc(s["param_in"], 16)
            sp.dma_start(omega[:], dram["omega"][None, :, :].to_broadcast([NST, 3, DM])).then_inc(s["table_in"], 16)
            sp.dma_start(ident[:], dram["ident"]).then_inc(s["x_in"], 16)
            sp.dma_start(xs[:], dram["x"].rearrange("b t d -> t b d")).then_inc(s["x_in"], 16)
            sp.dma_start(wpl[:], dram["wpl"]).then_inc(s["dft_in"], 16)
            sp.dma_start(dft[:], dram["dft"]).then_inc(s["dft_in"], 16)
            for tl in range(2):
                sp.dma_start(wq32[:, tl], wq_v[:, :, 512 * tl:512 * (tl + 1)]).then_inc(wq_in[tl], 16)
            sp.wait_ge(s["krow_done"], 1)
            sp.dma_start(dram["kpad"], krow[:]).then_inc(s["krow_out"], 16)
            sp.wait_ge(s["krow_out"], 16)
            sp.dma_start(toep[:], bass.AP(dram["kpad"].tensor, 1, [[1, 128], [1, DM]])).then_inc(s["toep_in"], 16)
            for b in range(B):
                sp.wait_ge(s["x1_done"], b + 1)
                sp.dma_start(dram["x1_d"][:, b, :], x1[:, b, :]).then_inc(s["x1_out"], 16)
            sp.wait_ge(s["ring_free"], B)
            for part in range(2):
                sp.dma_start(dram["x1t_d"][part], x1t[:, part]).then_inc(stores[part], 16)

            def group(j, last=False):
                for tl in range(2):
                    if not last:
                        sp.wait_ge(s["wsplit_done"], 2 * j + tl + 1)
                        sp.dma_start(wq32[:, tl], wq_v[:, :, bass.ds(1024 * j + 1024 + 512 * tl, 512)]).then_inc(wq_in[tl], 16)
                for tl in range(2):
                    sp.wait_ge(s["ring_free"], B + G * j + 4 * tl + 4)
                    for part in range(2):
                        sp.dma_start(qd[part, bass.ds(j, 1), :, :, 400 * tl:400 * (tl + 1)].rearrange("o p b n -> (o p) b n"),
                                     qst[:, part, :, 400 * tl:400 * (tl + 1)]).then_inc(stores[tl], 16)

            with sp.Fori(0, NKV - 1) as j:
                group(j)
            group(NKV - 1, last=True)
            for tl in range(2):
                sp.wait_ge(stores[tl], 16 + 32 * NKV)
            sp.wait_ge(s["x1_out"], 16 * B)

        @block.vector
        def _(dve):
            link = split_chain(dve, s["dve_chain"])
            V = nc.vector
            dve.wait_ge(s["param_in"], 16 * 8)
            link(V.tensor_tensor(vcb[:], vc[:], bp[:].rearrange("n (k o) -> n k o", o=1).to_broadcast([NST, NST, 2]), ALU.mult))
            link(V.tensor_reduce(bpair[:, 0, :], vcb[:].rearrange("n k c -> n c k"), AX.X, ALU.add))
            link(V.tensor_copy(bpair[:, 1, :], pq[:, 0, :]))
            link(V.tensor_copy(bswap[:, :, 0], bpair[:, :, 1]))
            link(V.tensor_scalar(bswap[:, :, 1], bpair[:, :, 0], -1.0, None, ALU.mult))
            for a, src in enumerate((ct[:], pq[:, 1, :])):
                link(V.tensor_scalar(num[:, a], bpair[:], src[:, 0:1], None, ALU.mult))
                link(V.scalar_tensor_tensor(num[:, a], bswap[:], src[:, 1:2], num[:, a], ALU.mult, ALU.add))
            link(V.tensor_scalar(numx[:, :, :, 0], num[:, :, :, 1], -1.0, None, ALU.mult))
            link(V.tensor_copy(numx[:, :, :, 1], num[:, :, :, 0]))
            link(V.tensor_scalar(nlam[:], lam[:], -1.0, None, ALU.mult))
            dve.wait_ge(s["alpha_exp"], 1)
            link(V.tensor_scalar(alpha[:], els[:], 2.0, None, ALU.mult))
            link(V.tensor_tensor(alr[:], alpha[:], lam[:, 0:1], ALU.add))
            link(V.tensor_scalar(dsk1[:], dsk[:], 1.0, None, ALU.add))
            dve.wait_ge(s["table_in"], 16)
            one_m, one_p, sin = omega[:, 0, :], omega[:, 1, :], omega[:, 2, :]
            link(V.tensor_scalar(tmpa[:], one_m, alpha[:], None, ALU.mult))
            link(V.scalar_tensor_tensor(tmpa[:], sin, nlam[:, 1:2], tmpa[:], ALU.mult, ALU.add))
            link(V.scalar_tensor_tensor(dre[:], one_p, nlam[:, 0:1], tmpa[:], ALU.mult, ALU.add))
            link(V.tensor_scalar(tmpb[:], sin, alr[:], None, ALU.mult))
            link(V.scalar_tensor_tensor(dim[:], one_p, nlam[:, 1:2], tmpb[:], ALU.mult, ALU.add))
            link(V.tensor_tensor(tmpa[:], dre[:], dre[:], ALU.mult))
            link(V.tensor_tensor(tmpb[:], dim[:], dim[:], ALU.mult))
            link(V.tensor_tensor(tmpa[:], tmpa[:], tmpb[:], ALU.add))
            link(V.reciprocal(tmpb[:], tmpa[:]))
            link(V.tensor_tensor(rre[:], dre[:], tmpb[:], ALU.mult))
            V.scalar_tensor_tensor(rim[:], dim[:], -1.0, tmpb[:], ALU.mult, ALU.mult).then_inc(s["res_done"], 1)
            dve.wait_ge(s["ksum_mm"], 1)
            link(V.tensor_copy(ksum[:], pmisc[:, 0, 0:KC * 8].rearrange("p (c v r) -> p c v r", c=KC, v=4)))
            dve.wait_ge(s["dft_in"], 32)
            kv = [ksum[:, :, v, :].rearrange("p c r -> p r c") for v in range(4)]

            def cmul(dst, a, b):
                link(V.tensor_tensor(dst[:, 0, :], a[:, 0, :], b[:, 0, :], ALU.mult))
                link(V.tensor_tensor(cxt[:, 0, :], a[:, 1, :], b[:, 1, :], ALU.mult))
                link(V.tensor_tensor(dst[:, 0, :], dst[:, 0, :], cxt[:, 0, :], ALU.subtract))
                link(V.tensor_tensor(dst[:, 1, :], a[:, 0, :], b[:, 1, :], ALU.mult))
                link(V.tensor_tensor(cxt[:, 1, :], a[:, 1, :], b[:, 0, :], ALU.mult))
                link(V.tensor_tensor(dst[:, 1, :], dst[:, 1, :], cxt[:, 1, :], ALU.add))

            wk11, k0110, nume, quot = cx[0], cx[1], cx[2], cx[3]
            cmul(wk11, wpl[:], kv[3])
            link(V.tensor_scalar(wk11[:, 0, :], wk11[:, 0, :], 1.0, None, ALU.add))
            cmul(k0110, kv[1], kv[2])
            cmul(nume, wpl[:], k0110[:])
            sq, inv, conj = cx[4], cx[5], cx[6]
            link(V.tensor_tensor(sq[:], wk11[:], wk11[:], ALU.mult))
            link(V.tensor_tensor(inv[:, 0, :], sq[:, 0, :], sq[:, 1, :], ALU.add))
            link(V.reciprocal(inv[:, 1, :], inv[:, 0, :]))
            link(V.tensor_tensor(conj[:, 0, :], wk11[:, 0, :], inv[:, 1, :], ALU.mult))
            link(V.scalar_tensor_tensor(conj[:, 1, :], wk11[:, 1, :], -1.0, inv[:, 1, :], ALU.mult, ALU.mult))
            cmul(quot, nume[:], conj[:])
            at = cx[7]
            link(V.tensor_tensor(at[:], kv[0], quot[:], ALU.subtract))
            s02, d02, s13, d13 = (bt[:, i, :] for i in range(4))
            link(V.tensor_tensor(s02, at[:, :, 0], at[:, :, 2], ALU.add))
            link(V.tensor_tensor(d02, at[:, :, 0], at[:, :, 2], ALU.subtract))
            link(V.tensor_tensor(s13, at[:, :, 1], at[:, :, 3], ALU.add))
            link(V.tensor_tensor(d13, at[:, :, 1], at[:, :, 3], ALU.subtract))
            link(V.tensor_tensor(bfly[:, :, 0], s02, s13, ALU.add))
            link(V.tensor_tensor(bfly[:, :, 2], s02, s13, ALU.subtract))
            link(V.tensor_tensor(bfly[:, 0, 1:2], d02[:, 0:1], d13[:, 1:2], ALU.subtract))
            link(V.tensor_tensor(bfly[:, 1, 1:2], d02[:, 1:2], d13[:, 0:1], ALU.add))
            link(V.tensor_tensor(bfly[:, 0, 3:4], d02[:, 0:1], d13[:, 1:2], ALU.add))
            link(V.tensor_tensor(bfly[:, 1, 3:4], d02[:, 1:2], d13[:, 0:1], ALU.subtract))
            V.memset(krow[0:1, 0:128], 0.0).then_inc(s["bfly_done"], 1)
            dve.wait_ge(s["kt_mm"], 1)
            V.tensor_copy(krow[0:1, 128:].rearrange("o (u r) -> o u r", r=4),
                          pmisc[0:1, 1, :].rearrange("o (r u) -> o u r", r=4)).then_inc(s["krow_done"], 1)
            for b in range(B):
                dve.wait_ge(s["y_mm"], b + 1)
                V.scalar_tensor_tensor(z[:, b % 2], xs[:, b, :], dsk1[:], pmisc[0:TOK, 2 + b % 2, :],
                                       ALU.mult, ALU.add).then_inc(s["y_used"], 1)
                dve.wait_ge(s["y_used"], b + 1)
                layernorm_rows(nc, dve, s["sqrt_in"], s["sqrt_out"], link, z[:, b % 2], stats[:], mv[:, b, :],
                               ve[:, b:b + 1], std[:, b:b + 1], rstd[:, b:b + 1], tmp1[:], b)
                V.tensor_scalar(x1[:, b, :], z[:, b % 2], mv[:, b, 0:1], rstd[:, b:b + 1],
                                ALU.subtract, ALU.mult).then_inc(s["x1_done"], 1)
                if b >= 1:
                    x1t_lo(V, dve, b - 1)
            x1t_lo(V, dve, B - 1)

            def split_lo(j, tl):
                dve.wait_ge(s["wsplit_hi"], 2 * j + tl + 1)
                V.scalar_tensor_tensor(wq16[:, tl, 1].rearrange("p c n -> p (c n)"), wq32[:, tl].rearrange("p c n -> p (c n)"), SW,
                                       wq16[:, tl, 0].rearrange("p c n -> p (c n)"), ALU.mult, ALU.subtract).then_inc(s["wsplit_done"], 1)

            def evac(j, h):
                dve.wait_ge(s["ring_hi"], B + G * j + h + 1)
                for hf in range(2):
                    lo = V.scalar_tensor_tensor(qst_half(1, h, hf), ring_half(h, hf), SQ / (SX * SW), qst_half(0, h, hf),
                                                ALU.mult, ALU.subtract)
                lo.then_inc(s["ring_free"], 1)

            q_schedule(dve, split_lo, evac)

        @block.scalar
        def _(act):
            A = nc.scalar
            act.wait_ge(s["param_in"], 16 * 8)
            A.activation(els[:], ls[:], ACT.Exp, scale=-1.0).then_inc(s["alpha_exp"], 1)
            act.wait_ge(s["x_in"], 32)
            for b in range(B):
                A.copy(xr[:, b, :], xs[:, b, ::-1]).then_inc(s["xr_done"], 1)
            for b in range(B):
                act.wait_ge(s["xT_mm"], b + 1)
                A.copy(xt[:, :, b * TOK:(b + 1) * TOK],
                       ring[:, b % 2, 1, :].rearrange("p (c n) -> p c n", c=KC)[:, :, 0:TOK]).then_inc(s["xT_done"], 1)
            for b in range(B):
                act.wait_ge(s["sqrt_in"], b + 1)
                A.activation(std[:, b:b + 1], ve[:, b:b + 1], ACT.Sqrt).then_inc(s["sqrt_out"], 1)
                if b >= 1:
                    x1t_hi(A, act, b - 1)
            x1t_hi(A, act, B - 1)

            def split_hi(j, tl):
                act.wait_ge(wq_in[tl], 16 * j + 16)
                A.mul(wq16[:, tl, 0], wq32[:, tl], SW).then_inc(s["wsplit_hi"], 1)

            def evac(j, h):
                act.wait_ge(s["q_mm"], G * j + h + 1)
                if h % 4 == 0:
                    act.wait_ge(stores[h // 4], 16 + 32 * j)
                for hf in range(2):
                    hi = A.mul(qst_half(0, h, hf), ring_half(h, hf), SQ / (SX * SW))
                hi.then_inc(s["ring_hi"], 1)

            q_schedule(act, split_hi, evac)

        @block.tensor
        def _(pe):
            T = nc.tensor
            pe.wait_ge(s["x_in"], 32)
            for b in range(B):
                pe.wait_ge(s["xr_done"], b + 1)
                if b >= 2:
                    pe.wait_ge(s["xT_done"], b - 1)
                for c in range(KC):
                    mm = T.transpose(ring[:, b % 2, 1, 128 * c:128 * c + TOK], xr[:, b, DM - 128 * (c + 1):DM - 128 * c], ident[0:TOK, 0:TOK])
                mm.then_inc(s["xT_mm"], 1)
            pe.wait_ge(s["res_done"], 1)
            for c in range(KC):
                out = pmisc[:, 0, 8 * c:8 * (c + 1)]
                T.matmul(out, rre[:, 128 * c:128 * (c + 1)], num[:].rearrange("n a b r -> n (a b r)"), start=True, stop=False)
                mm = T.matmul(out, rim[:, 128 * c:128 * (c + 1)], numx[:].rearrange("n a b r -> n (a b r)"), start=False, stop=True)
            mm.then_inc(s["ksum_mm"], 1)
            pe.wait_ge(s["bfly_done"], 1)
            for r in range(4):
                out = pmisc[0:1, 1, 128 * r:128 * (r + 1)]
                for part in range(2):
                    mm = T.matmul(out, bfly[:, part, r:r + 1], dft[:, part, r:DM:4], start=(part == 0), stop=(part == 1))
            mm.then_inc(s["kt_mm"], 1)
            pe.wait_ge(s["toep_in"], 16)
            pe.wait_ge(s["xT_done"], B)

            def x1_transpose(b):
                pe.wait_ge(s["x1_done"], b + 1)
                if b >= 2:
                    pe.wait_ge(s["ring_free"], b - 1)
                for c in range(KC):
                    mm = T.transpose(ring[:, b % 2, 0, 128 * c:128 * c + TOK], x1[:, b, 128 * c:128 * (c + 1)], ident[0:TOK, 0:TOK])
                mm.then_inc(s["x1T_mm"], 1)

            for b in range(B):
                if b >= 2:
                    pe.wait_ge(s["y_used"], b - 1)
                for c in range(KC):
                    mm = T.matmul(pmisc[0:TOK, 2 + b % 2, 128 * c:DM], xt[:, c, b * TOK:(b + 1) * TOK],
                                  toep[:, 0:DM - 128 * c], start=(c == 0), stop=(c == KC - 1))
                mm.then_inc(s["y_mm"], 1)
                if b >= 1:
                    x1_transpose(b - 1)
            x1_transpose(B - 1)

            def heads(j):
                for h in range(G):
                    tl = h // 4
                    if h % 4 == 0:
                        pe.wait_ge(s["wsplit_done"], 2 * j + tl + 1)
                    pe.wait_ge(s["ring_free"], B + G * j + h - 1)
                    w0 = 128 * (h % 4)
                    for hf in range(2):
                        n = 0
                        for wp, xp in ((0, 0), (0, 1), (1, 0)):
                            for c in range(KC):
                                mm = T.matmul(ring[:, h % 2, hf, 0:TH], wq16[:, tl, wp, c, w0:w0 + 128],
                                              x1t[:, xp, c, TH * hf:TH * (hf + 1)], start=(n == 0), stop=(n == 11))
                                n += 1
                    mm.then_inc(s["q_mm"], 1)

            with pe.Fori(0, NKV - 1) as j:
                heads(j)
            heads(NKV - 1)


PARTS = ((0, 0), (0, 1), (1, 0))
NTASK0 = NCT + NCH + 4


def batch_tasks(has_next):
    keys = lambda nxt, h: [("K", nxt, h, i) for i in range(4)]
    if not has_next:
        return [keys(0, 1), keys(0, 2), keys(0, 3), []]
    tt = [("T", 1, 0, i) for i in range(NCT)]
    vv = [("V", 1, 0, i) for i in range(NCH)]
    k1, k2, k3, k4 = keys(0, 1), keys(0, 2), keys(0, 3), keys(1, 0)
    return [k1 + [tt[0], vv[0], tt[1], tt[2], vv[1], tt[3], tt[4], tt[5]],
            k2[0:3] + [vv[2], k2[3], tt[6], tt[7], vv[3], tt[8], tt[9], vv[4], tt[10], tt[11]],
            k3[0:3] + vv[5:6] + k3[3:4] + vv[6:9],
            k4[0:3] + vv[9:10] + k4[3:4] + vv[10:13]]


def pair_plan(last):
    plan, n = [], 0
    for bb in range(2):
        for tasks in batch_tasks(not (last and bb == 1)):
            plan.append([(t, n + i) for i, t in enumerate(tasks)])
            n += len(tasks)
    return plan, n


PLAN, NTASK = pair_plan(False)
PLAN_LAST, _ = pair_plan(True)


AHEAD = 2
SPREAD = 9
LAG = 4
SERVE = 4
BEFORE = 5


def placing(tasks):
    inside, serve = {}, {}
    for k in range(2, min(BEFORE, len(tasks))):
        serve.setdefault(k - 2, []).append(k)
    for n, k in enumerate(range(BEFORE, len(tasks))):
        c = n * SPREAD // (len(tasks) - BEFORE)
        inside.setdefault(c, []).append(k)
        serve.setdefault(min(c + SERVE, NCH - 1), []).append(k)
    return inside, serve


POOL_LOW = (5, 9)


def low_count(gs, c):
    by_pool = c in POOL_LOW
    per = len(POOL_LOW) if by_pool else NCH - len(POOL_LOW)
    return by_pool, per * gs + sum((d in POOL_LOW) == by_pool for d in range(c + 1))


def attention(nc, dram):
    with ExitStack() as ctx:
        sb = lambda n, s, d=FP32: ctx.enter_context(nc.sbuf_tensor(n, s, d))
        sem = lambda n: ctx.enter_context(nc.semaphore(n))
        ident, identh = sb("b_ident", [128, 128]), sb("b_identh", [128, 128], BF16)
        ones = sb("ones", [128, 1])
        ebias = sb("ebias", [128, 1])
        wk16, wv16 = sb("wk16", [128, 2, KC, 512], FP16), sb("wv16", [128, 2, KC, 512], FP16)
        cnat = sb("cnat", [128, 3, DM])
        ctxt = sb("ctxt", [128, 2, 2, KC, KEYS], FP16)
        kt = sb("kt", [128, 2, 2, KEYS], FP16)
        v16 = sb("v16", [128, 2, 2, NCH, 512], FP16)
        q16 = sb("q16", [128, 2, 2, GQ], FP16)
        sc = sb("sc", [128, NCH, GQ])
        p32 = sb("p32", [128, 4, GQ])
        mb = sb("mb", [128, GQ])
        rm, acc, o32 = sb("rm", [128, GQ]), sb("acc", [128, GQ]), sb("o32", [128, GQ])
        ost = sb("ost", [128, 2, 2, GQ], FP16)
        m32, r32 = sb("m32", [TOK, G]), sb("r32", [TOK, G])
        mh, ml = sb("mh", [TOK, G], BF16), sb("ml", [TOK, G], BF16)
        rh, rl = sb("rh", [TOK, G], FP16), sb("rl", [TOK, G], FP16)
        pair = ctx.enter_context(nc.psum_tensor("pair", [128, 2, 2, 512], FP32))
        pv = ctx.enter_context(nc.psum_tensor("pv", [128, 2, 512], FP32))
        misc = ctx.enter_context(nc.psum_tensor("misc", [128, 2, 512], FP32))
        w32 = sc[:, :, :].rearrange("p c n -> p (c n)")[:, 0:2 * KC * 512].rearrange("p (w c n) -> p w c n", w=2, c=KC)
        pp = sc[:, :, :].bitcast(FP16)

        names = ("const_in", "wk_in", "wv_in", "w_hi", "w_lo", "const_set", "s_mm", "s_copied", "rm_done", "sum_mm", "max_step", "r_step",
                 "r_done", "rb_mm", "on_done", "o_copied", "o_hi", "o_lo", "max_mm", "m_done", "mb_mm", "mb_copied", "sub_done",
                 "exp_done", "p_hi", "p_lo", "p_lo_pool", "acc_done", "pv_mm", "task_mm", "task_hi", "task_lo",
                 "lat_in0", "lat_in1", "q_in0", "q_in1", "out0", "out1", "cn0", "cn1", "cn2")
        s = {n: sem("b_" + n) for n in names}
        lat_in, q_in, outs = ((s[n + "0"], s[n + "1"]) for n in ("lat_in", "q_in", "out"))
        cn_in = (s["cn0"], s["cn1"], s["cn2"])

        def p_part(part, c, r0, r1, c0, c1):
            return pp[r0:r1, c, GQ * part + c0:GQ * part + c1]

        def two(ap):
            return ap.rearrange("p (a n) -> p a n", a=2)

        def task_bank(task, n):
            kind, nxt, h, i = task
            bank = misc[:, (NTASK0 + n) % 2, :]
            if kind == "K":
                return bank[:, 0:KT_N]
            if kind == "V":
                return bank[0:ch_rows(i), :]
            r = min(128, CTX - 128 * i)
            return bank.rearrange("p (c n) -> p c n", c=KC)[:, :, 0:r]

        def task_dst(task, bpar, hpar, part):
            kind, nxt, h, i = task
            if kind == "K":
                return kt[:, hpar, part, KT_N * i:KT_N * (i + 1)]
            if kind == "V":
                return v16[0:ch_rows(i), bpar, part, i, :]
            r = min(128, CTX - 128 * i)
            return ctxt[:, bpar, part, :, 128 * i:128 * i + r]

        def task_scale(task):
            return SX if task[0] == "T" else SQ / (SX * SW)

        prologue_tasks = [("T", 0, 0, i) for i in range(NCT)] + [("V", 0, 0, i) for i in range(NCH)] + \
                         [("K", 0, 0, i) for i in range(4)]
        block = ctx.enter_context(nc.Block())

        @block.sync
        def _(sp):
            ctx_rows = dram["ctx"]

            def load_tile(b, t):
                r = min(128, CTX - 128 * t)
                src = ctx_rows[bass.ds(b, 1), 128 * t:128 * t + r, :].rearrange("o p d -> (o p) d")
                sp.dma_start(cnat[0:r, t % 3, :], src).then_inc(cn_in[t % 3], 16)

            def load_rows(b, par):
                for part in range(2):
                    sp.dma_start(ctxt[:, par, part, :, CTX:KEYS],
                                 dram["x1t_d"][part, :, :, bass.ds(b * TOK, TOK)]).then_inc(lat_in[par], 16)

            def load_q(gs, par):
                for part in range(2):
                    sp.dma_start(q16[:, par, part, :],
                                 dram["q_d"][part, bass.ds(gs, 1), :, :].rearrange("o p n -> (o p) n")).then_inc(q_in[par], 16)

            def tile_number(plan, bb, t):
                return next(n for step in plan[4 * bb:4 * bb + 4] for task, n in step if task[0] == "T" and task[3] == t)

            for par in range(2):
                sp.dma_start(ident[64 * par:64 * (par + 1), :], dram["ident"][64 * par:64 * (par + 1), :]).then_inc(outs[par], 16)
            sp.dma_start(w32[:, 0], dram["wk"].rearrange("(c p) n -> p c n", c=KC)).then_inc(s["wk_in"], 16)
            for t in range(3):
                load_tile(0, t)
            sp.dma_start(w32[:, 1], dram["wv"].rearrange("(c p) n -> p c n", c=KC)).then_inc(s["wv_in"], 16)
            load_rows(0, 0)
            load_q(0, 0)
            load_q(1, 1)
            for t in range(3, NCT):
                sp.wait_ge(s["task_mm"], t - 2)
                load_tile(0, t)
            sp.wait_ge(s["task_mm"], NCT)
            for t in range(3):
                load_tile(1, t)

            def store(it, st):
                sp.wait_ge(s["o_lo"], 8 * it + st + 1)
                for part in range(2):
                    sp.dma_start(dram["o_d"][part, st % 4, bass.ds(2 * it + st // 4, 1), :, :].rearrange("o p n -> (o p) n"),
                                 ost[:, st % 2, part, :]).then_inc(outs[st % 2], 16)

            def body(it, plan, last):
                for st in range(8):
                    bb, h, gs = st // 4, st % 4, 8 * it + st
                    b = 2 * it + bb
                    if not (last and st >= 6):
                        sp.wait_ge(s["s_mm"], NCH * (gs + 1))
                        load_q(gs + 2, st % 2)
                    has_next = not (last and bb == 1)
                    base = NTASK0 + NTASK * it
                    if h == 0 and has_next:
                        sp.wait_ge(s["task_mm"], base + plan[st][0][1])
                        load_rows(b + 1, (bb + 1) % 2)
                    if h in (0, 1) and has_next:
                        for t in (range(3, 9) if h == 0 else range(9, NCT)):
                            sp.wait_ge(s["task_mm"], base + tile_number(plan, bb, t - 3) + 1)
                            load_tile(b + 1, t)
                    if h == 3 and not last:
                        sp.wait_ge(s["task_mm"], base + tile_number(plan, bb, NCT - 1) + 1)
                        for t in range(3):
                            load_tile(b + 2, t)
                    if st > 0:
                        store(it, st - 1)
                store(it, 7)

            with sp.Fori(0, B // 2 - 1) as it:
                body(it, PLAN, False)
            body(B // 2 - 1, PLAN_LAST, True)
            for par in range(2):
                sp.wait_ge(outs[par], 16 + 32 * (NKV * B // 2))

        @block.tensor
        def _(pe):
            T = nc.tensor

            def do_task(task, n, idx, bpar, hpar, waits=()):
                kind, nxt, h, i = task
                if waits:
                    for sm, v in waits:
                        pe.wait_ge(sm, v)
                if not isinstance(idx, int) or idx >= 2:
                    pe.wait_ge(s["task_lo"], idx - 1)
                out = task_bank(task, n)
                if kind == "T":
                    for c in range(KC):
                        mm = T.transpose(misc[:, (NTASK0 + n) % 2, 128 * c:128 * (c + 1)], cnat[:, i % 3, 128 * c:128 * (c + 1)], ident[:])
                else:
                    k = 0
                    for wp, xp in PARTS:
                        for c in range(KC):
                            if kind == "K":
                                lhs, rhs = wk16[:, wp, c, HD * h:HD * (h + 1)], ctxt[:, bpar, xp, c, KT_N * i:KT_N * (i + 1)]
                            else:
                                lhs, rhs = ctxt[:, bpar, xp, c, 128 * i:128 * i + ch_rows(i)], wv16[:, wp, c, :]
                            mm = T.matmul(out, lhs, rhs, start=(k == 0), stop=(k == 11))
                            k += 1
                mm.then_inc(s["task_mm"], 1)

            def scores_chunk(gs, par, c):
                if c == 0 and not (isinstance(gs, int) and gs == 0):
                    pe.wait_ge(s["mb_copied"], gs)
                if c >= 2:
                    pe.wait_ge(s["s_copied"], NCH * gs + c - 1)
                r = ch_rows(c)
                for kp, qp in PARTS:
                    for hf in range(2):
                        mm = T.matmul(pair[0:r, c % 2, hf, 0:HALF], kt[:, par, kp, 128 * c:128 * c + r],
                                      q16[:, par, qp, HALF * hf:HALF * (hf + 1)], start=(kp == 0 and qp == 0), stop=(kp == 1))
                mm.then_inc(s["s_mm"], 1)

            def broadcast(cols, banks):
                for g in range(G):
                    for part in range(2):
                        mm = T.matmul(banks[:, g // 4, TOK * (g % 4):TOK * (g % 4 + 1)],
                                      cols[part][:, g:g + 1].to_broadcast([TOK, 128]), identh[0:TOK, 0:TOK],
                                      start=(part == 0), stop=(part == 1))
                return mm

            for par in range(2):
                pe.wait_ge(outs[par], 16)
            for n, task in enumerate(prologue_tasks):
                kind, i = task[0], task[3]
                waits = []
                if kind == "T":
                    waits.append((cn_in[i % 3], 16 * (i // 3 + 1)))
                elif kind == "V":
                    waits.append((s["task_lo"], i + 1 if i < NCT else NCT))
                    if i == 0:
                        waits.append((s["w_lo"], 2))
                    if i == NCT - 1:
                        waits.append((lat_in[0], 32))
                do_task(task, n - NTASK0, n, 0, 0, waits)
            pe.wait_ge(s["const_set"], 3)
            pe.wait_ge(q_in[0], 32)
            pe.wait_ge(s["task_lo"], NTASK0)
            for c in range(NCH):
                scores_chunk(0, 0, c)
            do_task(PLAN[0][0][0], 0, NTASK0, 0, 1)

            def body(it, plan, last):
                base = NTASK0 + NTASK * it
                for st in range(8):
                    bb, h, gs = st // 4, st % 4, 8 * it + st
                    final = last and st == 7

                    def side(k, tasks, nst):
                        task, n = tasks[k]
                        nbb, kind, i = nst // 4, task[0], task[3]
                        bpar = (nbb + task[1]) % 2
                        waits = []
                        nb = 2 * it + nbb + 1
                        if kind == "T":
                            waits.append((cn_in[i % 3], 64 * nb + 16 * (i // 3 + 1)))
                        if kind == "V":
                            t = min(i, NCT - 1)
                            tn = next(m for step in plan[4 * nbb:4 * nbb + 4] for tk, m in step if tk[0] == "T" and tk[3] == t)
                            waits.append((s["task_lo"], base + tn + 1))
                        if kind == "K" and task[1] == 1 and i == 0:
                            tn = next(m for step in plan[4 * nbb:4 * nbb + 4] for tk, m in step if tk[0] == "T" and tk[3] == NCT - 1)
                            waits.append((s["task_lo"], base + tn + 1))
                            waits.append((lat_in[bpar], 32 * it + 32 * ((nbb + 1) // 2 + 1)))
                        do_task(task, n, base + n, bpar, (nst + 1) % 2, waits)

                    def reciprocals_out():
                        pe.wait_ge(s["r_done"], gs)
                        broadcast((rh, rl), pv).then_inc(s["rb_mm"], 1)

                    tasks = plan[st]
                    pe.wait_ge(s["rm_done"], (NCH - 1) * (gs + 1))
                    pe.wait_ge(s["s_copied"], NCH * (gs + 1))
                    for g in range(G):
                        mm = T.transpose(pair[0:TOK, 1, g // 4, 128 * (g % 4):128 * (g % 4 + 1)], rm[:, TOK * g:TOK * (g + 1)], ident[:])
                    mm.then_inc(s["max_mm"], 1)
                    if len(tasks) > 1:
                        side(1, tasks, st)
                    pe.wait_ge(s["m_done"], gs + 1)
                    broadcast((mh, ml), pair[:, 0, :, :]).then_inc(s["mb_mm"], 1)
                    inside, _ = placing(tasks)
                    for k in range(2, min(BEFORE, len(tasks))):
                        side(k, tasks, st)
                        if k == 2 and st > 0:
                            reciprocals_out()
                    if len(tasks) < 3:
                        reciprocals_out()
                    if st > 0:
                        pe.wait_ge(s["on_done"], gs)
                    if h == 0:
                        pe.wait_ge(s["task_lo"], base + plan[st][0][1])
                    nst = st + 1
                    for c in range(NCH):
                        by_pool, count = low_count(gs, c)
                        pe.wait_ge(s["p_lo_pool" if by_pool else "p_lo"], count)
                        r = ch_rows(c)
                        for vp, pt in PARTS:
                            for hf in range(2):
                                mm = T.matmul(pv[:, hf, 0:HALF], v16[0:r, bb, vp, c, HD * h:HD * (h + 1)],
                                              p_part(pt, c, 0, r, HALF * hf, HALF * (hf + 1)),
                                              start=(c == 0 and vp == 0 and pt == 0), stop=(c == NCH - 1 and vp == 1))
                        if c == NCH - 1:
                            mm.then_inc(s["pv_mm"], 1)
                        if not final:
                            if c == 0:
                                pe.wait_ge(q_in[nst % 2], 32 * (4 * it + nst // 2 + 1))
                            keys_task = (128 * c + r - 1) // KT_N
                            if c == 0 or keys_task > (128 * c - 1) // KT_N:
                                pe.wait_ge(s["task_lo"], base + next(n for t, n in tasks if t[0] == "K" and t[3] == keys_task) + 1)
                            scores_chunk(gs + 1, nst % 2, c)
                        for k in inside.get(c, ()):
                            side(k, tasks, st)
                    if not final:
                        if nst < 8:
                            if plan[nst]:
                                side(0, plan[nst], nst)
                        else:
                            do_task(PLAN[0][0][0], NTASK, base + NTASK, 0, 1)
                    pe.wait_ge(s["acc_done"], (NCH - 1) * (gs + 1))
                    pe.wait_ge(s["o_copied"], gs + 1)
                    for g in range(G):
                        mm = T.matmul(pv[0:TOK, 0, HALF + g:HALF + g + 1], acc[:, TOK * g:TOK * (g + 1)], ones[:], start=True, stop=True)
                    mm.then_inc(s["sum_mm"], 1)
                pe.wait_ge(s["r_done"], 8 * it + 8)
                broadcast((rh, rl), pv).then_inc(s["rb_mm"], 1)

            with pe.Fori(0, B // 2 - 1) as it:
                body(it, PLAN, False)
            body(B // 2 - 1, PLAN_LAST, True)

        @block.scalar
        def _(act):
            A = nc.scalar

            def hi(task, n, idx, bpar, hpar):
                act.wait_ge(s["task_mm"], idx + 1)
                A.mul(task_dst(task, bpar, hpar, 0), task_bank(task, n), task_scale(task)).then_inc(s["task_hi"], 1)

            def copy_scores(gs, c):
                act.wait_ge(s["s_mm"], NCH * gs + c + 1)
                r = ch_rows(c)
                A.copy(two(sc[0:r, c, :]), pair[0:r, c % 2, :, 0:HALF]).then_inc(s["s_copied"], 1)

            for w in range(2):
                act.wait_ge(s[("wk_in", "wv_in")[w]], 16)
                A.mul((wk16, wv16)[w][:, 0], w32[:, w], SW).then_inc(s["w_hi"], 1)
            for n, task in enumerate(prologue_tasks):
                hi(task, n - NTASK0, n, 0, 0)
            for c in range(NCH):
                copy_scores(0, c)
            hi(PLAN[0][0][0], 0, NTASK0, 0, 1)
            act.wait_ge(s["const_set"], 3)

            def body(it, plan, last):
                base = NTASK0 + NTASK * it
                for st in range(8):
                    gs = 8 * it + st
                    final = last and st == 7

                    def side(k, tasks, nst):
                        task, n = tasks[k]
                        hi(task, n, base + n, (nst // 4 + task[1]) % 2, (nst + 1) % 2)

                    def output_high(st):
                        act.wait_ge(s["on_done"], 8 * it + st + 1)
                        act.wait_ge(outs[st % 2], 16 + 32 * (4 * it + st // 2))
                        A.copy(ost[:, st % 2, 0, :], o32[:]).then_inc(s["o_hi"], 1)

                    def p_high(c):
                        r = ch_rows(c)
                        act.wait_ge(s["exp_done"], NCH * gs + c + 1)
                        A.copy(p_part(0, c, 0, r, 0, GQ), p32[0:r, c % 4, :]).then_inc(s["p_hi"], 1)

                    tasks = plan[st]
                    _, serve = placing(tasks)
                    if len(tasks) > 1:
                        side(1, tasks, st)
                    act.wait_ge(s["mb_mm"], gs + 1)
                    A.copy(two(mb[:]), pair[:, 0, :, 0:HALF]).then_inc(s["mb_copied"], 1)
                    for c in range(NCH):
                        r = ch_rows(c)
                        act.wait_ge(s["sub_done"], NCH * gs + c + 1)
                        if c >= 4:
                            by_pool, count = low_count(gs, c - 4)
                            act.wait_ge(s["p_lo_pool" if by_pool else "p_lo"], count)
                            act.wait_ge(s["acc_done"], (NCH - 1) * gs + max(1, c - 4))
                        A.activation(p32[0:r, c % 4, :], sc[0:r, c, :], ACT.Exp, bias=ebias[0:r, :],
                                     scale=1.0 / (SQ * SQ * math.sqrt(HD))).then_inc(s["exp_done"], 1)
                        if c >= 1:
                            p_high(c - 1)
                        for k in serve.get(c, ()):
                            side(k, tasks, st)
                        if c == 2 and st > 0:
                            output_high(st - 1)
                        if not final and c >= LAG:
                            copy_scores(gs + 1, c - LAG)
                    p_high(NCH - 1)
                    if not final:
                        for c in range(NCH - LAG, NCH):
                            copy_scores(gs + 1, c)
                    act.wait_ge(s["pv_mm"], gs + 1)
                    A.mul(two(o32[:]), pv[:, :, 0:HALF], SO / (2.0 ** SP_LOG2 * SQ * SR)).then_inc(s["o_copied"], 1)
                    nst = st + 1
                    if not final:
                        if nst < 8:
                            if plan[nst]:
                                side(0, plan[nst], nst)
                        else:
                            hi(PLAN[0][0][0], NTASK, base + NTASK, 0, 1)
                    if st == 7:
                        output_high(st)

            with act.Fori(0, B // 2 - 1) as it:
                body(it, PLAN, False)
            body(B // 2 - 1, PLAN_LAST, True)

        @block.vector
        def _(dve):
            V = nc.vector

            def lo(task, n, idx, bpar, hpar):
                dve.wait_ge(s["task_hi"], idx + 1)
                V.scalar_tensor_tensor(task_dst(task, bpar, hpar, 1), task_bank(task, n), task_scale(task),
                                       task_dst(task, bpar, hpar, 0), ALU.mult, ALU.subtract).then_inc(s["task_lo"], 1)

            def running_max(gs, c):
                r = ch_rows(c)
                dve.wait_ge(s["s_copied"], NCH * gs + c + 1)
                if c >= 2:
                    dve.wait_ge(s["rm_done"], (NCH - 1) * gs + c - 1)
                V.tensor_tensor(rm[0:r, :], sc[0:r, 0, :] if c == 1 else rm[0:r, :], sc[0:r, c, :], ALU.max).then_inc(s["rm_done"], 1)

            V.memset(ebias[:], SP_LOG2 * math.log(2.0)).then_inc(s["const_set"], 1)
            V.memset(ones[:], 2.0 ** -SP_LOG2).then_inc(s["const_set"], 1)
            for par in range(2):
                dve.wait_ge(outs[par], 16)
            V.tensor_copy(identh[:], ident[:]).then_inc(s["const_set"], 1)
            for w in range(2):
                dve.wait_ge(s["w_hi"], w + 1)
                w16 = (wk16, wv16)[w]
                V.scalar_tensor_tensor(w16[:, 1].rearrange("p c n -> p (c n)"), w32[:, w].rearrange("p c n -> p (c n)"), SW,
                                       w16[:, 0].rearrange("p c n -> p (c n)"), ALU.mult, ALU.subtract).then_inc(s["w_lo"], 1)
            for n, task in enumerate(prologue_tasks):
                lo(task, n - NTASK0, n, 0, 0)
            for c in range(1, NCH):
                running_max(0, c)
            lo(PLAN[0][0][0], 0, NTASK0, 0, 1)

            def body(it, plan, last):
                base = NTASK0 + NTASK * it
                for st in range(8):
                    gs = 8 * it + st
                    final = last and st == 7

                    def side(k, tasks, nst):
                        task, n = tasks[k]
                        lo(task, n, base + n, (nst // 4 + task[1]) % 2, (nst + 1) % 2)

                    tasks = plan[st]
                    _, serve = placing(tasks)

                    def subtract(c):
                        r = ch_rows(c)
                        V.tensor_tensor(sc[0:r, c, :], sc[0:r, c, :], mb[0:r, :], ALU.subtract).then_inc(s["sub_done"], 1)

                    def p_low(c):
                        r = ch_rows(c)
                        dve.wait_ge(s["p_hi"], NCH * gs + c + 1)
                        V.tensor_tensor(p_part(1, c, 0, r, 0, GQ), p32[0:r, c % 4, :], p_part(0, c, 0, r, 0, GQ), ALU.subtract).then_inc(s["p_lo"], 1)

                    def reciprocals(gs):
                        dve.wait_ge(s["sum_mm"], gs + 1)
                        V.reciprocal(r32[:], pv[0:TOK, 0, HALF:HALF + G]).then_inc(s["r_step"], 1)
                        dve.wait_ge(s["r_step"], 2 * gs + 1)
                        V.tensor_scalar(rh[:], r32[:], SR, None, ALU.mult).then_inc(s["r_step"], 1)
                        dve.wait_ge(s["r_step"], 2 * gs + 2)
                        V.scalar_tensor_tensor(rl[:], r32[:], SR, rh[:], ALU.mult, ALU.subtract).then_inc(s["r_done"], 1)

                    def normalise(gs):
                        dve.wait_ge(s["rb_mm"], gs + 1)
                        V.tensor_tensor(two(o32[:]), two(o32[:]), pv[:, :, 0:HALF], ALU.mult).then_inc(s["on_done"], 1)

                    dve.wait_ge(s["max_mm"], gs + 1)
                    V.tensor_reduce(m32[:], pair[0:TOK, 1, :, :].rearrange("p a (g k) -> p (a g) k", k=128), AX.X, ALU.max).then_inc(s["max_step"], 1)
                    dve.wait_ge(s["max_step"], 2 * gs + 1)
                    V.tensor_copy(mh[:], m32[:]).then_inc(s["max_step"], 1)
                    dve.wait_ge(s["max_step"], 2 * gs + 2)
                    V.tensor_tensor(ml[:], m32[:], mh[:], ALU.subtract).then_inc(s["m_done"], 1)
                    if st > 0:
                        reciprocals(gs - 1)
                    if len(tasks) > 1:
                        side(1, tasks, st)
                    dve.wait_ge(s["mb_copied"], gs + 1)
                    for c in range(AHEAD):
                        subtract(c)
                    for c in range(NCH):
                        if c + AHEAD < NCH:
                            subtract(c + AHEAD)
                        if c >= 1 and c - 1 not in POOL_LOW:
                            p_low(c - 1)
                        for k in serve.get(c, ()):
                            side(k, tasks, st)
                        if c == 0 and st > 0:
                            normalise(gs - 1)
                        if not final and c - LAG - 1 >= 1:
                            running_max(gs + 1, c - LAG - 1)
                    p_low(NCH - 1)
                    if not final:
                        for c in range(max(1, NCH - LAG - 1), NCH):
                            running_max(gs + 1, c)
                    nst = st + 1
                    if not final:
                        if nst < 8:
                            if plan[nst]:
                                side(0, plan[nst], nst)
                        else:
                            lo(PLAN[0][0][0], NTASK, base + NTASK, 0, 1)
                    if st == 7:
                        reciprocals(gs)
                        normalise(gs)

            with dve.Fori(0, B // 2 - 1) as it:
                body(it, PLAN, False)
            body(B // 2 - 1, PLAN_LAST, True)

        @block.gpsimd
        def _(pool):
            P = nc.gpsimd

            def output_low(it, st):
                pool.wait_ge(s["o_hi"], 8 * it + st + 1)
                P.tensor_tensor(ost[:, st % 2, 1, :], o32[:], ost[:, st % 2, 0, :], ALU.subtract).then_inc(s["o_lo"], 1)

            def body(it):
                for st in range(8):
                    gs = 8 * it + st
                    for c in range(1, NCH):
                        r = ch_rows(c)
                        pool.wait_ge(s["exp_done"], NCH * gs + c + 1)
                        r = ch_rows(c)
                        if c >= 2:
                            pool.wait_ge(s["acc_done"], (NCH - 1) * gs + c - 1)
                        P.tensor_tensor(acc[0:r, :], p32[0:r, 0, :] if c == 1 else acc[0:r, :], p32[0:r, c % 4, :], ALU.add).then_inc(s["acc_done"], 1)
                        if c in POOL_LOW:
                            pool.wait_ge(s["p_hi"], NCH * gs + c + 1)
                            P.tensor_tensor(p_part(1, c, 0, r, 0, GQ), p32[0:r, c % 4, :], p_part(0, c, 0, r, 0, GQ), ALU.subtract).then_inc(s["p_lo_pool"], 1)
                        if c == 4 and st > 0:
                            output_low(it, st - 1)
                output_low(it, 7)

            with pool.Fori(0, B // 2) as it:
                body(it)


HT = -(-HID // 128)

def h_rows(t):
    return min(128, HID - 128 * t)


def prep_tasks():
    tasks = []
    for w in range(3):
        tasks += [("B", w, i) for i in range(3 if w < 2 else 1)] + [("X", w, t) for t in range(HT)]
    return tasks


PREP = prep_tasks()
GH = G // 2


def ffn_phase(nc, dram):
    with ExitStack() as ctx:
        sb = lambda n, s, d=FP32: ctx.enter_context(nc.sbuf_tensor(n, s, d))
        sem = lambda n: ctx.enter_context(nc.semaphore(n))
        ident = sb("c_ident", [128, 128])
        zrow = sb("zrow", [1, 512], FP16)
        w13t = sb("w13t", [128, 2, 2, KC, HID], FP16)
        w2t = sb("w2t", [128, 2, HT, DM], FP16)
        xr = sb("xr_c", [TOK, B, DM])
        xt16 = sb("xt16", [128, 2, KC, NTOK], FP16)
        natural = 2 * HT * DM + KC * HID + 3 * HT * RANK + 2 * HID
        o_n, wo_n = B * GQ, GH * DM
        region = sb("region", [128, natural + o_n + wo_n])
        flat16 = region[:].bitcast(FP16)

        def take(at, n):
            return region[:, at:at + n]

        wn13 = take(0, 2 * HT * DM).rearrange("p (w t n) -> p w t n", w=2, t=HT)
        wn2 = take(2 * HT * DM, KC * HID).rearrange("p (t n) -> p t n", t=KC)
        bn = take(2 * HT * DM + KC * HID, 3 * HT * RANK).rearrange("p (w t n) -> p w t n", w=3, t=HT)
        la = region[0:RANK, natural - 2 * HID:natural - HID]
        lb = region[0:RANK, natural - HID:natural]
        la13 = sb("la13", [RANK, 2, DM])
        o_at, wo_at = (natural, 0), (natural + o_n, o_n)
        o16 = [take(at, o_n).bitcast(FP16).rearrange("p (l b n) -> p l b n", l=2, b=B) for at in o_at]
        wo32 = [take(at, wo_n).rearrange("p (g n) -> p g n", g=GH) for at in wo_at]
        w0 = o_n + wo_n
        wo16 = take(w0, 2 * G * DM).bitcast(FP16).rearrange("p (s l g n) -> p s l g n", s=2, l=2, g=G)
        att = take(w0 + 2 * G * DM, KC * NTOK).rearrange("p (c n) -> p c n", c=KC)
        assert w0 + 2 * G * DM + KC * NTOK <= natural
        g16 = flat16[:, 0:2 * HT * NTOK].rearrange("p (l t n) -> p l t n", l=2, t=HT)
        a = HT * NTOK
        sg = region[:, a:a + 2 * NTOK].rearrange("p (s n) -> p s n", s=2)
        g32 = region[:, a + 2 * NTOK:a + 4 * NTOK].rearrange("p (s n) -> p s n", s=2)
        z = sb("z_c", [TOK, 2, DM])
        stats, mv, ve, std = sb("stats_c", [TOK, 6]), sb("mv_c", [TOK, 2 * B, 2]), sb("ve_c", [TOK, 2 * B]), sb("std_c", [TOK, 2 * B])
        rstd, tmp1 = sb("rstd_c", [TOK, 2 * B]), sb("tmp1_c", [TOK, 1])
        ps = ctx.enter_context(nc.psum_tensor("ps_c", [128, 8, 512], FP32))

        names = ("w1_in", "w2_in", "w3_in", "w1_first", "w1_rest", "w3_first", "w3_rest", "id_in", "x1_in", "prep_mm", "prep_hi", "prep_done", "zrow_set", "wo_in0", "wo_in1",
                 "o_in0", "o_in1", "wo_hi", "wo_lo", "wo_mm", "proj_mm", "att_done", "turn_mm", "turn_used", "x2_done",
                 "x2T_mm", "x2T_hi", "x2T_done", "sqrt_in", "sqrt_out", "chain", "h_mm", "silu", "g_done", "g_hi", "g_lo",
                 "y_mm", "y_used", "y_done", "out_done")
        s = {n: sem("c_" + n) for n in names}
        w_in = (s["w1_in"], s["w3_in"], s["w2_in"])
        wf_in, wr_in = (s["w1_first"], s["w3_first"]), (s["w1_rest"], s["w3_rest"])
        wo_in, o_in = (s["wo_in0"], s["wo_in1"]), (s["o_in0"], s["o_in1"])
        NP = len(PREP)
        x_ord = [i for i, t in enumerate(PREP) if t[0] == "X"]

        def x_operands(w, t):
            r = h_rows(t)
            if w < 2:
                return (lambda bank: bank.rearrange("p (c n) -> p c n", c=KC)[:, :, 0:r]), (lambda part: w13t[:, w, part, :, 128 * t:128 * t + r])
            return (lambda bank: bank[0:r, :]), (lambda part: w2t[0:r, part, t, :])

        block = ctx.enter_context(nc.Block())

        @block.sync
        def _(sp):
            sp.dma_start(ident[:], dram["ident"]).then_inc(s["id_in"], 16)
            full = 128 * (HT - 1)
            for w, (wn, ln, an) in enumerate((("w1", "lb1", "la1"), ("w3", "lb3", "la3"))):
                src, bsrc = dram[wn], dram[ln]
                sp.dma_start(bn[:, w, 0:HT - 1, :], bsrc[0:full].rearrange("(t p) n -> p t n", p=128)).then_inc(w_in[w], 16)
                sp.dma_start(bn[0:HID - full, w, HT - 1, :], bsrc[full:HID]).then_inc(w_in[w], 16)
                sp.dma_start(la13[:, w, :], dram[an]).then_inc(w_in[w], 16)
                first = 4 * 128
                sp.dma_start(wn13[:, w, 0:4, :], src[0:first].rearrange("(t p) n -> p t n", p=128)).then_inc(wf_in[w], 16)
                sp.dma_start(wn13[:, w, 4:HT - 1, :], src[first:full].rearrange("(t p) n -> p t n", p=128)).then_inc(wr_in[w], 16)
                sp.dma_start(wn13[0:HID - full, w, HT - 1, :], src[full:HID]).then_inc(wr_in[w], 16)
            sp.dma_start(bn[:, 2, 0:KC, :], dram["lb2"].rearrange("(t p) n -> p t n", p=128)).then_inc(w_in[2], 16)
            sp.dma_start(la, dram["la2"]).then_inc(w_in[2], 16)
            sp.dma_start(wn2, dram["w2"].rearrange("(t p) n -> p t n", p=128)).then_inc(w_in[2], 16)
            wo_v = dram["wo"].rearrange("(k g p) n -> k p g n", k=2 * NKV, g=GH)

            def load_o(kv, sl):
                for part in range(2):
                    sp.dma_start(o16[sl][:, part], dram["o_d"][part, bass.ds(kv, 1)].rearrange("k b p n -> (k p) b n")).then_inc(o_in[sl], 16)

            def load_wo(half, sl):
                sp.dma_start(wo32[sl], wo_v[bass.ds(half, 1)].rearrange("k p g n -> (k p) g n")).then_inc(wo_in[sl], 16)

            load_wo(0, 0)
            load_o(0, 0)
            sp.dma_start(xr[:], dram["x1_d"]).then_inc(s["x1_in"], 16)
            sp.wait_ge(s["prep_done"], NP)
            load_wo(1, 1)
            load_o(1, 1)

            def body(j, last=False):
                for n in range(4):
                    if not (last and n >= 2):
                        sp.wait_ge(s["wo_lo"], 4 * j + n + 1)
                        load_wo(4 * j + n + 2, n % 2)
                if not last:
                    for sl in range(2):
                        sp.wait_ge(s["wo_mm"], 2 * j + sl + 1)
                        load_o(2 * j + 2 + sl, sl)

            body(0)
            body(1, last=True)
            for b in range(B):
                sp.wait_ge(s["y_done"], b + 1)
                sp.dma_start(dram["out"][b], xr[:, b, :]).then_inc(s["out_done"], 16)
            sp.wait_ge(s["out_done"], 16 * B)

        @block.tensor
        def _(pe):
            T = nc.tensor
            pe.wait_ge(s["id_in"], 16)
            b_last = {t[1]: i for i, t in enumerate(PREP) if t[0] == "B"}
            for n, (kind, w, i) in enumerate(PREP):
                if n >= 8:
                    pe.wait_ge(s["prep_done"], n - 7)
                bank = ps[:, n % 8, :]
                if kind == "B":
                    if i == 0:
                        pe.wait_ge(w_in[w], 48)
                    for t in range(4 * i, min(4 * i + 4, HT if w < 2 else KC)):
                        r = h_rows(t) if w < 2 else 128
                        mm = T.transpose(bank[0:RANK, 128 * (t % 4):128 * (t % 4) + r], bn[0:r, w, t, :], ident[0:r, 0:r])
                else:
                    r = h_rows(i)
                    if i == 0:
                        pe.wait_ge(s["prep_done"], b_last[w] + 1)
                        if w < 2:
                            pe.wait_ge(wf_in[w], 16)
                    if i == 4 and w < 2:
                        pe.wait_ge(wr_in[w], 32)
                    for c in range(KC):
                        if w < 2:
                            out = bank[:, 128 * c:128 * c + r]
                            T.matmul(out, wn13[0:r, w, i, 128 * c:128 * (c + 1)], ident[0:r, 0:r], start=True, stop=False)
                            mm = T.matmul(out, la13[:, w, 128 * c:128 * (c + 1)], lb[:, 128 * i:128 * i + r], start=False, stop=True)
                        else:
                            out = bank[0:r, 128 * c:128 * (c + 1)]
                            T.matmul(out, wn2[:, c, 128 * i:128 * i + r], ident[:], start=True, stop=False)
                            mm = T.matmul(out, la[:, 128 * i:128 * i + r], lb[:, 128 * c:128 * (c + 1)], start=False, stop=True)
                mm.then_inc(s["prep_mm"], 1)
            pe.wait_ge(s["prep_done"], NP)
            pe.wait_ge(s["zrow_set"], 1)

            def edge(stop):
                for k in range(8):
                    mm = T.matmul(ps[:, k, 0:TH], zrow[:, 0:128], zrow[:, 0:TH], start=not stop, stop=stop)
                return mm

            edge(False)

            def body(j):
                for sl in range(2):
                    pe.wait_ge(o_in[sl], 32 * j + 32)
                    for g in range(G):
                        if g % GH == 0:
                            pe.wait_ge(s["wo_lo"], 4 * j + 2 * sl + g // GH + 1)
                        for m in range(KC):
                            for wp, op in PARTS:
                                for hf in range(2):
                                    mm = T.matmul(ps[:, 2 * m + hf, 0:TH], wo16[:, sl, wp, g, 128 * m:128 * (m + 1)],
                                                  o16[sl][:, op, 4 * hf:4 * hf + 4, TOK * g:TOK * (g + 1)], start=False, stop=False)
                    mm.then_inc(s["wo_mm"], 1)

            with pe.Fori(0, NKV // 2) as j:
                body(j)
            edge(True).then_inc(s["proj_mm"], 1)
            pe.wait_ge(s["att_done"], 2 * KC)

            def x2_turn(b):
                pe.wait_ge(s["x2_done"], b + 1)
                if b >= 2:
                    pe.wait_ge(s["x2T_done"], b - 1)
                for c in range(KC):
                    mm = T.transpose(ps[:, 2 + b % 2, 128 * c:128 * c + TOK], xr[:, b, 128 * c:128 * (c + 1)], ident[0:TOK, 0:TOK])
                mm.then_inc(s["x2T_mm"], 1)

            for b in range(B):
                if b >= 2:
                    pe.wait_ge(s["turn_used"], b - 1)
                for c in range(KC):
                    mm = T.transpose(ps[0:TOK, b % 2, 128 * c:128 * (c + 1)], att[:, c, TOK * b:TOK * (b + 1)], ident[:])
                mm.then_inc(s["turn_mm"], 1)
                if b >= 1:
                    x2_turn(b - 1)
            x2_turn(B - 1)
            pe.wait_ge(s["x2T_done"], B)
            for t in range(HT):
                r, k0 = h_rows(t), 4 * (t % 2)
                if t >= 2:
                    pe.wait_ge(s["g_done"], t - 1)
                for w in range(2):
                    for n, (wp, xp) in enumerate(PARTS):
                        for c in range(KC):
                            for hf in range(2):
                                mm = T.matmul(ps[0:r, k0 + 2 * w + hf, 0:TH], w13t[:, w, wp, c, 128 * t:128 * t + r],
                                              xt16[:, xp, c, TH * hf:TH * (hf + 1)], start=(n == 0 and c == 0), stop=(n == 2 and c == KC - 1))
                mm.then_inc(s["h_mm"], 1)
            pe.wait_ge(s["g_lo"], HT)
            for b in range(B):
                if b >= 2:
                    pe.wait_ge(s["y_used"], b - 1)
                for n, (gp, wp) in enumerate(PARTS):
                    for t in range(HT):
                        r = h_rows(t)
                        mm = T.matmul(ps[0:TOK, b % 2, :], g16[0:r, gp, t, TOK * b:TOK * (b + 1)], w2t[0:r, wp, t, :],
                                      start=(n == 0 and t == 0), stop=(n == 2 and t == HT - 1))
                mm.then_inc(s["y_mm"], 1)

        @block.scalar
        def _(act):
            A = nc.scalar
            for n, (kind, w, i) in enumerate(PREP):
                if kind == "X":
                    cols, dst = x_operands(w, i)
                    act.wait_ge(s["prep_mm"], n + 1)
                    A.mul(dst(0), cols(ps[:, n % 8, :]), SW).then_inc(s["prep_hi"], 1)

            act.wait_ge(s["prep_done"], NP)
            for half in range(2 * NKV):
                kv, st = half // 2, half % 2
                act.wait_ge(wo_in[st], 16 * kv + 16)
                if kv >= 2:
                    act.wait_ge(s["wo_mm"], kv - 1)
                A.mul(wo16[:, kv % 2, 0, GH * st:GH * (st + 1)], wo32[st], SW).then_inc(s["wo_hi"], 1)
            act.wait_ge(s["proj_mm"], 1)
            for k in range(2 * KC):
                A.mul(att[:, k // 2, TH * (k % 2):TH * (k % 2 + 1)], ps[:, k, 0:TH], 1.0 / (SO * SW)).then_inc(s["att_done"], 1)

            def x2t_hi(b):
                act.wait_ge(s["x2T_mm"], b + 1)
                A.mul(xt16[:, 0, :, b * TOK:(b + 1) * TOK],
                      ps[:, 2 + b % 2, :].rearrange("p (c n) -> p c n", c=KC)[:, :, 0:TOK], SX).then_inc(s["x2T_hi"], 1)

            for b in range(B):
                act.wait_ge(s["sqrt_in"], b + 1)
                A.activation(std[:, b:b + 1], ve[:, b:b + 1], ACT.Sqrt).then_inc(s["sqrt_out"], 1)
                if b >= 1:
                    x2t_hi(b - 1)
            x2t_hi(B - 1)

            def g_high(t):
                r = h_rows(t)
                act.wait_ge(s["g_done"], t + 1)
                A.copy(g16[0:r, 0, t, :], g32[0:r, t % 2, :]).then_inc(s["g_hi"], 1)

            for t in range(HT):
                r, k0 = h_rows(t), 4 * (t % 2)
                act.wait_ge(s["h_mm"], t + 1)
                A.activation(sg[0:r, t % 2, :].rearrange("p (a n) -> p a n", a=2), ps[0:r, k0:k0 + 2, 0:TH], ACT.Silu,
                             scale=1.0 / (SX * SW)).then_inc(s["silu"], 1)
                if t >= 1:
                    g_high(t - 1)
            g_high(HT - 1)
            for b in range(B):
                act.wait_ge(s["sqrt_in"], B + b + 1)
                A.activation(std[:, B + b:B + b + 1], ve[:, B + b:B + b + 1], ACT.Sqrt).then_inc(s["sqrt_out"], 1)

        @block.vector
        def _(dve):
            V = nc.vector
            link = split_chain(dve, s["chain"])
            V.memset(zrow[:], 0.0).then_inc(s["zrow_set"], 1)
            for n, (kind, w, i) in enumerate(PREP):
                bank = ps[:, n % 8, :]
                if kind == "B":
                    dve.wait_ge(s["prep_mm"], n + 1)
                    c0, c1 = 512 * i, min(512 * i + 512, HID if w < 2 else DM)
                    V.tensor_scalar(lb[:, c0:c1], bank[0:RANK, 0:c1 - c0], LORA, None, ALU.mult).then_inc(s["prep_done"], 1)
                else:
                    cols, dst = x_operands(w, i)
                    dve.wait_ge(s["prep_hi"], x_ord.index(n) + 1)
                    V.scalar_tensor_tensor(dst(1), cols(bank), SW, dst(0), ALU.mult, ALU.subtract).then_inc(s["prep_done"], 1)
            for half in range(2 * NKV):
                kv, st = half // 2, half % 2
                dve.wait_ge(s["wo_hi"], half + 1)
                V.scalar_tensor_tensor(wo16[:, kv % 2, 1, GH * st:GH * (st + 1)].rearrange("p g n -> p (g n)"),
                                       wo32[st].rearrange("p g n -> p (g n)"), SW,
                                       wo16[:, kv % 2, 0, GH * st:GH * (st + 1)].rearrange("p g n -> p (g n)"),
                                       ALU.mult, ALU.subtract).then_inc(s["wo_lo"], 1)

            def x2t_lo(b):
                dve.wait_ge(s["x2T_hi"], b + 1)
                V.scalar_tensor_tensor(xt16[:, 1, :, b * TOK:(b + 1) * TOK],
                                       ps[:, 2 + b % 2, :].rearrange("p (c n) -> p c n", c=KC)[:, :, 0:TOK], SX,
                                       xt16[:, 0, :, b * TOK:(b + 1) * TOK], ALU.mult, ALU.subtract).then_inc(s["x2T_done"], 1)

            def normalise(n, b, ready, used, bank, scale, done):
                dve.wait_ge(ready, b + 1)
                V.scalar_tensor_tensor(z[:, b % 2], bank, scale, xr[:, b, :], ALU.mult, ALU.add).then_inc(used, 1)
                dve.wait_ge(used, b + 1)
                layernorm_rows(nc, dve, s["sqrt_in"], s["sqrt_out"], link, z[:, b % 2], stats[:], mv[:, n, :],
                               ve[:, n:n + 1], std[:, n:n + 1], rstd[:, n:n + 1], tmp1[:], n)
                V.tensor_scalar(xr[:, b, :], z[:, b % 2], mv[:, n, 0:1], rstd[:, n:n + 1], ALU.subtract, ALU.mult).then_inc(done, 1)

            dve.wait_ge(s["x1_in"], 16)
            for b in range(B):
                normalise(b, b, s["turn_mm"], s["turn_used"], ps[0:TOK, b % 2, :], 1.0, s["x2_done"])
                if b >= 1:
                    x2t_lo(b - 1)
            x2t_lo(B - 1)

            def g_low(t):
                r = h_rows(t)
                dve.wait_ge(s["g_hi"], t + 1)
                V.tensor_tensor(g16[0:r, 1, t, :], g32[0:r, t % 2, :], g16[0:r, 0, t, :], ALU.subtract).then_inc(s["g_lo"], 1)

            for t in range(HT):
                r, k0 = h_rows(t), 4 * (t % 2)
                dve.wait_ge(s["silu"], t + 1)
                if t >= 2:
                    dve.wait_ge(s["g_lo"], t - 1)
                V.scalar_tensor_tensor(g32[0:r, t % 2, :].rearrange("p (a n) -> p a n", a=2), ps[0:r, k0 + 2:k0 + 4, 0:TH],
                                       SG / (SX * SW), sg[0:r, t % 2, :].rearrange("p (a n) -> p a n", a=2),
                                       ALU.mult, ALU.mult).then_inc(s["g_done"], 1)
                if t >= 1:
                    g_low(t - 1)
            g_low(HT - 1)
            for b in range(B):
                normalise(B + b, b, s["y_mm"], s["y_used"], ps[0:TOK, b % 2, :], 1.0 / (SG * SW), s["y_done"])


def build(nc, dram):
    scratch = lambda n, s, d=FP32: nc.dram_tensor(n, s, d).ap()
    dram["kpad"] = scratch("kpad", (1, 128 + DM))
    dram["x1_d"] = scratch("x1_d", (TOK, B, DM))
    dram["x1t_d"] = scratch("x1t_d", (2, 128, KC, NTOK), FP16)
    dram["q_d"] = scratch("q_d", (2, B * NKV, 128, GQ), FP16)
    dram["o_d"] = scratch("o_d", (2, NKV, B, 128, GQ), FP16)
    s4_and_queries(nc, dram)
    attention(nc, dram)
    ffn_phase(nc, dram)


_INS = {"x": "x", "ctx_4096": "ctx", "L0_attn_Lambda_ri": "lam", "L0_attn_p_ri": "p", "L0_attn_q_ri": "q",
        "L0_attn_Vc_ri": "vc", "L0_attn_Ct_ri": "ct", "L0_attn_Bp": "bp", "L0_attn_D": "dskip",
        "L0_attn_log_step": "ls", "L0_xattn_Wq": "wq", "L0_xattn_Wk": "wk", "L0_xattn_Wv": "wv", "L0_xattn_Wo": "wo",
        "L0_ffn_w1": "w1", "L0_ffn_w3": "w3", "L0_ffn_w2": "w2", "L0_ffn_lora_A1": "la1", "L0_ffn_lora_B1": "lb1",
        "L0_ffn_lora_A3": "la3", "L0_ffn_lora_B3": "lb3", "L0_ffn_lora_A2": "la2", "L0_ffn_lora_B2": "lb2"}


def shape_tables():
    m = np.arange(DM)
    th = 2 * np.pi * m / DM
    omega = np.stack([1 - np.cos(th), 1 + np.cos(th), np.sin(th)])
    omega[:2] = np.abs(omega[:2])
    wpl = np.stack([(1 + np.cos(th)).reshape(KC, 128).T, (-np.sin(th)).reshape(KC, 128).T], axis=1)
    ang = 2 * np.pi * np.outer(np.arange(128), m) / DM
    dft = np.stack([np.cos(ang), -np.sin(ang)], axis=1) * (2.0 / DM)
    return {"omega": omega.astype(np.float32), "wpl": wpl.astype(np.float32), "dft": dft.astype(np.float32),
            "ident": np.eye(128, dtype=np.float32)}


def kernel(**inputs):
    import numpy as _np
    import concourse.bacc as _bacc
    from concourse import mybir as _mybir
    from concourse.bass_utils import run_bass_kernel_spmd as _run

    nc = _bacc.Bacc("TRN2", target_bir_lowering=False, num_devices=1, dynamic_dma_scratch_size=1024)
    arrays, dram = {}, {}
    given = {short: inputs[name] for name, short in _INS.items()} | shape_tables()
    for short, a in given.items():
        a = _np.ascontiguousarray(a)
        arrays[f"in_{short}_dram"] = a
        dram[short] = nc.dram_tensor(f"in_{short}_dram", a.shape, _mybir.dt.from_np(a.dtype), kind="ExternalInput").ap()
    dram["out"] = nc.dram_tensor("out_0_dram", (B, TOK, DM), FP32, kind="ExternalOutput").ap()
    build(nc, dram)
    r = _run(nc, [arrays], core_ids=[0])
    return r.results[0]["out_0_dram"]
```

```python
import math
from contextlib import ExitStack

import numpy as np
import concourse.bass as bass
from concourse import mybir

FP32 = mybir.dt.float32
FP16 = mybir.dt.float16
BF16 = mybir.dt.bfloat16
ALU = mybir.AluOpType
ACT = mybir.ActivationFunctionType
AX = mybir.AxisListType

B, TOK, DM = 8, 100, 512
NTOK = B * TOK
CTX = 1444
KEYS = CTX + TOK
NH, NKV, HD = 32, 4, 128
G = NH // NKV
HID, RANK = 1376, 16
NST = 64
KC = DM // 128
EPS = 1e-5
LORA = 2.0

NCH = -(-KEYS // 128)
LASTK = KEYS - 128 * (NCH - 1)
NCT = -(-CTX // 128)
KT_N = KEYS // 4
GQ = G * TOK
HALF = GQ // 2
TH = NTOK // 2

SX = 32.0
SW = 512.0
SQ = 32.0
SP_LOG2 = 13
SO = 256.0
SG = 64.0
SR = 1024.0


def ch_rows(c):
    return 128 if c < NCH - 1 else LASTK


def split_chain(eng, sem):
    count = [0]

    def link(ins):
        count[0] += 1
        ins.then_inc(sem, 1)
        eng.wait_ge(sem, count[0])

    return link


def row_statistics(nc, link, rows, stats, mv):
    link(nc.vector.bn_stats(stats, rows))
    link(nc.vector.bn_aggr(mv, stats))


def reciprocal_deviations(nc, dve, sqrt_in, sqrt_out, link, mv, var_eps, std, rstd, tmp, n):
    nc.vector.tensor_scalar(var_eps, mv, EPS, None, ALU.add).then_inc(sqrt_in, 1)
    dve.wait_ge(sqrt_out, n + 1)
    link(nc.vector.reciprocal(rstd, std))
    link(nc.vector.tensor_tensor(tmp, rstd, rstd, ALU.mult))
    dve.wait_ge(sqrt_in, n + 1)
    link(nc.vector.tensor_tensor(tmp, tmp, var_eps, ALU.mult))
    link(nc.vector.tensor_scalar(tmp, tmp, -0.5, 1.5, ALU.mult, ALU.add))
    link(nc.vector.tensor_tensor(rstd, rstd, tmp, ALU.mult))


HB = B // 2
MAKE_AND_TURN = [("make", b) for b in range(HB + 2)] + [("turn", 0), ("make", HB + 2), ("turn", 1), ("make", HB + 3)] + \
                [("turn", b) for b in range(2, B)]


def s4_and_queries(nc, dram, kept):
    with ExitStack() as ctx:
        sb = lambda n, s, d=FP32: ctx.enter_context(nc.sbuf_tensor(n, s, d))
        sem = lambda n: ctx.enter_context(nc.semaphore(n))
        ident, cnat, kv16 = kept["ident"], kept["cnat"], (kept["wk16"], kept["wv16"])
        lam, pq, ct = sb("lam", [NST, 2]), sb("pq", [NST, 2, 2]), sb("ct", [NST, 2])
        vc, bp = sb("vc", [NST, NST, 2]), sb("bp", [NST, NST])
        vcb, bpair = sb("vcb", [NST, NST, 2]), sb("bpair", [NST, 2, 2])
        bswap = sb("bswap", [NST, 2, 2])
        num, numx = sb("num", [NST, 2, 2, 2]), sb("numx", [NST, 2, 2, 2])
        ls, alpha, nlam, alr = sb("ls", [NST, 1]), sb("alpha", [NST, 1]), sb("nlam", [NST, 2]), sb("alr", [NST, 1])
        els = sb("els", [NST, 1])
        omega = sb("omega", [NST, 3, DM])
        dre, dim, tmpa, tmpb = (sb(f"s4_{n}", [NST, DM]) for n in ("dre", "dim", "ta", "tb"))
        rre, rim = sb("s4_rre", [NST, DM]), sb("s4_rim", [NST, DM])
        ksum = sb("ksum", [128, KC, 4, 2])
        wpl = sb("wpl", [128, 2, KC])
        cx = [sb(f"cx{i}", [128, 2, KC]) for i in range(8)]
        cxt = sb("cxt", [128, 2, KC])
        bfly, bt = sb("bfly", [128, 2, 4]), sb("bt", [128, 4, 2])
        dft = sb("dft", [128, 2, DM])
        krow = sb("krow", [1, 128 + DM])
        toep = sb("toep", [128, DM])
        dsk, dsk1 = sb("dsk", [TOK, 1]), sb("dsk1", [TOK, 1])
        xs, xr, x1 = (sb(n, [TOK, B, DM]) for n in ("xs", "xr", "x1"))
        xt = sb("xt", [128, KC, NTOK])
        stats, mv, ve, std = sb("stats", [TOK, B, 6]), sb("mv", [TOK, B, 2]), sb("ve", [TOK, B]), sb("std", [TOK, B])
        rstd, tmp1 = sb("rstd", [TOK, B]), sb("tmp1", [TOK, B])
        x1t = sb("x1t", [128, 2, KC, NTOK], FP16)
        wq32 = sb("wq32", [128, 2, KC, 512])
        wq16 = sb("wq16", [128, 2, 2, KC, 512], FP16)
        qst = sb("qst", [128, 2, B, GQ], FP16)
        ring = ctx.enter_context(nc.psum_tensor("a_ring", [128, 2, 2, 512], FP32))
        pmisc = ctx.enter_context(nc.psum_tensor("a_misc", [128, 4, 512], FP32))

        names = ("xr_done", "x_in", "param_in", "table_in", "dft_in", "alpha_exp", "dve_chain", "res_done", "ksum_mm",
                 "bfly_done", "kt_mm", "krow_done", "krow_out", "toep_in", "xT_mm", "xT_done", "y_mm", "y_used",
                 "sqrt_in", "sqrt_out", "x1_done", "x1T_mm", "ring_hi", "ring_free", "x1_out",
                 "wsplit_hi", "wsplit_done", "q_mm", "ctx_in", "wq_in0", "wq_in1", "store0", "store1")
        s = {n: sem("a_" + n) for n in names}
        wq_in = (s["wq_in0"], s["wq_in1"])
        stores = (s["store0"], s["store1"])
        wq_v = dram["wq"].rearrange("(c p) n -> p c n", c=KC)
        qd = dram["q_d"].rearrange("l (b k) p n -> l k p b n", k=NKV)
        def qst_half(part, h, hf):
            return qst[:, part, 4 * hf:4 * hf + 4, h * TOK:(h + 1) * TOK]

        def ring_half(h, hf):
            return ring[:, h % 2, hf, 0:TH].rearrange("p (b n) -> p b n", n=TOK)

        def x1t_lo(V, dve, b):
            dve.wait_ge(s["ring_hi"], b + 1)
            V.scalar_tensor_tensor(x1t[:, 1, :, b * TOK:(b + 1) * TOK], ring[:, b % 2, 0, :].rearrange("p (c n) -> p c n", c=KC)[:, :, 0:TOK],
                                   SX, x1t[:, 0, :, b * TOK:(b + 1) * TOK], ALU.mult, ALU.subtract).then_inc(s["ring_free"], 1)

        def split_part(j, tl, part):
            return kv16[tl][:, part] if isinstance(j, int) and j == NKV else wq16[:, tl, part]

        def q_schedule(eng, split, evac):
            def group(j, last=False):
                split(j, 1)
                for h in range(4):
                    evac(j, h)
                split(j + 1, 0)
                for h in range(4, G):
                    evac(j, h)
                if last:
                    split(j + 1, 1)
            with eng.Fori(0, NKV - 1) as j:
                group(j)
            group(NKV - 1, last=True)

        def x1t_hi(A, act, b):
            act.wait_ge(s["x1T_mm"], b + 1)
            A.mul(x1t[:, 0, :, b * TOK:(b + 1) * TOK],
                  ring[:, b % 2, 0, :].rearrange("p (c n) -> p c n", c=KC)[:, :, 0:TOK], SX).then_inc(s["ring_hi"], 1)

        block = ctx.enter_context(nc.Block())

        @block.sync
        def _(sp):
            sp.dma_start(vc[:], dram["vc"]).then_inc(s["param_in"], 16)
            for dst, src in ((lam[:], dram["lam"]), (pq[:, 0, :], dram["p"]), (pq[:, 1, :], dram["q"]),
                             (ct[:], dram["ct"][0])):
                sp.dma_start(dst, src).then_inc(s["param_in"], 16)
            sp.dma_start(bp[:], dram["bp"].rearrange("k o -> o k").to_broadcast([NST, NST])).then_inc(s["param_in"], 16)
            sp.dma_start(ls[:], dram["ls"][None, :].to_broadcast([NST, 1])).then_inc(s["param_in"], 16)
            sp.dma_start(dsk[:], dram["dskip"][None, :].to_broadcast([TOK, 1])).then_inc(s["param_in"], 16)
            sp.dma_start(omega[:], dram["omega"][None, :, :].to_broadcast([NST, 3, DM])).then_inc(s["table_in"], 16)
            sp.dma_start(ident[:], dram["ident"]).then_inc(s["x_in"], 16)
            sp.dma_start(xs[:], dram["x"].rearrange("b t d -> t b d")).then_inc(s["x_in"], 16)
            sp.dma_start(wpl[:], dram["wpl"]).then_inc(s["dft_in"], 16)
            sp.dma_start(dft[:], dram["dft"]).then_inc(s["dft_in"], 16)
            for tl in range(2):
                sp.dma_start(wq32[:, tl], wq_v[:, :, 512 * tl:512 * (tl + 1)]).then_inc(wq_in[tl], 16)
            sp.wait_ge(s["krow_done"], 1)
            sp.dma_start(dram["kpad"], krow[:]).then_inc(s["krow_out"], 16)
            sp.wait_ge(s["krow_out"], 16)
            sp.dma_start(toep[:], bass.AP(dram["kpad"].tensor, 1, [[1, 128], [1, DM]])).then_inc(s["toep_in"], 16)
            for b in range(B):
                sp.wait_ge(s["x1_done"], b + 1)
                sp.dma_start(dram["x1_d"][:, b, :], x1[:, b, :]).then_inc(s["x1_out"], 16)
            sp.wait_ge(s["ring_free"], B)
            for part in range(2):
                sp.dma_start(dram["x1t_d"][part], x1t[:, part]).then_inc(stores[part], 16)

            def group(j, last=False):
                for tl in range(2):
                    sp.wait_ge(s["wsplit_done"], 2 * j + tl + 1)
                    if last:
                        src = dram[("wk", "wv")[tl]].rearrange("(c p) n -> p c n", c=KC)
                    else:
                        src = wq_v[:, :, bass.ds(1024 * j + 1024 + 512 * tl, 512)]
                    sp.dma_start(wq32[:, tl], src).then_inc(wq_in[tl], 16)
                if last:
                    for t in range(3):
                        sp.dma_start(cnat[:, t, :], dram["ctx"][0, 128 * t:128 * (t + 1), :]).then_inc(s["ctx_in"], 16)
                for tl in range(2):
                    sp.wait_ge(s["ring_free"], B + G * j + 4 * tl + 4)
                    for part in range(2):
                        sp.dma_start(qd[part, bass.ds(j, 1), :, :, 400 * tl:400 * (tl + 1)].rearrange("o p b n -> (o p) b n"),
                                     qst[:, part, :, 400 * tl:400 * (tl + 1)]).then_inc(stores[tl], 16)

            with sp.Fori(0, NKV - 1) as j:
                group(j)
            group(NKV - 1, last=True)
            for tl in range(2):
                sp.wait_ge(stores[tl], 16 + 32 * NKV)
            sp.wait_ge(s["x1_out"], 16 * B)
            sp.wait_ge(s["ctx_in"], 16 * 3)

        @block.vector
        def _(dve):
            link = split_chain(dve, s["dve_chain"])
            V = nc.vector
            dve.wait_ge(s["param_in"], 16 * 8)
            link(V.tensor_tensor(vcb[:], vc[:], bp[:].rearrange("n (k o) -> n k o", o=1).to_broadcast([NST, NST, 2]), ALU.mult))
            link(V.tensor_reduce(bpair[:, 0, :], vcb[:].rearrange("n k c -> n c k"), AX.X, ALU.add))
            link(V.tensor_copy(bpair[:, 1, :], pq[:, 0, :]))
            link(V.tensor_copy(bswap[:, :, 0], bpair[:, :, 1]))
            link(V.tensor_scalar(bswap[:, :, 1], bpair[:, :, 0], -1.0, None, ALU.mult))
            for a, src in enumerate((ct[:], pq[:, 1, :])):
                link(V.tensor_scalar(num[:, a], bpair[:], src[:, 0:1], None, ALU.mult))
                link(V.scalar_tensor_tensor(num[:, a], bswap[:], src[:, 1:2], num[:, a], ALU.mult, ALU.add))
            link(V.tensor_scalar(numx[:, :, :, 0], num[:, :, :, 1], -1.0, None, ALU.mult))
            link(V.tensor_copy(numx[:, :, :, 1], num[:, :, :, 0]))
            link(V.tensor_scalar(nlam[:], lam[:], -1.0, None, ALU.mult))
            dve.wait_ge(s["alpha_exp"], 1)
            link(V.tensor_scalar(alpha[:], els[:], 2.0, None, ALU.mult))
            link(V.tensor_tensor(alr[:], alpha[:], lam[:, 0:1], ALU.add))
            link(V.tensor_scalar(dsk1[:], dsk[:], 1.0, None, ALU.add))
            dve.wait_ge(s["table_in"], 16)
            one_m, one_p, sin = omega[:, 0, :], omega[:, 1, :], omega[:, 2, :]
            link(V.tensor_scalar(tmpa[:], one_m, alpha[:], None, ALU.mult))
            link(V.scalar_tensor_tensor(tmpa[:], sin, nlam[:, 1:2], tmpa[:], ALU.mult, ALU.add))
            link(V.scalar_tensor_tensor(dre[:], one_p, nlam[:, 0:1], tmpa[:], ALU.mult, ALU.add))
            link(V.tensor_scalar(tmpb[:], sin, alr[:], None, ALU.mult))
            link(V.scalar_tensor_tensor(dim[:], one_p, nlam[:, 1:2], tmpb[:], ALU.mult, ALU.add))
            link(V.tensor_tensor(tmpa[:], dre[:], dre[:], ALU.mult))
            link(V.tensor_tensor(tmpb[:], dim[:], dim[:], ALU.mult))
            link(V.tensor_tensor(tmpa[:], tmpa[:], tmpb[:], ALU.add))
            link(V.reciprocal(tmpb[:], tmpa[:]))
            link(V.tensor_tensor(rre[:], dre[:], tmpb[:], ALU.mult))
            V.scalar_tensor_tensor(rim[:], dim[:], -1.0, tmpb[:], ALU.mult, ALU.mult).then_inc(s["res_done"], 1)
            dve.wait_ge(s["ksum_mm"], 1)
            link(V.tensor_copy(ksum[:], pmisc[:, 0, 0:KC * 8].rearrange("p (c v r) -> p c v r", c=KC, v=4)))
            dve.wait_ge(s["dft_in"], 32)
            kv = [ksum[:, :, v, :].rearrange("p c r -> p r c") for v in range(4)]

            def cmul(dst, a, b):
                link(V.tensor_tensor(dst[:, 0, :], a[:, 0, :], b[:, 0, :], ALU.mult))
                link(V.tensor_tensor(cxt[:, 0, :], a[:, 1, :], b[:, 1, :], ALU.mult))
                link(V.tensor_tensor(dst[:, 0, :], dst[:, 0, :], cxt[:, 0, :], ALU.subtract))
                link(V.tensor_tensor(dst[:, 1, :], a[:, 0, :], b[:, 1, :], ALU.mult))
                link(V.tensor_tensor(cxt[:, 1, :], a[:, 1, :], b[:, 0, :], ALU.mult))
                link(V.tensor_tensor(dst[:, 1, :], dst[:, 1, :], cxt[:, 1, :], ALU.add))

            wk11, k0110, nume, quot = cx[0], cx[1], cx[2], cx[3]
            cmul(wk11, wpl[:], kv[3])
            link(V.tensor_scalar(wk11[:, 0, :], wk11[:, 0, :], 1.0, None, ALU.add))
            cmul(k0110, kv[1], kv[2])
            cmul(nume, wpl[:], k0110[:])
            sq, inv, conj = cx[4], cx[5], cx[6]
            link(V.tensor_tensor(sq[:], wk11[:], wk11[:], ALU.mult))
            link(V.tensor_tensor(inv[:, 0, :], sq[:, 0, :], sq[:, 1, :], ALU.add))
            link(V.reciprocal(inv[:, 1, :], inv[:, 0, :]))
            link(V.tensor_tensor(conj[:, 0, :], wk11[:, 0, :], inv[:, 1, :], ALU.mult))
            link(V.scalar_tensor_tensor(conj[:, 1, :], wk11[:, 1, :], -1.0, inv[:, 1, :], ALU.mult, ALU.mult))
            cmul(quot, nume[:], conj[:])
            at = cx[7]
            link(V.tensor_tensor(at[:], kv[0], quot[:], ALU.subtract))
            s02, d02, s13, d13 = (bt[:, i, :] for i in range(4))
            link(V.tensor_tensor(s02, at[:, :, 0], at[:, :, 2], ALU.add))
            link(V.tensor_tensor(d02, at[:, :, 0], at[:, :, 2], ALU.subtract))
            link(V.tensor_tensor(s13, at[:, :, 1], at[:, :, 3], ALU.add))
            link(V.tensor_tensor(d13, at[:, :, 1], at[:, :, 3], ALU.subtract))
            link(V.tensor_tensor(bfly[:, :, 0], s02, s13, ALU.add))
            link(V.tensor_tensor(bfly[:, :, 2], s02, s13, ALU.subtract))
            link(V.tensor_tensor(bfly[:, 0, 1:2], d02[:, 0:1], d13[:, 1:2], ALU.subtract))
            link(V.tensor_tensor(bfly[:, 1, 1:2], d02[:, 1:2], d13[:, 0:1], ALU.add))
            link(V.tensor_tensor(bfly[:, 0, 3:4], d02[:, 0:1], d13[:, 1:2], ALU.add))
            link(V.tensor_tensor(bfly[:, 1, 3:4], d02[:, 1:2], d13[:, 0:1], ALU.subtract))
            V.memset(krow[0:1, 0:128], 0.0).then_inc(s["bfly_done"], 1)
            dve.wait_ge(s["kt_mm"], 1)
            V.tensor_copy(krow[0:1, 128:].rearrange("o (u r) -> o u r", r=4),
                          pmisc[0:1, 1, :].rearrange("o (r u) -> o u r", r=4)).then_inc(s["krow_done"], 1)
            def split_lo(j, tl):
                dve.wait_ge(s["wsplit_hi"], 2 * j + tl + 1)
                V.scalar_tensor_tensor(split_part(j, tl, 1).rearrange("p c n -> p (c n)"), wq32[:, tl].rearrange("p c n -> p (c n)"), SW,
                                       split_part(j, tl, 0).rearrange("p c n -> p (c n)"), ALU.mult, ALU.subtract).then_inc(s["wsplit_done"], 1)

            split_lo(0, 0)
            for half in range(2):
                b0, b1 = HB * half, HB * (half + 1)
                for b in range(b0, b1):
                    dve.wait_ge(s["y_mm"], b + 1)
                    V.scalar_tensor_tensor(xs[:, b, :], xs[:, b, :], dsk1[:], pmisc[0:TOK, 2 + b % 2, :],
                                           ALU.mult, ALU.add).then_inc(s["y_used"], 1)
                    dve.wait_ge(s["y_used"], b + 1)
                    row_statistics(nc, link, xs[:, b, :], stats[:, b, :], mv[:, b, :])
                    if half:
                        x1t_lo(V, dve, b - HB)
                reciprocal_deviations(nc, dve, s["sqrt_in"], s["sqrt_out"], link, mv[:, b0:b1, 1], ve[:, b0:b1],
                                      std[:, b0:b1], rstd[:, b0:b1], tmp1[:, b0:b1], half)
                for b in range(b0, b1):
                    V.tensor_scalar(x1[:, b, :], xs[:, b, :], mv[:, b, 0:1], rstd[:, b:b + 1],
                                    ALU.subtract, ALU.mult).then_inc(s["x1_done"], 1)
            for b in range(HB, B):
                x1t_lo(V, dve, b)

            def evac(j, h):
                dve.wait_ge(s["ring_hi"], B + G * j + h + 1)
                for hf in range(2):
                    lo = V.scalar_tensor_tensor(qst_half(1, h, hf), ring_half(h, hf), SQ / (SX * SW), qst_half(0, h, hf),
                                                ALU.mult, ALU.subtract)
                lo.then_inc(s["ring_free"], 1)

            q_schedule(dve, split_lo, evac)

        @block.scalar
        def _(act):
            A = nc.scalar
            act.wait_ge(s["param_in"], 16 * 8)
            A.activation(els[:], ls[:], ACT.Exp, scale=-1.0).then_inc(s["alpha_exp"], 1)
            act.wait_ge(s["x_in"], 32)
            for b in range(B):
                A.copy(xr[:, b, :], xs[:, b, ::-1]).then_inc(s["xr_done"], 1)
            for b in range(B):
                act.wait_ge(s["xT_mm"], b + 1)
                A.copy(xt[:, :, b * TOK:(b + 1) * TOK],
                       ring[:, b % 2, 1, :].rearrange("p (c n) -> p c n", c=KC)[:, :, 0:TOK]).then_inc(s["xT_done"], 1)
            def split_hi(j, tl):
                act.wait_ge(wq_in[tl], 16 * j + 16)
                A.mul(split_part(j, tl, 0), wq32[:, tl], SW).then_inc(s["wsplit_hi"], 1)

            split_hi(0, 0)
            for half in range(2):
                b0, b1 = HB * half, HB * (half + 1)
                act.wait_ge(s["sqrt_in"], half + 1)
                A.activation(std[:, b0:b1], ve[:, b0:b1], ACT.Sqrt).then_inc(s["sqrt_out"], 1)
                for b in range(b0, b1):
                    x1t_hi(A, act, b)

            def evac(j, h):
                act.wait_ge(s["q_mm"], G * j + h + 1)
                if h % 4 == 0:
                    act.wait_ge(stores[h // 4], 16 + 32 * j)
                for hf in range(2):
                    hi = A.mul(qst_half(0, h, hf), ring_half(h, hf), SQ / (SX * SW))
                hi.then_inc(s["ring_hi"], 1)

            q_schedule(act, split_hi, evac)

        @block.tensor
        def _(pe):
            T = nc.tensor
            pe.wait_ge(s["x_in"], 32)
            for b in range(B):
                pe.wait_ge(s["xr_done"], b + 1)
                if b >= 2:
                    pe.wait_ge(s["xT_done"], b - 1)
                for c in range(KC):
                    mm = T.transpose(ring[:, b % 2, 1, 128 * c:128 * c + TOK], xr[:, b, DM - 128 * (c + 1):DM - 128 * c], ident[0:TOK, 0:TOK])
                mm.then_inc(s["xT_mm"], 1)
            pe.wait_ge(s["res_done"], 1)
            for c in range(KC):
                out = pmisc[:, 0, 8 * c:8 * (c + 1)]
                T.matmul(out, rre[:, 128 * c:128 * (c + 1)], num[:].rearrange("n a b r -> n (a b r)"), start=True, stop=False)
                mm = T.matmul(out, rim[:, 128 * c:128 * (c + 1)], numx[:].rearrange("n a b r -> n (a b r)"), start=False, stop=True)
            mm.then_inc(s["ksum_mm"], 1)
            pe.wait_ge(s["bfly_done"], 1)
            for r in range(4):
                out = pmisc[0:1, 1, 128 * r:128 * (r + 1)]
                for part in range(2):
                    mm = T.matmul(out, bfly[:, part, r:r + 1], dft[:, part, r:DM:4], start=(part == 0), stop=(part == 1))
            mm.then_inc(s["kt_mm"], 1)
            pe.wait_ge(s["toep_in"], 16)
            pe.wait_ge(s["xT_done"], B)

            def x1_transpose(b):
                pe.wait_ge(s["x1_done"], b + 1)
                if b >= 2:
                    pe.wait_ge(s["ring_free"], b - 1)
                for c in range(KC):
                    mm = T.transpose(ring[:, b % 2, 0, 128 * c:128 * c + TOK], x1[:, b, 128 * c:128 * (c + 1)], ident[0:TOK, 0:TOK])
                mm.then_inc(s["x1T_mm"], 1)

            for kind, b in MAKE_AND_TURN:
                if kind == "turn":
                    x1_transpose(b)
                    continue
                if b >= 2:
                    pe.wait_ge(s["y_used"], b - 1)
                for c in range(KC):
                    mm = T.matmul(pmisc[0:TOK, 2 + b % 2, 128 * c:DM], xt[:, c, b * TOK:(b + 1) * TOK],
                                  toep[:, 0:DM - 128 * c], start=(c == 0), stop=(c == KC - 1))
                mm.then_inc(s["y_mm"], 1)

            def heads(j):
                for h in range(G):
                    tl = h // 4
                    if h % 4 == 0:
                        pe.wait_ge(s["wsplit_done"], 2 * j + tl + 1)
                    pe.wait_ge(s["ring_free"], B + G * j + h - 1)
                    w0 = 128 * (h % 4)
                    for hf in range(2):
                        n = 0
                        for wp, xp in ((0, 0), (0, 1), (1, 0)):
                            for c in range(KC):
                                mm = T.matmul(ring[:, h % 2, hf, 0:TH], wq16[:, tl, wp, c, w0:w0 + 128],
                                              x1t[:, xp, c, TH * hf:TH * (hf + 1)], start=(n == 0), stop=(n == 11))
                                n += 1
                    mm.then_inc(s["q_mm"], 1)

            pe.wait_ge(s["ring_free"], B)
            with pe.Fori(0, NKV - 1) as j:
                heads(j)
            heads(NKV - 1)


LAST = NCH - 1
STACK = tuple(slice(32 * k, 32 * k + LASTK) for k in range(3))
STACKED = 64 + LASTK
PARTS = ((0, 0), (0, 1), (1, 0))
NTASK0 = NCT + NCH + 4


def batch_tasks(has_next):
    keys = lambda nxt, h: [("K", nxt, h, i) for i in range(4)]
    if not has_next:
        return [keys(0, 1), keys(0, 2), keys(0, 3), []]
    tt = [("T", 1, 0, i) for i in range(NCT)]
    vv = [("V", 1, 0, i) for i in range(NCH)]
    k1, k2, k3, k4 = keys(0, 1), keys(0, 2), keys(0, 3), keys(1, 0)
    return [k1 + [tt[0], tt[1], vv[0], tt[2], tt[3], vv[1], tt[4], tt[5]],
            k2[0:3] + [vv[2], k2[3], tt[6], tt[7], vv[3], tt[8], tt[9], vv[4], tt[10], tt[11]],
            k3[0:3] + vv[5:6] + k3[3:4] + vv[6:9],
            k4[0:3] + vv[9:10] + k4[3:4] + vv[10:13]]


def pair_plan(last):
    plan, n = [], 0
    for bb in range(2):
        for tasks in batch_tasks(not (last and bb == 1)):
            plan.append([(t, n + i) for i, t in enumerate(tasks)])
            n += len(tasks)
    return plan, n


PLAN, NTASK = pair_plan(False)
PLAN_LAST, _ = pair_plan(True)


AHEAD = 2
SPREAD = 9
LAG = 4
SERVE = 4
BEFORE = 5


def placing(tasks):
    inside, serve = {}, {}
    for k in range(2, min(BEFORE, len(tasks))):
        serve.setdefault(k - 2, []).append(k)
    for n, k in enumerate(range(BEFORE, len(tasks))):
        c = n * SPREAD // (len(tasks) - BEFORE)
        inside.setdefault(c, []).append(k)
        serve.setdefault(min(c + SERVE, NCH - 1), []).append(k)
    return inside, serve


POOL_LOW = (5, 9)


def low_count(gs, c):
    by_pool = c in POOL_LOW
    per = len(POOL_LOW) if by_pool else NCH - len(POOL_LOW)
    return by_pool, per * gs + sum((d in POOL_LOW) == by_pool for d in range(c + 1))


def attention(nc, dram, kept):
    with ExitStack() as ctx:
        sb = lambda n, s, d=FP32: ctx.enter_context(nc.sbuf_tensor(n, s, d))
        sem = lambda n: ctx.enter_context(nc.semaphore(n))
        ident, wk16, wv16, cnat = (kept[n] for n in ("ident", "wk16", "wv16", "cnat"))
        ident2, identh = sb("b_ident", [128, 128]), sb("b_identh", [128, 128], BF16)
        ones = sb("ones", [128, 1])
        ebias = sb("ebias", [128, 1])
        ctxt = sb("ctxt", [128, 2, 2, KC, KEYS], FP16)
        kt = sb("kt", [128, 2, 2, KEYS], FP16)
        v16 = sb("v16", [128, 2, 2, NCH, 512], FP16)
        q16 = sb("q16", [128, 2, 2, GQ], FP16)
        sc = sb("sc", [128, NCH, GQ])
        p32 = sb("p32", [128, 4, GQ])
        mb = sb("mb", [128, GQ])
        rm, acc, o32 = sb("rm", [128, GQ]), sb("acc", [128, GQ]), sb("o32", [128, GQ])
        ost = sb("ost", [128, 2, 2, GQ], FP16)
        m32, r32 = sb("m32", [TOK, G]), sb("r32", [TOK, G])
        mh, ml = sb("mh", [TOK, G], BF16), sb("ml", [TOK, G], BF16)
        rh, rl = sb("rh", [TOK, G], FP16), sb("rl", [TOK, G], FP16)
        pair = ctx.enter_context(nc.psum_tensor("pair", [128, 2, 2, 512], FP32))
        pv = ctx.enter_context(nc.psum_tensor("pv", [128, 2, 512], FP32))
        misc = ctx.enter_context(nc.psum_tensor("misc", [128, 2, 512], FP32))
        pp = sc[:, :, :].bitcast(FP16)

        names = ("const_set", "s_mm", "s_copied", "rm_done", "sum_mm", "max_step", "r_step",
                 "r_done", "rb_mm", "on_done", "o_copied", "o_hi", "o_lo", "max_mm", "m_done", "mb_mm", "mb_copied", "sub_done",
                 "exp_done", "p_hi", "p_lo", "p_lo_pool", "acc_done", "pv_mm", "task_mm", "task_hi", "task_lo",
                 "lat_in0", "lat_in1", "q_in0", "q_in1", "out0", "out1", "cn0", "cn1", "cn2")
        s = {n: sem("b_" + n) for n in names}
        lat_in, q_in, outs = ((s[n + "0"], s[n + "1"]) for n in ("lat_in", "q_in", "out"))
        cn_in = (s["cn0"], s["cn1"], s["cn2"])

        def p_part(part, c, r0, r1, c0, c1):
            return pp[r0:r1, c, GQ * part + c0:GQ * part + c1]

        def two(ap):
            return ap.rearrange("p (a n) -> p a n", a=2)

        def task_bank(task, n):
            kind, nxt, h, i = task
            bank = misc[:, (NTASK0 + n) % 2, :]
            if kind == "K":
                return bank[:, 0:KT_N]
            if kind == "V":
                return bank[0:ch_rows(i), :]
            r = min(128, CTX - 128 * i)
            return bank.rearrange("p (c n) -> p c n", c=KC)[:, :, 0:r]

        def task_dst(task, bpar, hpar, part):
            kind, nxt, h, i = task
            if kind == "K":
                return kt[:, hpar, part, KT_N * i:KT_N * (i + 1)]
            if kind == "V":
                return v16[STACK[2] if i == LAST and part else slice(0, ch_rows(i)), bpar, 0 if i == LAST else part, i, :]
            r = min(128, CTX - 128 * i)
            return ctxt[:, bpar, part, :, 128 * i:128 * i + r]

        def task_scale(task):
            return SX if task[0] == "T" else SQ / (SX * SW)

        prologue_tasks = [("T", 0, 0, i) for i in range(NCT)] + [("V", 0, 0, i) for i in range(NCH)] + \
                         [("K", 0, 0, i) for i in range(4)]
        block = ctx.enter_context(nc.Block())

        @block.sync
        def _(sp):
            ctx_rows = dram["ctx"]

            def load_tile(b, t):
                r = min(128, CTX - 128 * t)
                src = ctx_rows[bass.ds(b, 1), 128 * t:128 * t + r, :].rearrange("o p d -> (o p) d")
                sp.dma_start(cnat[0:r, t % 3, :], src).then_inc(cn_in[t % 3], 16)

            def load_rows(b, par):
                for part in range(2):
                    sp.dma_start(ctxt[:, par, part, :, CTX:KEYS],
                                 dram["x1t_d"][part, :, :, bass.ds(b * TOK, TOK)]).then_inc(lat_in[par], 16)

            def load_q(gs, par):
                for part in range(2):
                    sp.dma_start(q16[:, par, part, :],
                                 dram["q_d"][part, bass.ds(gs, 1), :, :].rearrange("o p n -> (o p) n")).then_inc(q_in[par], 16)

            def tile_number(plan, bb, t):
                return next(n for step in plan[4 * bb:4 * bb + 4] for task, n in step if task[0] == "T" and task[3] == t)

            for par in range(2):
                sp.dma_start(ident2[64 * par:64 * (par + 1), :], dram["ident"][64 * par:64 * (par + 1), :]).then_inc(outs[par], 16)
            for t in range(3, NCT):
                sp.wait_ge(s["task_mm"], t - 2)
                load_tile(0, t)
            load_rows(0, 0)
            load_q(0, 0)
            load_q(1, 1)
            sp.wait_ge(s["task_mm"], NCT)
            for t in range(3):
                load_tile(1, t)

            def store(it, st):
                sp.wait_ge(s["o_lo"], 8 * it + st + 1)
                for part in range(2):
                    sp.dma_start(dram["o_d"][part, st % 4, bass.ds(2 * it + st // 4, 1), :, :].rearrange("o p n -> (o p) n"),
                                 ost[:, st % 2, part, :]).then_inc(outs[st % 2], 16)

            def body(it, plan, last):
                for st in range(8):
                    bb, h, gs = st // 4, st % 4, 8 * it + st
                    b = 2 * it + bb
                    if not (last and st >= 6):
                        sp.wait_ge(s["s_mm"], NCH * (gs + 1))
                        load_q(gs + 2, st % 2)
                    has_next = not (last and bb == 1)
                    base = NTASK0 + NTASK * it
                    if h == 0 and has_next:
                        sp.wait_ge(s["task_mm"], base + plan[st][0][1])
                        load_rows(b + 1, (bb + 1) % 2)
                    if h in (0, 1) and has_next:
                        for t in (range(3, 9) if h == 0 else range(9, NCT)):
                            sp.wait_ge(s["task_mm"], base + tile_number(plan, bb, t - 3) + 1)
                            load_tile(b + 1, t)
                    if h == 3 and not last:
                        sp.wait_ge(s["task_mm"], base + tile_number(plan, bb, NCT - 1) + 1)
                        for t in range(3):
                            load_tile(b + 2, t)
                    if st > 0:
                        store(it, st - 1)
                store(it, 7)

            with sp.Fori(0, B // 2 - 1) as it:
                body(it, PLAN, False)
            body(B // 2 - 1, PLAN_LAST, True)
            for par in range(2):
                sp.wait_ge(outs[par], 16 + 32 * (NKV * B // 2))

        @block.tensor
        def _(pe):
            T = nc.tensor

            def do_task(task, n, idx, bpar, hpar, waits=()):
                kind, nxt, h, i = task
                if waits:
                    for sm, v in waits:
                        pe.wait_ge(sm, v)
                if not isinstance(idx, int) or idx >= 2:
                    pe.wait_ge(s["task_lo"], idx - 1)
                out = task_bank(task, n)
                if kind == "T":
                    for c in range(KC):
                        mm = T.transpose(misc[:, (NTASK0 + n) % 2, 128 * c:128 * (c + 1)], cnat[:, i % 3, 128 * c:128 * (c + 1)], ident[:])
                else:
                    k = 0
                    for wp, xp in PARTS:
                        for c in range(KC):
                            if kind == "K":
                                lhs, rhs = wk16[:, wp, c, HD * h:HD * (h + 1)], ctxt[:, bpar, xp, c, KT_N * i:KT_N * (i + 1)]
                            else:
                                lhs, rhs = ctxt[:, bpar, xp, c, 128 * i:128 * i + ch_rows(i)], wv16[:, wp, c, :]
                            mm = T.matmul(out, lhs, rhs, start=(k == 0), stop=(k == 11))
                            k += 1
                mm.then_inc(s["task_mm"], 1)

            def scores_chunk(gs, par, c):
                if c == 0 and not (isinstance(gs, int) and gs == 0):
                    pe.wait_ge(s["mb_copied"], gs)
                if c >= 2:
                    pe.wait_ge(s["s_copied"], NCH * gs + c - 1)
                r = ch_rows(c)
                for kp, qp in PARTS:
                    for hf in range(2):
                        mm = T.matmul(pair[0:r, c % 2, hf, 0:HALF], kt[:, par, kp, 128 * c:128 * c + r],
                                      q16[:, par, qp, HALF * hf:HALF * (hf + 1)], start=(kp == 0 and qp == 0), stop=(kp == 1))
                mm.then_inc(s["s_mm"], 1)

            def broadcast(cols, banks):
                for g in range(G):
                    for part in range(2):
                        mm = T.matmul(banks[:, g // 4, TOK * (g % 4):TOK * (g % 4 + 1)],
                                      cols[part][:, g:g + 1].to_broadcast([TOK, 128]), identh[0:TOK, 0:TOK],
                                      start=(part == 0), stop=(part == 1))
                return mm

            for n, task in enumerate(prologue_tasks):
                kind, i = task[0], task[3]
                waits = []
                if kind == "T" and i >= 3:
                    waits.append((cn_in[i % 3], 16 * (i // 3)))
                elif kind == "V":
                    waits.append((s["task_lo"], i + 1 if i < NCT else NCT))
                    if i == NCT - 1:
                        waits.append((lat_in[0], 32))
                do_task(task, n - NTASK0, n, 0, 0, waits)
            pe.wait_ge(s["const_set"], 6)
            pe.wait_ge(q_in[0], 32)
            pe.wait_ge(s["task_lo"], NTASK0)
            for c in range(NCH):
                scores_chunk(0, 0, c)
            do_task(PLAN[0][0][0], 0, NTASK0, 0, 1)

            def body(it, plan, last):
                base = NTASK0 + NTASK * it
                for st in range(8):
                    bb, h, gs = st // 4, st % 4, 8 * it + st
                    final = last and st == 7

                    def side(k, tasks, nst):
                        task, n = tasks[k]
                        nbb, kind, i = nst // 4, task[0], task[3]
                        bpar = (nbb + task[1]) % 2
                        waits = []
                        nb = 2 * it + nbb + 1
                        if kind == "T":
                            waits.append((cn_in[i % 3], 64 * nb + 16 * (i // 3)))
                        if kind == "V":
                            t = min(i, NCT - 1)
                            tn = next(m for step in plan[4 * nbb:4 * nbb + 4] for tk, m in step if tk[0] == "T" and tk[3] == t)
                            waits.append((s["task_lo"], base + tn + 1))
                        if kind == "K" and task[1] == 1 and i == 0:
                            tn = next(m for step in plan[4 * nbb:4 * nbb + 4] for tk, m in step if tk[0] == "T" and tk[3] == NCT - 1)
                            waits.append((s["task_lo"], base + tn + 1))
                            waits.append((lat_in[bpar], 32 * it + 32 * ((nbb + 1) // 2 + 1)))
                        do_task(task, n, base + n, bpar, (nst + 1) % 2, waits)

                    def reciprocals_out():
                        pe.wait_ge(s["r_done"], gs)
                        broadcast((rh, rl), pv).then_inc(s["rb_mm"], 1)

                    tasks = plan[st]
                    pe.wait_ge(s["rm_done"], (NCH - 1) * (gs + 1))
                    pe.wait_ge(s["s_copied"], NCH * (gs + 1))
                    for g in range(G):
                        mm = T.transpose(pair[0:TOK, 1, g // 4, 128 * (g % 4):128 * (g % 4 + 1)], rm[:, TOK * g:TOK * (g + 1)], ident[:])
                    mm.then_inc(s["max_mm"], 1)
                    if len(tasks) > 1:
                        side(1, tasks, st)
                    pe.wait_ge(s["m_done"], gs + 1)
                    broadcast((mh, ml), pair[:, 0, :, :]).then_inc(s["mb_mm"], 1)
                    inside, _ = placing(tasks)
                    for k in range(2, min(BEFORE, len(tasks))):
                        side(k, tasks, st)
                        if k == 2 and st > 0:
                            reciprocals_out()
                    if len(tasks) < 3:
                        reciprocals_out()
                    if st > 0:
                        pe.wait_ge(s["on_done"], gs)
                    if h == 0:
                        pe.wait_ge(s["task_lo"], base + plan[st][0][1])
                    nst = st + 1
                    for c in range(NCH):
                        by_pool, count = low_count(gs, c)
                        pe.wait_ge(s["p_lo_pool" if by_pool else "p_lo"], count)
                        r = ch_rows(c)
                        for vp, pt in PARTS if c < LAST else ():
                            for hf in range(2):
                                T.matmul(pv[:, hf, 0:HALF], v16[0:r, bb, vp, c, HD * h:HD * (h + 1)],
                                         p_part(pt, c, 0, r, HALF * hf, HALF * (hf + 1)),
                                         start=(c == 0 and vp == 0 and pt == 0), stop=False)
                        if c == LAST:
                            for hf in range(2):
                                mm = T.matmul(pv[:, hf, 0:HALF], v16[0:STACKED, bb, 0, c, HD * h:HD * (h + 1)],
                                              p_part(0, c, 0, STACKED, HALF * hf, HALF * (hf + 1)), start=False, stop=True)
                            mm.then_inc(s["pv_mm"], 1)
                        if not final:
                            if c == 0:
                                pe.wait_ge(q_in[nst % 2], 32 * (4 * it + nst // 2 + 1))
                            keys_task = (128 * c + r - 1) // KT_N
                            if c == 0 or keys_task > (128 * c - 1) // KT_N:
                                pe.wait_ge(s["task_lo"], base + next(n for t, n in tasks if t[0] == "K" and t[3] == keys_task) + 1)
                            scores_chunk(gs + 1, nst % 2, c)
                        for k in inside.get(c, ()):
                            side(k, tasks, st)
                    if not final:
                        if nst < 8:
                            if plan[nst]:
                                side(0, plan[nst], nst)
                        else:
                            do_task(PLAN[0][0][0], NTASK, base + NTASK, 0, 1)
                    pe.wait_ge(s["acc_done"], (NCH - 1) * (gs + 1))
                    pe.wait_ge(s["o_copied"], gs + 1)
                    for g in range(G):
                        mm = T.matmul(pv[0:TOK, 0, HALF + g:HALF + g + 1], acc[:, TOK * g:TOK * (g + 1)], ones[:], start=True, stop=True)
                    mm.then_inc(s["sum_mm"], 1)
                pe.wait_ge(s["r_done"], 8 * it + 8)
                broadcast((rh, rl), pv).then_inc(s["rb_mm"], 1)

            with pe.Fori(0, B // 2 - 1) as it:
                body(it, PLAN, False)
            body(B // 2 - 1, PLAN_LAST, True)

        @block.scalar
        def _(act):
            A = nc.scalar

            def hi(task, n, idx, bpar, hpar):
                act.wait_ge(s["task_mm"], idx + 1)
                if task[0] == "V" and task[3] == LAST:
                    A.mul(v16[STACK[1], bpar, 0, LAST, :], task_bank(task, n), task_scale(task))
                A.mul(task_dst(task, bpar, hpar, 0), task_bank(task, n), task_scale(task)).then_inc(s["task_hi"], 1)

            def copy_scores(gs, c):
                act.wait_ge(s["s_mm"], NCH * gs + c + 1)
                r = ch_rows(c)
                A.copy(two(sc[0:r, c, :]), pair[0:r, c % 2, :, 0:HALF]).then_inc(s["s_copied"], 1)

            act.wait_ge(s["const_set"], 5)
            for n, task in enumerate(prologue_tasks):
                hi(task, n - NTASK0, n, 0, 0)
            for c in range(NCH):
                copy_scores(0, c)
            hi(PLAN[0][0][0], 0, NTASK0, 0, 1)
            act.wait_ge(s["const_set"], 6)

            def body(it, plan, last):
                base = NTASK0 + NTASK * it
                for st in range(8):
                    gs = 8 * it + st
                    final = last and st == 7

                    def side(k, tasks, nst):
                        task, n = tasks[k]
                        hi(task, n, base + n, (nst // 4 + task[1]) % 2, (nst + 1) % 2)

                    def output_high(st):
                        act.wait_ge(s["on_done"], 8 * it + st + 1)
                        act.wait_ge(outs[st % 2], 16 + 32 * (4 * it + st // 2))
                        A.copy(ost[:, st % 2, 0, :], o32[:]).then_inc(s["o_hi"], 1)

                    def p_high(c):
                        r = ch_rows(c)
                        act.wait_ge(s["exp_done"], NCH * gs + c + 1)
                        if c == LAST:
                            A.copy(pp[STACK[2], c, 0:GQ], p32[0:r, c % 4, :])
                        A.copy(p_part(0, c, 0, r, 0, GQ), p32[0:r, c % 4, :]).then_inc(s["p_hi"], 1)

                    tasks = plan[st]
                    _, serve = placing(tasks)
                    if len(tasks) > 1:
                        side(1, tasks, st)
                    act.wait_ge(s["mb_mm"], gs + 1)
                    A.copy(two(mb[:]), pair[:, 0, :, 0:HALF]).then_inc(s["mb_copied"], 1)
                    for c in range(NCH):
                        r = ch_rows(c)
                        act.wait_ge(s["sub_done"], NCH * gs + c + 1)
                        if c >= 4:
                            by_pool, count = low_count(gs, c - 4)
                            act.wait_ge(s["p_lo_pool" if by_pool else "p_lo"], count)
                            act.wait_ge(s["acc_done"], (NCH - 1) * gs + max(1, c - 4))
                        A.activation(p32[0:r, c % 4, :], sc[0:r, c, :], ACT.Exp, bias=ebias[0:r, :],
                                     scale=1.0 / (SQ * SQ * math.sqrt(HD))).then_inc(s["exp_done"], 1)
                        if c >= 1:
                            p_high(c - 1)
                        if not final and c >= LAG:
                            copy_scores(gs + 1, c - LAG)
                        for k in serve.get(c, ()):
                            side(k, tasks, st)
                        if c == 2 and st > 0:
                            output_high(st - 1)
                    p_high(NCH - 1)
                    if not final:
                        for c in range(NCH - LAG, NCH):
                            copy_scores(gs + 1, c)
                    act.wait_ge(s["pv_mm"], gs + 1)
                    A.mul(two(o32[:]), pv[:, :, 0:HALF], SO / (2.0 ** SP_LOG2 * SQ * SR)).then_inc(s["o_copied"], 1)
                    nst = st + 1
                    if not final:
                        if nst < 8:
                            if plan[nst]:
                                side(0, plan[nst], nst)
                        else:
                            hi(PLAN[0][0][0], NTASK, base + NTASK, 0, 1)
                    if st == 7:
                        output_high(st)

            with act.Fori(0, B // 2 - 1) as it:
                body(it, PLAN, False)
            body(B // 2 - 1, PLAN_LAST, True)

        @block.vector
        def _(dve):
            V = nc.vector

            def lo(task, n, idx, bpar, hpar):
                dve.wait_ge(s["task_hi"], idx + 1)
                V.scalar_tensor_tensor(task_dst(task, bpar, hpar, 1), task_bank(task, n), task_scale(task),
                                       task_dst(task, bpar, hpar, 0), ALU.mult, ALU.subtract).then_inc(s["task_lo"], 1)

            def running_max(gs, c):
                r = ch_rows(c)
                dve.wait_ge(s["s_copied"], NCH * gs + c + 1)
                if c >= 2:
                    dve.wait_ge(s["rm_done"], (NCH - 1) * gs + c - 1)
                V.tensor_tensor(rm[0:r, :], sc[0:r, 0, :] if c == 1 else rm[0:r, :], sc[0:r, c, :], ALU.max).then_inc(s["rm_done"], 1)

            for par in range(2):
                V.memset(v16[:, par, 0, LAST, :], 0.0).then_inc(s["const_set"], 1)
            V.memset(sc[:, LAST, :], 0.0).then_inc(s["const_set"], 1)
            V.memset(ebias[:], SP_LOG2 * math.log(2.0)).then_inc(s["const_set"], 1)
            V.memset(ones[:], 2.0 ** -SP_LOG2).then_inc(s["const_set"], 1)
            for par in range(2):
                dve.wait_ge(outs[par], 16)
            V.tensor_copy(identh[:], ident2[:]).then_inc(s["const_set"], 1)
            for n, task in enumerate(prologue_tasks):
                lo(task, n - NTASK0, n, 0, 0)
            for c in range(1, NCH):
                running_max(0, c)
            lo(PLAN[0][0][0], 0, NTASK0, 0, 1)

            def body(it, plan, last):
                base = NTASK0 + NTASK * it
                for st in range(8):
                    gs = 8 * it + st
                    final = last and st == 7

                    def side(k, tasks, nst):
                        task, n = tasks[k]
                        lo(task, n, base + n, (nst // 4 + task[1]) % 2, (nst + 1) % 2)

                    tasks = plan[st]
                    _, serve = placing(tasks)

                    def subtract(c):
                        r = ch_rows(c)
                        V.tensor_tensor(sc[0:r, c, :], sc[0:r, c, :], mb[0:r, :], ALU.subtract).then_inc(s["sub_done"], 1)

                    def p_low(c):
                        r = ch_rows(c)
                        dve.wait_ge(s["p_hi"], NCH * gs + c + 1)
                        low = p_part(1, c, 0, r, 0, GQ) if c < LAST else pp[STACK[1], c, 0:GQ]
                        V.tensor_tensor(low, p32[0:r, c % 4, :], p_part(0, c, 0, r, 0, GQ), ALU.subtract).then_inc(s["p_lo"], 1)

                    def reciprocals(gs):
                        dve.wait_ge(s["sum_mm"], gs + 1)
                        V.reciprocal(r32[:], pv[0:TOK, 0, HALF:HALF + G]).then_inc(s["r_step"], 1)
                        dve.wait_ge(s["r_step"], 2 * gs + 1)
                        V.tensor_scalar(rh[:], r32[:], SR, None, ALU.mult).then_inc(s["r_step"], 1)
                        dve.wait_ge(s["r_step"], 2 * gs + 2)
                        V.scalar_tensor_tensor(rl[:], r32[:], SR, rh[:], ALU.mult, ALU.subtract).then_inc(s["r_done"], 1)

                    def normalise(gs):
                        dve.wait_ge(s["rb_mm"], gs + 1)
                        V.tensor_tensor(two(o32[:]), two(o32[:]), pv[:, :, 0:HALF], ALU.mult).then_inc(s["on_done"], 1)

                    dve.wait_ge(s["max_mm"], gs + 1)
                    V.tensor_reduce(m32[:], pair[0:TOK, 1, :, :].rearrange("p a (g k) -> p (a g) k", k=128), AX.X, ALU.max).then_inc(s["max_step"], 1)
                    dve.wait_ge(s["max_step"], 2 * gs + 1)
                    V.tensor_copy(mh[:], m32[:]).then_inc(s["max_step"], 1)
                    dve.wait_ge(s["max_step"], 2 * gs + 2)
                    V.tensor_tensor(ml[:], m32[:], mh[:], ALU.subtract).then_inc(s["m_done"], 1)
                    if st > 0:
                        reciprocals(gs - 1)
                    if len(tasks) > 1:
                        side(1, tasks, st)
                    dve.wait_ge(s["mb_copied"], gs + 1)
                    for c in range(AHEAD):
                        subtract(c)
                    for c in range(NCH):
                        if c + AHEAD < NCH:
                            subtract(c + AHEAD)
                        if c >= 1 and c - 1 not in POOL_LOW:
                            p_low(c - 1)
                        for k in serve.get(c, ()):
                            side(k, tasks, st)
                        if c == 0 and st > 0:
                            normalise(gs - 1)
                        if not final and c - LAG - 1 >= 1:
                            running_max(gs + 1, c - LAG - 1)
                    p_low(NCH - 1)
                    if not final:
                        for c in range(max(1, NCH - LAG - 1), NCH):
                            running_max(gs + 1, c)
                    nst = st + 1
                    if not final:
                        if nst < 8:
                            if plan[nst]:
                                side(0, plan[nst], nst)
                        else:
                            lo(PLAN[0][0][0], NTASK, base + NTASK, 0, 1)
                    if st == 7:
                        reciprocals(gs)
                        normalise(gs)

            with dve.Fori(0, B // 2 - 1) as it:
                body(it, PLAN, False)
            body(B // 2 - 1, PLAN_LAST, True)

        @block.gpsimd
        def _(pool):
            P = nc.gpsimd

            def output_low(it, st):
                pool.wait_ge(s["o_hi"], 8 * it + st + 1)
                P.tensor_tensor(ost[:, st % 2, 1, :], o32[:], ost[:, st % 2, 0, :], ALU.subtract).then_inc(s["o_lo"], 1)

            def body(it):
                for st in range(8):
                    gs = 8 * it + st
                    for c in range(1, NCH):
                        r = ch_rows(c)
                        pool.wait_ge(s["exp_done"], NCH * gs + c + 1)
                        if c >= 2:
                            pool.wait_ge(s["acc_done"], (NCH - 1) * gs + c - 1)
                        P.tensor_tensor(acc[0:r, :], p32[0:r, 0, :] if c == 1 else acc[0:r, :], p32[0:r, c % 4, :], ALU.add).then_inc(s["acc_done"], 1)
                        if c in POOL_LOW:
                            pool.wait_ge(s["p_hi"], NCH * gs + c + 1)
                            P.tensor_tensor(p_part(1, c, 0, r, 0, GQ), p32[0:r, c % 4, :], p_part(0, c, 0, r, 0, GQ), ALU.subtract).then_inc(s["p_lo_pool"], 1)
                        if c == 4 and st > 0:
                            output_low(it, st - 1)
                output_low(it, 7)

            with pool.Fori(0, B // 2) as it:
                body(it)


HT = -(-HID // 128)

HCUTS = ((0, 512), (512, 1024), (1024, HID))
STK = 96


Y_BANKS = (4, 5) if HT % 2 else (0, 1)


def h_rows(t):
    return min(128, HID - 128 * t)


def prep_tasks():
    turned = lambda w: [("B", w, i) for i in range(3 if w < 2 else 1)]
    adds = [("E", w, t) for w in range(2) for t in range(HT)] + [("E", 2, (t, i)) for t in range(KC) for i in range(len(HCUTS))]
    splits = [("X", w, t) for w in range(3) for t in range(HT)]
    tasks, behind = turned(0), len(KC * HCUTS)
    for k in range(max(len(adds), len(splits) + behind)):
        tasks += adds[k:k + 1] + (splits[k - behind:k - behind + 1] if k >= behind else [])
        if adds[k:k + 1] and adds[k][0:1] + adds[k][2:] == ("E", 8):
            tasks += turned(adds[k][1] + 1)
    return tasks


PREP = prep_tasks()
POOL_ADDS = [n for n, t in enumerate(PREP) if t[0] == "E"][1::3]
GH = G // 2


def ffn_phase(nc, dram):
    with ExitStack() as ctx:
        sb = lambda n, s, d=FP32: ctx.enter_context(nc.sbuf_tensor(n, s, d))
        sem = lambda n: ctx.enter_context(nc.semaphore(n))
        ident = sb("c_ident", [128, 128])
        zrow = sb("zrow", [1, 512], FP16)
        w13t = sb("w13t", [128, 2, 2, KC, HID], FP16)
        w2t = sb("w2t", [128, 2, HT, DM], FP16)
        rows = sb("rows_c", [128, B * DM])
        xr = rows[0:TOK, :].rearrange("p (b n) -> p b n", b=B)
        cols = sb("cols_c", [128, 2 * KC * NTOK], FP16)
        xt16 = cols[:].rearrange("p (l c n) -> p l c n", l=2, c=KC)
        o_n, wo_n = B * GQ, GH * DM
        natural = max(2 * HT * DM + KC * HID + HID, o_n + wo_n + 2 * G * DM + KC * NTOK)
        region = sb("region", [128, natural + o_n + wo_n])
        flat16 = region[:].bitcast(FP16)

        def take(at, n):
            return region[:, at:at + n]

        wn13 = take(0, 2 * HT * DM).rearrange("p (w t n) -> p w t n", w=2, t=HT)
        wn2 = take(2 * HT * DM, KC * HID).rearrange("p (t n) -> p t n", t=KC)
        la2 = region[0:STK, 2 * HT * DM + KC * HID:2 * HT * DM + KC * HID + HID]
        la13 = sb("la13", [STK, 2, DM])
        product = sb("product", [128, 2, DM])
        b3_n, b1_n = 3 * HT * STK, 3 * HT * RANK
        bn3 = rows[:, 0:b3_n].rearrange("p (w t n) -> p w t n", w=3, t=HT)
        bn = rows[:, b3_n:b3_n + b1_n].rearrange("p (w t n) -> p w t n", w=3, t=HT)
        a13s = cols[0:STK, 0:2 * DM].rearrange("p (w n) -> p w n", w=2)
        a2s = cols[0:STK, 2 * DM:2 * DM + HID]
        b_at = 2 * DM + HID
        bs = [cols[0:STK, b_at + w * HID:b_at + w * HID + (HID if w < 2 else DM)] for w in range(3)]
        o_at, wo_at = (natural, 0), (natural + o_n, o_n)
        o16 = [take(at, o_n).bitcast(FP16).rearrange("p (l b n) -> p l b n", l=2, b=B) for at in o_at]
        wo32 = [take(at, wo_n).rearrange("p (g n) -> p g n", g=GH) for at in wo_at]
        w0 = o_n + wo_n
        wo16 = take(w0, 2 * G * DM).bitcast(FP16).rearrange("p (s l g n) -> p s l g n", s=2, l=2, g=G)
        att = take(w0 + 2 * G * DM, KC * NTOK).rearrange("p (c n) -> p c n", c=KC)
        assert w0 + 2 * G * DM + KC * NTOK <= natural
        g16 = flat16[:, 0:2 * HT * NTOK].rearrange("p (l t n) -> p l t n", l=2, t=HT)
        a = HT * NTOK
        sg = region[:, a:a + 2 * NTOK].rearrange("p (s n) -> p s n", s=2)
        g32 = region[:, a + 2 * NTOK:a + 4 * NTOK].rearrange("p (s n) -> p s n", s=2)
        stats, mv, ve, std = sb("stats_c", [TOK, B, 6]), sb("mv_c", [TOK, 2 * B, 2]), sb("ve_c", [TOK, 2 * B]), sb("std_c", [TOK, 2 * B])
        rstd, tmp1 = sb("rstd_c", [TOK, 2 * B]), sb("tmp1_c", [TOK, 2 * B])
        ps = ctx.enter_context(nc.psum_tensor("ps_c", [128, 8, 512], FP32))

        names = ("w1_in", "w2_in", "w3_in", "w1_first", "w1_rest", "w3_first", "w3_rest", "w2_natural",
                 "id_in", "zeroed", "b_wide", "a_hi", "a_lo", "x1_in", "prep_mm", "prep_hi", "prep_done", "pool_added",
                 "zrow_set", "wo_in0", "wo_in1",
                 "o_in0", "o_in1", "wo_hi", "wo_lo", "wo_mm", "proj_mm", "att_done", "turn_mm", "turn_used", "x2_done",
                 "x2T_mm", "x2T_hi", "x2T_done", "sqrt_in", "sqrt_out", "chain", "h_mm", "silu", "g_done", "g_hi", "g_lo",
                 "y_mm", "y_used", "y_done", "out_done")
        s = {n: sem("c_" + n) for n in names}
        w_in = (s["w1_in"], s["w3_in"], s["w2_in"])
        wf_in, wr_in = (s["w1_first"], s["w3_first"]), (s["w1_rest"], s["w3_rest"])
        wo_in, o_in = (s["wo_in0"], s["wo_in1"]), (s["o_in0"], s["o_in1"])
        NP = len(PREP)
        ND = NP - len(POOL_ADDS)
        in_act = lambda n: PREP[n][0] in "BX" or n in POOL_ADDS
        hi_count = [sum(in_act(m) for m in range(n + 1)) for n in range(NP)]

        def finished(n):
            in_pool = sum(m <= n for m in POOL_ADDS)
            return (s["pool_added"], in_pool) if n in POOL_ADDS else (s["prep_done"], n + 1 - in_pool)

        def add_operands(n):
            _, w, i = PREP[n]
            bank = ps[:, n % 8, :]
            if w < 2:
                return wn13[0:h_rows(i), w, i, :], bank[0:h_rows(i), :], DM
            c0, c1 = HCUTS[i[1]]
            return wn2[:, i[0], c0:c1], bank[:, 0:c1 - c0], c1 - c0

        def stacks(w):
            return (la13[:, w, :], a13s[:, w, :]) if w < 2 else (la2, a2s)

        def b_columns(w, i):
            return 512 * i, min(512 * i + 512, HID if w < 2 else DM)

        def x_operands(w, t):
            r = h_rows(t)
            if w < 2:
                return (lambda bank: bank.rearrange("p (c n) -> p c n", c=KC)[:, :, 0:r]), (lambda part: w13t[:, w, part, :, 128 * t:128 * t + r])
            return (lambda bank: bank[0:r, :]), (lambda part: w2t[0:r, part, t, :])

        block = ctx.enter_context(nc.Block())

        @block.sync
        def _(sp):
            sp.dma_start(ident[:], dram["ident"]).then_inc(s["id_in"], 16)
            full, first = 128 * (HT - 1), 4 * 128
            wparts = [("w1", "lb1", "la1"), ("w3", "lb3", "la3")]
            for w, (wn, ln, an) in enumerate(wparts):
                src, bsrc = dram[wn], dram[ln]
                sp.dma_start(wn13[:, w, 0:4, :], src[0:first].rearrange("(t p) n -> p t n", p=128)).then_inc(wf_in[w], 16)
                if w == 0:
                    sp.wait_ge(s["zeroed"], 2)
                sp.dma_start(bn[:, w, 0:HT - 1, :], bsrc[0:full].rearrange("(t p) n -> p t n", p=128)).then_inc(w_in[w], 16)
                sp.dma_start(bn[0:HID - full, w, HT - 1, :], bsrc[full:HID]).then_inc(w_in[w], 16)
                for k in range(3):
                    sp.dma_start(la13[32 * k:32 * k + RANK, w, :], dram[an]).then_inc(w_in[w], 16)
                sp.dma_start(wn13[:, w, 4:HT - 1, :], src[first:full].rearrange("(t p) n -> p t n", p=128)).then_inc(wr_in[w], 16)
                sp.dma_start(wn13[0:HID - full, w, HT - 1, :], src[full:HID]).then_inc(wr_in[w], 16)
            sp.dma_start(bn[:, 2, 0:KC, :], dram["lb2"].rearrange("(t p) n -> p t n", p=128)).then_inc(w_in[2], 16)
            sp.wait_ge(s["zeroed"], 4)
            for k in range(3):
                sp.dma_start(la2[32 * k:32 * k + RANK, :], dram["la2"]).then_inc(w_in[2], 16)
            sp.dma_start(wn2, dram["w2"].rearrange("(t p) n -> p t n", p=128)).then_inc(s["w2_natural"], 16)
            wo_v = dram["wo"].rearrange("(k g p) n -> k p g n", k=2 * NKV, g=GH)

            def load_o(kv, sl):
                for part in range(2):
                    sp.dma_start(o16[sl][:, part], dram["o_d"][part, bass.ds(kv, 1)].rearrange("k b p n -> (k p) b n")).then_inc(o_in[sl], 16)

            def load_wo(half, sl):
                sp.dma_start(wo32[sl], wo_v[bass.ds(half, 1)].rearrange("k p g n -> (k p) g n")).then_inc(wo_in[sl], 16)

            load_wo(0, 0)
            load_o(0, 0)
            sp.wait_ge(s["prep_done"], ND)
            load_wo(1, 1)
            load_o(1, 1)
            sp.dma_start(xr, dram["x1_d"]).then_inc(s["x1_in"], 16)

            def body(j, last=False):
                for n in range(4):
                    if not (last and n >= 2):
                        sp.wait_ge(s["wo_lo"], 4 * j + n + 1)
                        load_wo(4 * j + n + 2, n % 2)
                if not last:
                    for sl in range(2):
                        sp.wait_ge(s["wo_mm"], 2 * j + sl + 1)
                        load_o(2 * j + 2 + sl, sl)

            body(0)
            body(1, last=True)
            for b in range(B):
                sp.wait_ge(s["y_done"], b + 1)
                sp.dma_start(dram["out"][b], xr[:, b, :]).then_inc(s["out_done"], 16)
            sp.wait_ge(s["out_done"], 16 * B)

        @block.tensor
        def _(pe):
            T = nc.tensor
            pe.wait_ge(s["id_in"], 16)
            last = {}
            for n, (kind, w, i) in enumerate(PREP):
                if n >= 8:
                    if n - 8 in POOL_ADDS:
                        pe.wait_ge(s["prep_hi"], hi_count[n - 8])
                    else:
                        pe.wait_ge(*finished(n - 8))
                bank = ps[:, n % 8, :]
                if kind == "B":
                    if i == 0:
                        pe.wait_ge(s["b_wide"], 3 * w + 3)
                    for t in range(4 * i, min(4 * i + 4, HT if w < 2 else KC)):
                        r = h_rows(t) if w < 2 else 128
                        mm = T.transpose(bank[0:STK, 128 * (t % 4):128 * (t % 4) + r], bn3[0:r, w, t, :], ident[0:r, 0:r])
                elif kind == "E":
                    if ("E", w) not in last:
                        pe.wait_ge(*finished(last[("B", w)]))
                        pe.wait_ge(s["a_lo"], w + 1)
                    if w < 2:
                        mm = T.matmul(bank[0:h_rows(i), :], bs[w][:, 128 * i:128 * i + h_rows(i)], a13s[:, w, :], start=True, stop=True)
                    else:
                        t, cut = i
                        c0, c1 = HCUTS[cut]
                        mm = T.matmul(bank[:, 0:c1 - c0], bs[w][:, 128 * t:128 * (t + 1)], a2s[:, c0:c1], start=True, stop=True)
                else:
                    r = h_rows(i)
                    if w < 2:
                        pe.wait_ge(*finished(PREP.index(("E", w, i))))
                        for c in range(KC):
                            mm = T.transpose(bank[:, 128 * c:128 * c + r], wn13[0:r, w, i, 128 * c:128 * (c + 1)], ident[0:r, 0:r])
                    else:
                        if i == 0:
                            pe.wait_ge(*finished(max(m for m in range(n) if PREP[m][0] == "E" and m not in POOL_ADDS)))
                            pe.wait_ge(s["pool_added"], len(POOL_ADDS))
                        for t in range(KC):
                            mm = T.transpose(bank[0:r, 128 * t:128 * (t + 1)], wn2[:, t, 128 * i:128 * i + r], ident[:])
                last[(kind, w)] = n
                mm.then_inc(s["prep_mm"], 1)
            pe.wait_ge(s["prep_done"], ND)
            pe.wait_ge(s["zrow_set"], 1)

            def edge(stop):
                for k in range(8):
                    mm = T.matmul(ps[:, k, 0:TH], zrow[:, 0:128], zrow[:, 0:TH], start=not stop, stop=stop)
                return mm

            edge(False)

            def body(j):
                for sl in range(2):
                    pe.wait_ge(o_in[sl], 32 * j + 32)
                    for g in range(G):
                        if g % GH == 0:
                            pe.wait_ge(s["wo_lo"], 4 * j + 2 * sl + g // GH + 1)
                        for m in range(KC):
                            for wp, op in PARTS:
                                for hf in range(2):
                                    mm = T.matmul(ps[:, 2 * m + hf, 0:TH], wo16[:, sl, wp, g, 128 * m:128 * (m + 1)],
                                                  o16[sl][:, op, 4 * hf:4 * hf + 4, TOK * g:TOK * (g + 1)], start=False, stop=False)
                    mm.then_inc(s["wo_mm"], 1)

            with pe.Fori(0, NKV // 2) as j:
                body(j)
            edge(True).then_inc(s["proj_mm"], 1)
            pe.wait_ge(s["att_done"], 2 * KC)

            def x2_turn(b):
                pe.wait_ge(s["x2_done"], b + 1)
                if b >= 2:
                    pe.wait_ge(s["x2T_done"], b - 1)
                for c in range(KC):
                    mm = T.transpose(ps[:, 2 + b % 2, 128 * c:128 * c + TOK], xr[:, b, 128 * c:128 * (c + 1)], ident[0:TOK, 0:TOK])
                mm.then_inc(s["x2T_mm"], 1)

            for kind, b in MAKE_AND_TURN:
                if kind == "turn":
                    x2_turn(b)
                    continue
                if b >= 2:
                    pe.wait_ge(s["turn_used"], b - 1)
                for c in range(KC):
                    mm = T.transpose(ps[0:TOK, b % 2, 128 * c:128 * (c + 1)], att[:, c, TOK * b:TOK * (b + 1)], ident[:])
                mm.then_inc(s["turn_mm"], 1)
            pe.wait_ge(s["x2T_done"], B)
            for t in range(HT):
                r, k0 = h_rows(t), 4 * (t % 2)
                if t >= 2:
                    pe.wait_ge(s["g_done"], t - 1)
                for w in range(2):
                    for n, (wp, xp) in enumerate(PARTS):
                        for c in range(KC):
                            for hf in range(2):
                                mm = T.matmul(ps[0:r, k0 + 2 * w + hf, 0:TH], w13t[:, w, wp, c, 128 * t:128 * t + r],
                                              xt16[:, xp, c, TH * hf:TH * (hf + 1)], start=(n == 0 and c == 0), stop=(n == 2 and c == KC - 1))
                mm.then_inc(s["h_mm"], 1)
            for b in range(B):
                if b >= 2:
                    pe.wait_ge(s["y_used"], b - 1)
                for n, (gp, wp) in enumerate(PARTS):
                    for t in range(HT):
                        if b == 0 and n == 0 and t in (0, HT - 1):
                            pe.wait_ge(s["g_hi"], HT - 1 if t == 0 else HT)
                        if b == 0 and n == 1 and t == 0:
                            pe.wait_ge(s["g_lo"], HT)
                        r = h_rows(t)
                        mm = T.matmul(ps[0:TOK, Y_BANKS[b % 2], :], g16[0:r, gp, t, TOK * b:TOK * (b + 1)], w2t[0:r, wp, t, :],
                                      start=(n == 0 and t == 0), stop=(n == 2 and t == HT - 1))
                mm.then_inc(s["y_mm"], 1)

        @block.scalar
        def _(act):
            A = nc.scalar
            for n, (kind, w, i) in enumerate(PREP):
                bank = ps[:, n % 8, :]
                if kind == "B":
                    if i == 0:
                        a32, a16 = stacks(w)
                        act.wait_ge(w_in[w], 80 if w < 2 else 64)
                        act.wait_ge(s["zeroed"], 2 if w < 2 else 4)
                        A.mul(a16, a32, SW).then_inc(s["a_hi"], 1)
                    c0, c1 = b_columns(w, i)
                    act.wait_ge(s["prep_mm"], n + 1)
                    A.mul(bs[w][:, c0:c1], bank[0:STK, 0:c1 - c0], SW).then_inc(s["prep_hi"], 1)
                elif n in POOL_ADDS:
                    k = POOL_ADDS.index(n)
                    _, src, width = add_operands(n)
                    act.wait_ge(s["prep_mm"], n + 1)
                    if k >= 2:
                        act.wait_ge(s["pool_added"], k - 1)
                    A.mul(product[0:src.shape[0], k % 2, 0:width], src, LORA / (SW * SW)).then_inc(s["prep_hi"], 1)
                elif kind == "X":
                    src, dst = x_operands(w, i)
                    act.wait_ge(s["prep_mm"], n + 1)
                    A.mul(dst(0), src(bank), SW).then_inc(s["prep_hi"], 1)

            act.wait_ge(s["prep_done"], ND)
            for half in range(2 * NKV):
                kv, st = half // 2, half % 2
                act.wait_ge(wo_in[st], 16 * kv + 16)
                if kv >= 2:
                    act.wait_ge(s["wo_mm"], kv - 1)
                A.mul(wo16[:, kv % 2, 0, GH * st:GH * (st + 1)], wo32[st], SW).then_inc(s["wo_hi"], 1)
            act.wait_ge(s["proj_mm"], 1)
            for k in range(2 * KC):
                A.mul(att[:, k // 2, TH * (k % 2):TH * (k % 2 + 1)], ps[:, k, 0:TH], 1.0 / (SO * SW)).then_inc(s["att_done"], 1)

            def x2t_hi(b):
                act.wait_ge(s["x2T_mm"], b + 1)
                A.mul(xt16[:, 0, :, b * TOK:(b + 1) * TOK],
                      ps[:, 2 + b % 2, :].rearrange("p (c n) -> p c n", c=KC)[:, :, 0:TOK], SX).then_inc(s["x2T_hi"], 1)

            for half in range(2):
                b0, b1 = HB * half, HB * (half + 1)
                act.wait_ge(s["sqrt_in"], half + 1)
                A.activation(std[:, b0:b1], ve[:, b0:b1], ACT.Sqrt).then_inc(s["sqrt_out"], 1)
                for b in range(b0, b1):
                    x2t_hi(b)

            def g_high(t):
                r = h_rows(t)
                act.wait_ge(s["g_done"], t + 1)
                A.copy(g16[0:r, 0, t, :], g32[0:r, t % 2, :]).then_inc(s["g_hi"], 1)

            for t in range(HT):
                r, k0 = h_rows(t), 4 * (t % 2)
                act.wait_ge(s["h_mm"], t + 1)
                A.activation(sg[0:r, t % 2, :].rearrange("p (a n) -> p a n", a=2), ps[0:r, k0:k0 + 2, 0:TH], ACT.Silu,
                             scale=1.0 / (SX * SW)).then_inc(s["silu"], 1)
                if t >= 1:
                    g_high(t - 1)
            g_high(HT - 1)
            for b in range(B):
                act.wait_ge(s["sqrt_in"], 2 + b + 1)
                A.activation(std[:, B + b:B + b + 1], ve[:, B + b:B + b + 1], ACT.Sqrt).then_inc(s["sqrt_out"], 1)

        @block.vector
        def _(dve):
            V = nc.vector
            link = split_chain(dve, s["chain"])
            V.memset(bn, 0.0).then_inc(s["zeroed"], 1)
            V.memset(la13[:], 0.0).then_inc(s["zeroed"], 1)
            V.memset(bn3[:, 0], 0.0).then_inc(s["zeroed"], 1)
            V.memset(la2, 0.0).then_inc(s["zeroed"], 1)
            V.memset(bn3[:, 1:3], 0.0).then_inc(s["zeroed"], 1)
            V.memset(zrow[:], 0.0).then_inc(s["zrow_set"], 1)
            def widen(w):
                nt = HT if w < 2 else KC
                dve.wait_ge(w_in[w], 80 if w < 2 else 64)
                for k in range(3):
                    V.tensor_copy(bn3[:, w, 0:nt, 32 * k:32 * k + RANK], bn[:, w, 0:nt, :]).then_inc(s["b_wide"], 1)

            dve.wait_ge(s["zeroed"], 5)
            widen(0)
            for n, (kind, w, i) in enumerate(PREP):
                bank = ps[:, n % 8, :]
                if kind == "B":
                    if i == 0:
                        a32, a16 = stacks(w)
                        dve.wait_ge(s["a_hi"], w + 1)
                        V.scalar_tensor_tensor(a16[32:64, :], a32[32:64, :], SW, a16[32:64, :], ALU.mult, ALU.subtract).then_inc(s["a_lo"], 1)
                    c0, c1 = b_columns(w, i)
                    dve.wait_ge(s["prep_hi"], hi_count[n])
                    V.scalar_tensor_tensor(bs[w][64:STK, c0:c1], bank[64:STK, 0:c1 - c0], SW, bs[w][64:STK, c0:c1],
                                           ALU.mult, ALU.subtract).then_inc(s["prep_done"], 1)
                elif kind == "E":
                    if w < 2 and i in (0, 4):
                        dve.wait_ge((wf_in, wr_in)[i // 4][w], (16, 32)[i // 4])
                    if (w, i) == (2, (0, 0)):
                        dve.wait_ge(s["w2_natural"], 16)
                    if n not in POOL_ADDS:
                        wn, pr, _ = add_operands(n)
                        dve.wait_ge(s["prep_mm"], n + 1)
                        V.scalar_tensor_tensor(wn, pr, LORA / (SW * SW), wn, ALU.mult, ALU.add).then_inc(s["prep_done"], 1)
                    if i == 4 and w < 2:
                        widen(w + 1)
                else:
                    src, dst = x_operands(w, i)
                    dve.wait_ge(s["prep_hi"], hi_count[n])
                    V.scalar_tensor_tensor(dst(1), src(bank), SW, dst(0), ALU.mult, ALU.subtract).then_inc(s["prep_done"], 1)
            for half in range(2 * NKV):
                kv, st = half // 2, half % 2
                dve.wait_ge(s["wo_hi"], half + 1)
                V.scalar_tensor_tensor(wo16[:, kv % 2, 1, GH * st:GH * (st + 1)].rearrange("p g n -> p (g n)"),
                                       wo32[st].rearrange("p g n -> p (g n)"), SW,
                                       wo16[:, kv % 2, 0, GH * st:GH * (st + 1)].rearrange("p g n -> p (g n)"),
                                       ALU.mult, ALU.subtract).then_inc(s["wo_lo"], 1)

            def x2t_lo(b):
                dve.wait_ge(s["x2T_hi"], b + 1)
                V.scalar_tensor_tensor(xt16[:, 1, :, b * TOK:(b + 1) * TOK],
                                       ps[:, 2 + b % 2, :].rearrange("p (c n) -> p c n", c=KC)[:, :, 0:TOK], SX,
                                       xt16[:, 0, :, b * TOK:(b + 1) * TOK], ALU.mult, ALU.subtract).then_inc(s["x2T_done"], 1)

            def add_rows(b, ready, used, scale, banks):
                dve.wait_ge(ready, b + 1)
                V.scalar_tensor_tensor(xr[:, b, :], ps[0:TOK, banks[b % 2], :], scale, xr[:, b, :], ALU.mult, ALU.add).then_inc(used, 1)
                dve.wait_ge(used, b + 1)

            def deviations(n0, n1, n):
                reciprocal_deviations(nc, dve, s["sqrt_in"], s["sqrt_out"], link, mv[:, n0:n1, 1], ve[:, n0:n1],
                                      std[:, n0:n1], rstd[:, n0:n1], tmp1[:, n0:n1], n)

            def normalise(b, n, done):
                V.tensor_scalar(xr[:, b, :], xr[:, b, :], mv[:, n, 0:1], rstd[:, n:n + 1], ALU.subtract, ALU.mult).then_inc(done, 1)

            dve.wait_ge(s["x1_in"], 16)
            for half in range(2):
                for b in range(HB * half, HB * (half + 1)):
                    add_rows(b, s["turn_mm"], s["turn_used"], 1.0, (0, 1))
                    row_statistics(nc, link, xr[:, b, :], stats[:, b, :], mv[:, b, :])
                    if half:
                        x2t_lo(b - HB)
                deviations(HB * half, HB * (half + 1), half)
                for b in range(HB * half, HB * (half + 1)):
                    normalise(b, b, s["x2_done"])
            for b in range(HB, B):
                x2t_lo(b)

            def g_low(t):
                r = h_rows(t)
                dve.wait_ge(s["g_hi"], t + 1)
                V.tensor_tensor(g16[0:r, 1, t, :], g32[0:r, t % 2, :], g16[0:r, 0, t, :], ALU.subtract).then_inc(s["g_lo"], 1)

            for t in range(HT):
                r, k0 = h_rows(t), 4 * (t % 2)
                dve.wait_ge(s["silu"], t + 1)
                if t >= 2:
                    dve.wait_ge(s["g_lo"], t - 1)
                V.scalar_tensor_tensor(g32[0:r, t % 2, :].rearrange("p (a n) -> p a n", a=2), ps[0:r, k0 + 2:k0 + 4, 0:TH],
                                       SG / (SX * SW), sg[0:r, t % 2, :].rearrange("p (a n) -> p a n", a=2),
                                       ALU.mult, ALU.mult).then_inc(s["g_done"], 1)
                if t >= 1:
                    g_low(t - 1)
            g_low(HT - 1)
            for b in range(B):
                if b == 0:
                    dve.wait_ge(s["x2_done"], B)
                add_rows(b, s["y_mm"], s["y_used"], 1.0 / (SG * SW), Y_BANKS)
                row_statistics(nc, link, xr[:, b, :], stats[:, b, :], mv[:, B + b, :])
                deviations(B + b, B + b + 1, 2 + b)
                normalise(b, B + b, s["y_done"])

        @block.gpsimd
        def _(pool):
            for k, n in enumerate(POOL_ADDS):
                _, w, i = PREP[n]
                wn, _, width = add_operands(n)
                if w < 2:
                    pool.wait_ge(*((wf_in[w], 16) if i < 4 else (wr_in[w], 32)))
                else:
                    pool.wait_ge(s["w2_natural"], 16)
                pool.wait_ge(s["prep_hi"], hi_count[n])
                nc.gpsimd.tensor_tensor(wn, wn, product[0:wn.shape[0], k % 2, 0:width], ALU.add).then_inc(s["pool_added"], 1)


def build(nc, dram):
    scratch = lambda n, s, d=FP32: nc.dram_tensor(n, s, d).ap()
    dram["kpad"] = scratch("kpad", (1, 128 + DM))
    dram["x1_d"] = scratch("x1_d", (TOK, B, DM))
    dram["x1t_d"] = scratch("x1t_d", (2, 128, KC, NTOK), FP16)
    dram["q_d"] = scratch("q_d", (2, B * NKV, 128, GQ), FP16)
    dram["o_d"] = scratch("o_d", (2, NKV, B, 128, GQ), FP16)
    with ExitStack() as ctx:
        sb = lambda n, s, d=FP32: ctx.enter_context(nc.sbuf_tensor(n, s, d))
        kept = {"ident": sb("ident_ab", [128, 128]), "wk16": sb("wk16", [128, 2, KC, 512], FP16),
                "wv16": sb("wv16", [128, 2, KC, 512], FP16), "cnat": sb("cnat", [128, 3, DM])}
        s4_and_queries(nc, dram, kept)
        attention(nc, dram, kept)
    ffn_phase(nc, dram)


_INS = {"x": "x", "ctx_4096": "ctx", "L0_attn_Lambda_ri": "lam", "L0_attn_p_ri": "p", "L0_attn_q_ri": "q",
        "L0_attn_Vc_ri": "vc", "L0_attn_Ct_ri": "ct", "L0_attn_Bp": "bp", "L0_attn_D": "dskip",
        "L0_attn_log_step": "ls", "L0_xattn_Wq": "wq", "L0_xattn_Wk": "wk", "L0_xattn_Wv": "wv", "L0_xattn_Wo": "wo",
        "L0_ffn_w1": "w1", "L0_ffn_w3": "w3", "L0_ffn_w2": "w2", "L0_ffn_lora_A1": "la1", "L0_ffn_lora_B1": "lb1",
        "L0_ffn_lora_A3": "la3", "L0_ffn_lora_B3": "lb3", "L0_ffn_lora_A2": "la2", "L0_ffn_lora_B2": "lb2"}


def shape_tables():
    m = np.arange(DM)
    th = 2 * np.pi * m / DM
    omega = np.stack([1 - np.cos(th), 1 + np.cos(th), np.sin(th)])
    omega[:2] = np.abs(omega[:2])
    wpl = np.stack([(1 + np.cos(th)).reshape(KC, 128).T, (-np.sin(th)).reshape(KC, 128).T], axis=1)
    ang = 2 * np.pi * np.outer(np.arange(128), m) / DM
    dft = np.stack([np.cos(ang), -np.sin(ang)], axis=1) * (2.0 / DM)
    return {"omega": omega.astype(np.float32), "wpl": wpl.astype(np.float32), "dft": dft.astype(np.float32),
            "ident": np.eye(128, dtype=np.float32)}


def kernel(**inputs):
    import numpy as _np
    import concourse.bacc as _bacc
    from concourse import mybir as _mybir
    from concourse.bass_utils import run_bass_kernel_spmd as _run

    nc = _bacc.Bacc("TRN2", target_bir_lowering=False, num_devices=1, dynamic_dma_scratch_size=1024)
    arrays, dram = {}, {}
    given = {short: inputs[name] for name, short in _INS.items()} | shape_tables()
    for short, a in given.items():
        a = _np.ascontiguousarray(a)
        arrays[f"in_{short}_dram"] = a
        dram[short] = nc.dram_tensor(f"in_{short}_dram", a.shape, _mybir.dt.from_np(a.dtype), kind="ExternalInput").ap()
    dram["out"] = nc.dram_tensor("out_0_dram", (B, TOK, DM), FP32, kind="ExternalOutput").ap()
    build(nc, dram)
    r = _run(nc, [arrays], core_ids=[0])
    return r.results[0]["out_0_dram"]
```
